# Optimizing a Trainium2 kernel written in Bass

```python
import numpy as np
import jax
import jax.numpy as jnp

def _softmax(x, axis=-1):
    return jax.nn.softmax(x, axis=axis)

def _gelu(x):
    return jax.nn.gelu(x, approximate=True)

def _silu(x):
    return jax.nn.silu(x)

def _sigmoid(x):
    return jax.nn.sigmoid(x)

def _layernorm(x, axis=-1, eps=1e-05):
    m = jnp.mean(x, axis=axis, keepdims=True)
    v = jnp.var(x, axis=axis, keepdims=True)
    return (x - m) / jnp.sqrt(v + eps)

def _scatter_add(tgt, idx, src, axis=0):
    return tgt.at[idx].add(src)

def _segment_sum(src, seg, n):
    return jax.ops.segment_sum(src, seg, n)
kernel_name = 'mk_decoder_preln_d1_seqx_r4_a82b40'

def setup_inputs(seed: int=0):
    np.random.seed(seed)
    _w = jnp.asarray

    def _rec_inputs():
        import jax
        import jax.numpy as jnp
        _rk = jax.random.key(seed)
        x = -0.0002928 + 1 * jax.random.normal(jax.random.fold_in(_rk, 1), (32, 128, 256), jnp.float32)
        _lenS = 128 - jax.random.randint(jax.random.fold_in(_rk, 7), (32,), 0, max(1, 128 // 4) + 1, jnp.int32)
        _lenS2 = 128 - jax.random.randint(jax.random.fold_in(_rk, 8), (32,), 0, max(1, 128 // 4) + 1, jnp.int32)
        _ctx_1024P = jax.random.normal(jax.random.fold_in(_rk, 11), (32, 16, 256), jnp.float32)
        _ctx_1024c = jax.random.dirichlet(jax.random.fold_in(_rk, 511), 0.3 * jnp.ones((16,), jnp.float32), (32, 128))
        _ctx_1024t = jnp.einsum('bsk,bkd->bsd', _ctx_1024c, _ctx_1024P)
        _ctx_1024t = _ctx_1024t * jax.lax.rsqrt(jnp.mean(jnp.square(_ctx_1024t)) + 1e-12) * 0.953939
        ctx_1024 = 4.13588e-05 + 0.999923 * (_ctx_1024t + 0.3 * jax.random.normal(jax.random.fold_in(_rk, 611), (32, 128, 256), jnp.float32))
        return (x, ctx_1024)
    x, ctx_1024 = _rec_inputs()

    def _L0_attn_setup():
        import jax, jax.numpy as jnp
        import numpy as np
        N_HEAD = 8
        HEAD = 64
        RATIO = 2
        DEG = 2
        N_EMBD = 256
        QKV = (RATIO + 2) * N_HEAD * HEAD

        def _rope(t):
            B, T, h, d = t.shape
            div = 2.0 * np.pi / float(T) ** (np.arange(0, d, 2, dtype=np.float32) / d)
            ang = jnp.arange(T, dtype=jnp.float32)[:, None] * jnp.asarray(div)[None, :]
            sin = jnp.repeat(jnp.sin(ang), 2, axis=-1)[None, :, None, :]
            cos = jnp.repeat(jnp.cos(ang), 2, axis=-1)[None, :, None, :]
            x1 = t[..., ::2]
            x2 = t[..., 1::2]
            rot = jnp.stack((-x2, x1), axis=-1).reshape(t.shape)
            return t * cos + rot * sin
        key = jax.random.key(seed)
        k1, k2, k3 = jax.random.split(key, 3)
        B, T = (1, 512)
        x = jax.random.normal(k1, (B, T, N_EMBD), dtype=jnp.float32)
        w_attn = jax.random.normal(k2, (N_EMBD, QKV + N_HEAD), dtype=jnp.float32) * N_EMBD ** (-0.5)
        w_proj = jax.random.normal(k3, (RATIO * N_HEAD * HEAD, N_EMBD), dtype=jnp.float32) * (RATIO * N_HEAD * HEAD) ** (-0.5)
        ln_w = jnp.ones((HEAD,), dtype=jnp.float32)
        return {'x': x, 'w_attn': w_attn, 'w_proj': w_proj, 'ln_w': ln_w}
    _L0_attn_all = _L0_attn_setup()
    _L0_attn_in = {k: v for k, v in _L0_attn_all.items() if k in ('w_attn', 'w_proj', 'ln_w')}
    del _L0_attn_all

    def _L0_xattn_setup():
        import jax, jax.numpy as jnp
        import numpy as np
        HIDDEN = 256
        HEADS = 16
        HEAD_DIM = 64
        key = jax.random.key(seed)
        ks = jax.random.split(key, 7)
        B, Q, K = (2, 512, 1024)
        s = 1.0 / np.sqrt(HIDDEN)
        return {'query': jax.random.normal(ks[0], (B, Q, HIDDEN), dtype=jnp.float32), 'key': jax.random.normal(ks[1], (B, K, HIDDEN), dtype=jnp.float32), 'value': jax.random.normal(ks[2], (B, K, HIDDEN), dtype=jnp.float32), 'w_q': jax.random.normal(ks[3], (HIDDEN, HEADS * HEAD_DIM), dtype=jnp.float32) * s, 'w_k': jax.random.normal(ks[4], (HIDDEN, HEADS * HEAD_DIM), dtype=jnp.float32) * s, 'w_v': jax.random.normal(ks[5], (HIDDEN, HEADS * HEAD_DIM), dtype=jnp.float32) * s, 'w_o': jax.random.normal(ks[6], (HEADS * HEAD_DIM, HIDDEN), dtype=jnp.float32) * s}
    _L0_xattn_all = _L0_xattn_setup()
    _L0_xattn_in = {k: v for k, v in _L0_xattn_all.items() if k in ('w_q', 'w_k', 'w_v', 'w_o')}
    del _L0_xattn_all

    def _L0_ffn_setup():
        import jax, jax.numpy as jnp
        import numpy as np
        D_MODEL, D_FF, N_EXPERTS, TOP_K = (256, 512, 8, 2)
        B, S = (2, 512)
        key = jax.random.key(seed)
        k1, k2, k3, k4 = jax.random.split(key, 4)
        scale = 0.02
        return {'x': jax.random.normal(k1, (B, S, D_MODEL), dtype=jnp.float32), 'gate_w': jax.random.normal(k2, (D_MODEL, N_EXPERTS), dtype=jnp.float32) * scale, 'w1': jax.random.normal(k3, (N_EXPERTS, D_MODEL, D_FF), dtype=jnp.float32) * scale, 'w2': jax.random.normal(k4, (N_EXPERTS, D_FF, D_MODEL), dtype=jnp.float32) * scale}
    _L0_ffn_all = _L0_ffn_setup()
    _L0_ffn_in = {k: v for k, v in _L0_ffn_all.items() if k in ('gate_w', 'w1', 'w2')}
    del _L0_ffn_all
    return {'x': x, 'ctx_1024': ctx_1024, 'L0_attn_w_attn': _L0_attn_in['w_attn'], 'L0_attn_w_proj': _L0_attn_in['w_proj'], 'L0_attn_ln_w': _L0_attn_in['ln_w'], 'L0_xattn_w_q': _L0_xattn_in['w_q'], 'L0_xattn_w_k': _L0_xattn_in['w_k'], 'L0_xattn_w_v': _L0_xattn_in['w_v'], 'L0_xattn_w_o': _L0_xattn_in['w_o'], 'L0_ffn_gate_w': _L0_ffn_in['gate_w'], 'L0_ffn_w1': _L0_ffn_in['w1'], 'L0_ffn_w2': _L0_ffn_in['w2']}

def reference(x, ctx_1024, L0_attn_w_attn, L0_attn_w_proj, L0_attn_ln_w, L0_xattn_w_q, L0_xattn_w_k, L0_xattn_w_v, L0_xattn_w_o, L0_ffn_gate_w, L0_ffn_w1, L0_ffn_w2):
    import jax
    import jax.numpy as jnp

    def _L0_attn_ref(x, w_attn, w_proj, ln_w):
        import jax, jax.numpy as jnp
        import numpy as np
        N_HEAD = 8
        HEAD = 64
        RATIO = 2
        DEG = 2
        N_EMBD = 256
        QKV = (RATIO + 2) * N_HEAD * HEAD

        def _rope(t):
            B, T, h, d = t.shape
            div = 2.0 * np.pi / float(T) ** (np.arange(0, d, 2, dtype=np.float32) / d)
            ang = jnp.arange(T, dtype=jnp.float32)[:, None] * jnp.asarray(div)[None, :]
            sin = jnp.repeat(jnp.sin(ang), 2, axis=-1)[None, :, None, :]
            cos = jnp.repeat(jnp.cos(ang), 2, axis=-1)[None, :, None, :]
            x1 = t[..., ::2]
            x2 = t[..., 1::2]
            rot = jnp.stack((-x2, x1), axis=-1).reshape(t.shape)
            return t * cos + rot * sin
        B, T, C = x.shape
        h, d, r = (N_HEAD, HEAD, RATIO)
        hq = r * h
        qkvg = x @ w_attn
        q = qkvg[..., :hq * d].reshape(B, T, hq, d)
        k = qkvg[..., hq * d:(hq + h) * d].reshape(B, T, h, d)
        v = qkvg[..., (hq + h) * d:QKV].reshape(B, T, h, d)
        log_g = jax.nn.log_sigmoid(6.906768 + qkvg[..., QKV:])
        q = _rope(q)
        k = _rope(k)
        k = jnp.repeat(k, r, axis=2)
        v = jnp.repeat(v, r, axis=2)
        log_G = jnp.repeat(jnp.cumsum(log_g, axis=1), r, axis=2).transpose(0, 2, 1)
        scale = 1.0 / d ** 0.5
        s = jnp.einsum('bthd,bshd->bhts', q, k) * scale
        logits = DEG * jnp.log(jnp.abs(s) + 1e-30) + log_G[:, :, :, None] - log_G[:, :, None, :]
        mask = jnp.tril(jnp.ones((T, T), dtype=bool))
        logits = jnp.where(mask, logits, -jnp.inf)
        m = jax.lax.stop_gradient(jnp.max(logits, axis=-1, keepdims=True))
        a = jnp.exp(logits - m)
        if DEG % 2 == 1:
            a = a * jnp.sign(s)
        a = jnp.where(mask, a, 0.0)
        num = jnp.einsum('bhts,bshd->bthd', a, v)
        den = jnp.sum(a, axis=-1).transpose(0, 2, 1)
        y = num / (den[..., None] + 1e-06)
        mu = jnp.mean(y, axis=-1, keepdims=True)
        var = jnp.mean((y - mu) ** 2, axis=-1, keepdims=True)
        y = (y - mu) / jnp.sqrt(var + 1e-09) * ln_w
        return y.reshape(B, T, hq * d) @ w_proj

    def _L0_xattn_ref(query, key, value, w_q, w_k, w_v, w_o):
        import jax, jax.numpy as jnp
        import numpy as np
        HIDDEN = 256
        HEADS = 16
        HEAD_DIM = 64
        B, Q, _ = query.shape
        Kl = key.shape[1]
        scale = HEAD_DIM ** (-0.5)
        q = (query @ w_q).reshape(B, Q, HEADS, HEAD_DIM).transpose(0, 2, 1, 3)
        k = (key @ w_k).reshape(B, Kl, HEADS, HEAD_DIM).transpose(0, 2, 1, 3)
        v = (value @ w_v).reshape(B, Kl, HEADS, HEAD_DIM).transpose(0, 2, 1, 3)
        scores = jnp.einsum('bhqd,bhkd->bhqk', q, k) * scale
        attn = jax.nn.softmax(scores, axis=-1)
        out = jnp.einsum('bhqk,bhkd->bhqd', attn, v)
        out = out.transpose(0, 2, 1, 3).reshape(B, Q, HEADS * HEAD_DIM)
        return out @ w_o

    def _L0_ffn_ref(x, gate_w, w1, w2):
        import jax, jax.numpy as jnp
        import numpy as np
        D_MODEL, D_FF, N_EXPERTS, TOP_K = (256, 512, 8, 2)
        B, S = (2, 512)
        router_logits = jnp.einsum('bsd,de->bse', x, gate_w)
        top_logits, top_idx = jax.lax.top_k(router_logits, TOP_K)
        top_w = jax.nn.softmax(top_logits, axis=-1)
        combine = jnp.sum(jax.nn.one_hot(top_idx, N_EXPERTS, dtype=x.dtype) * top_w[..., None], axis=-2)
        h = jax.nn.silu(jnp.einsum('bsd,edf->ebsf', x, w1))
        y = jnp.einsum('ebsf,efd->ebsd', h, w2)
        out = jnp.einsum('ebsd,bse->bsd', y, combine)
        return out
    x = x + _L0_attn_ref(_layernorm(x, axis=-1), L0_attn_w_attn, L0_attn_w_proj, L0_attn_ln_w)
    x = x + _L0_xattn_ref(_layernorm(x, axis=-1), ctx_1024, ctx_1024, L0_xattn_w_q, L0_xattn_w_k, L0_xattn_w_v, L0_xattn_w_o)
    x = x + _L0_ffn_ref(_layernorm(x, axis=-1), L0_ffn_gate_w, L0_ffn_w1, L0_ffn_w2)
    return x

_drawn_inputs = setup_inputs


def setup_inputs(seed=0):
    import zlib

    import numpy as np

    out = dict(_drawn_inputs(seed))
    spreads = {'L0_attn_ln_w': (1.0, 0.2)}
    factors = {}
    for name, (base, spread) in spreads.items():
        noise = np.random.default_rng([zlib.crc32(name.encode()), seed]).standard_normal(out[name].shape)
        drawn = base * np.exp(spread * noise) if base else spread * noise
        out[name] = jnp.asarray(drawn.astype(out[name].dtype))
    for name, factor in factors.items():
        out[name] = (out[name] * factor).astype(out[name].dtype)
    return out
```

```python
from contextlib import ExitStack

import concourse.bass as bass
import numpy as np
from concourse import mybir

ALU = mybir.AluOpType
ACT = mybir.ActivationFunctionType
AX = mybir.AxisListType
F32 = mybir.dt.float32
F32R = mybir.dt.float32r
BF16 = mybir.dt.bfloat16

P = 128
D = 256
KD = D // P
HD = 64
NQ, NKV = 16, 8
RING = 4


class Ring:

    def __init__(self, banks, filled_sem, orders, read_by, before, mids, unroll):
        self.banks, self.filled_sem, self.orders, self.read_by = banks, filled_sem, orders, read_by
        self.base, self.step = {}, unroll * len(orders["mid"])
        assert self.step % RING == 0 and orders["first"][-RING:] == orders["mid"][-RING:]
        n = before
        for kind, count in (("pro", 1), ("first", 1), ("mid", mids), ("last", 1), ("tail", 1)):
            self.base[kind] = n
            n += len(orders[kind]) * count
        self.end = n

    def number(self, it, name):
        return self.base[it.kind] + self.orders[it.kind].index(name) + it.u * len(self.orders[it.kind])

    def start(self, pe, it, name):
        kind, b, at = it.kind, it.b, self.orders[it.kind].index(name) - RING
        while at < 0 and kind != "pro":
            kind, b = {"first": "pro", "mid": "mid", "last": "mid", "tail": "last"}[kind], b - 1
            at += len(self.orders[kind])
        if at >= 0:
            read, a, c = self.read_by[self.orders[kind][at]]
            pe.wait_ge(read, b * a + c)
        return self.banks[self.number(it, name) % RING]

    def wait_filled(self, eng, it, name):
        n = self.number(it, name) + 1
        eng.wait_ge(self.filled_sem, n if it.kind != "mid" else it.m * self.step + n)

    def filled(self, eng, it, name):
        self.wait_filled(eng, it, name)
        return self.banks[self.number(it, name) % RING]


class Turn:

    def __init__(self, kind, b, u=0, m=None, unroll=1):
        self.kind, self.b, self.u, self.m = kind, b, u, m
        self.par = b % 2 if m is None else (1 + u) % 2
        self.cur = kind in ("first", "mid", "last")
        self.nxt = kind in ("pro", "first", "mid")
        self.prev = kind in ("mid", "last", "tail")


def turns(eng, n, unroll):
    yield Turn("pro", -1)
    yield Turn("first", 0)
    with eng.Fori(0, (n - 2) // unroll) as m:
        for u in range(unroll):
            yield Turn("mid", m * unroll + (1 + u), u, m)
    yield Turn("last", n - 1)
    yield Turn("tail", n)


class Shared:

    def __init__(self, nc, ctx, B):
        def sb(name, shape, dt=F32):
            return ctx.enter_context(nc.sbuf_tensor(name, shape, dt))

        self.B = B
        self.sem = lambda name: ctx.enter_context(nc.semaphore(name))
        self.ring = [ctx.enter_context(nc.psum_tensor(f"ring{i}", [P, 512], F32)) for i in range(RING)]
        self.score_bank = [ctx.enter_context(nc.psum_tensor(f"score{i}", [P, 4, P], F32)) for i in range(4)]
        self.ring_filled = self.sem("ring_filled")
        self.x_sb = sb("x_sb", [P, B, D])
        self.ident = sb("ident", [P, P])
        self.pow_half = sb("pow_half", [P, 16])


def self_attention(nc, sh, x, w_attn, w_proj, ln_w2, rope_cos, rope_sin, cross_weights, cross_raw_in, xs_dram, xs_cleared):
    B, x_sb, ident, pow_half, sem = sh.B, sh.x_sb, sh.ident, sh.pow_half, sh.sem
    ring, score_bank, ring_filled = sh.ring, sh.score_bank, sh.ring_filled
    QC, KC = NQ * HD, NKV * HD
    G = QC + 2 * KC

    with ExitStack() as ctx:
        def sb(name, shape, dt=F32):
            return ctx.enter_context(nc.sbuf_tensor(name, shape, dt))

        ident_b = sb("ident_b", [P, P], BF16)
        until = sb("until", [P, P])
        after = sb("after", [P, P])
        hidden_b = sb("hidden_b", [P, 4, P], BF16)
        cos_sb = sb("cos_sb", [P, HD])
        sin_sb = sb("sin_sb", [P, HD])
        lnw_sb = sb("lnw_sb", [P, 1])
        stage = sh.raw[:, 0:KD * (G + 8)].rearrange("p (k n) -> p k n", k=KD)
        wa_hi = sb("wa_hi", [P, KD, G + 8], F32R)
        wa_lo = sb("wa_lo", [P, KD, G + 8], F32R)
        wp_stage = sh.raw[:, KD * (G + 8):KD * (G + 8) + 8 * D].rearrange("p (k n) -> p k n", k=8)
        wp_hi = sb("wp_hi", [P, 8, D], F32R)
        wp_lo = sb("wp_lo", [P, 8, D], F32R)
        vmean = sb("vmean", [P, KD, NKV])
        bn6 = sb("bn6", [P, 6])
        bn2 = sb("bn2", [P, 2])
        vpe = sb("vpe", [P, 1])
        rstd = sb("rstd", [P, 1])
        xn = sb("xn", [P, D])
        xT_hi = sb("xT_hi", [P, KD, P], F32R)
        xT_lo = sb("xT_lo", [P, KD, P], F32R)
        zero_row = sb("zero_row", [P, D])
        t1 = [sb(f"t1_{j}", [P, 8, 2, 32]) for j in range(3)]
        t2 = [sb(f"t2_{j}", [P, 8, 2, 32]) for j in range(3)]
        qr = [sb(f"qr_{j}", [P, 4, P]) for j in range(3)]
        qkT = [sb(f"qkT_{i}", [P, 12, P]) for i in range(2)]
        v_sb = [sb(f"v_{i}", [P, NKV, HD + 1]) for i in range(2)]
        z = sb("z", [P, 8])
        az = sb("az", [P, 8])
        ez = sb("ez", [P, 8])
        sp = sb("sp", [P, 8])
        lg = sb("lg", [P, 8])
        d_rhs = sb("d_rhs", [P, 8, P])
        decay = [sb(f"decay_{i}", [P, 8, P]) for i in range(2)]
        abs_s = [sb(f"abs_{g}", [P, 4, P]) for g in range(4)]
        r_sb = [sb(f"r_{g}", [P, 4, P]) for g in range(4)]
        rmax = sb("rmax", [P, 16])
        rinv = sb("rinv", [P, 16])
        aT = [sb(f"aT_{i}", [P, 4, P]) for i in range(2)]
        y_sb = sb("y_sb", [P, 16, HD + 1])
        sq = sb("sq", [P, 16, HD])
        ms = sb("ms", [P, 16])
        den = sb("den", [P, 16])
        den2 = sb("den2", [P, 16])
        var_y = sb("var_y", [P, 16])
        f_sb = sb("f_sb", [P, 16])
        yn = sb("yn", [P, 8, P])
        yT_hi = sb("yT_hi", [P, 8, P], F32R)
        yT_lo = sb("yT_lo", [P, 8, P], F32R)

        x_in = [sem("x_in0"), sem("x_in1")]
        w_in, wp_in, tab_in = sem("w_in"), sem("wp_in"), sem("tab_in")
        const_done, const_step = sem("const_done"), sem("const_step")
        ident_done = sem("ident_done")
        vmean_done, vcent_done, wa_hi_done, wa_done, wp_scaled, wp_hi_done, wp_done = (
            sem(n) for n in ("vmean_done", "vcent_done", "wa_hi_done", "wa_done", "wp_scaled", "wp_hi_done", "wp_done"))
        bn6_done, bn6_seen, bn2_done, vpe_done, rstd_done, xn_done = (sem(n) for n in ("bn6_done", "bn6_seen", "bn2_done", "vpe_done", "rstd_done", "xn_done"))
        xT_hi_done, xT_done = sem("xT_hi_done"), sem("xT_done")
        rope_done, rope_added, qkT_done, v_done = (sem(n) for n in ("rope_done", "rope_added", "qkT_done", "v_done"))
        z_done, az_done, ez_done, sp_done, lg_done, drhs_done, decay_done = (
            sem(n) for n in ("z_done", "az_done", "ez_done", "sp_done", "lg_done", "drhs_done", "decay_done"))
        scores_done, abs_done, r_done, rmax_done, rinv_done, b_done, aT_done = (
            sem(n) for n in ("scores_done", "abs_done", "r_done", "rmax_done", "rinv_done", "b_done", "aT_done"))
        y_done, sq_done, ms_done, den_done, den2_done, var_done, f_done, yn_done = (
            sem(n) for n in ("y_done", "sq_done", "ms_done", "den_done", "den2_done", "var_done", "f_done", "yn_done"))
        yT_hi_done, yT_done, x_added = sem("yT_hi_done"), sem("yT_done"), sem("x_added")

        jobs = Ring(ring, ring_filled, {
            "pro": ["xT", "q0", "q1", "g", "k", "v", "QT0", "QT1", "D0", "QT2", "D1"],
            "first": ["xT", "tr0", "q0", "q1", "tr1", "g", "k", "AV0", "v", "tr2", "AV1", "QT0", "tr3", "QT1",
                      "AV2", "D0", "QT2", "D1", "AV3"],
            "mid": ["yT0", "yT1", "xT", "tr0", "q0", "q1", "wproj", "tr1", "g", "k", "AV0", "v", "tr2", "AV1", "QT0",
                    "tr3", "QT1", "AV2", "D0", "QT2", "D1", "AV3"],
            "last": ["yT0", "yT1", "tr0", "wproj", "tr1", "AV0", "tr2", "AV1", "tr3", "AV2", "AV3"],
            "tail": ["yT0", "yT1", "wproj"],
        }, {
            "yT0": (yT_done, 2, -1), "yT1": (yT_done, 2, 0), "wproj": (x_added, 1, 0), "xT": (xT_done, 1, 2),
            "q0": (rope_done, 3, 4), "q1": (rope_done, 3, 5), "k": (rope_done, 3, 6), "g": (z_done, 1, 2),
            "v": (v_done, 1, 2), "QT0": (qkT_done, 3, 4), "QT1": (qkT_done, 3, 5), "QT2": (qkT_done, 3, 6),
            "D0": (decay_done, 2, 3), "D1": (decay_done, 2, 4),
            **{f"tr{g}": (aT_done, 4, g + 1) for g in range(4)}, **{f"AV{g}": (y_done, 4, g + 1) for g in range(4)},
        }, 0, B - 2, 2)
        start, filled = jobs.start, jobs.filled

        block = ctx.enter_context(nc.Block())

        @block.sync
        def _(sp_):
            xv = x.rearrange("b t d -> t b d")
            sp_.dma_start(x_sb[:, 0:2, :], xv[:, 0:2, :]).then_inc(x_in[0], 16)
            sp_.dma_start(stage, w_attn.rearrange("(k p) n -> p k n", p=P)).then_inc(w_in, 16)
            sp_.dma_start(cos_sb[:], rope_cos).then_inc(tab_in, 16)
            sp_.dma_start(sin_sb[:], rope_sin).then_inc(tab_in, 16)
            sp_.dma_start(lnw_sb[:], ln_w2).then_inc(tab_in, 16)
            sp_.dma_start(wp_stage, w_proj.rearrange("(k p) n -> p k n", p=P)).then_inc(wp_in, 16)
            sp_.dma_start(x_sb[:, 2:B, :], xv[:, 2:B, :]).then_inc(x_in[1], 16)
            sp_.wait_ge(wa_done, KD)
            sp_.wait_ge(wp_done, 1)
            for n, w in enumerate(cross_weights):
                sp_.dma_start(sh.raw[:, 2048 * n:2048 * n + 2048].rearrange("p (k n) -> p k n", n=w.shape[1]),
                              w.rearrange("(k p) n -> p k n", p=P)).then_inc(cross_raw_in, 16)
            sp_.wait_ge(const_done, 1)
            for xs in xs_dram:
                sp_.dma_start(xs.rearrange("(n p) d -> p n d", p=P),
                              zero_row[:].rearrange("p (o d) -> p o d", o=1).to_broadcast([P, xs.shape[0] // P, D])).then_inc(xs_cleared, 16)
            sp_.wait_ge(xs_cleared, 32)

        @block.tensor
        def _(pe):
            def project(out, a_hi, a_lo, w_hi, w_lo, cols, K):
                for k in range(K):
                    nc.tensor.matmul(out, a_hi[:, k, :], w_lo[:, k, cols], start=(k == 0), stop=False)
                    nc.tensor.matmul(out, a_lo[:, k, :], w_hi[:, k, cols], start=False, stop=False)
                    last = nc.tensor.matmul(out, a_hi[:, k, :], w_hi[:, k, cols], start=False, stop=(k == K - 1))
                return last

            def scores(it, o):
                b, qk = it.b, qkT[it.par]
                if o == 0:
                    pe.wait_ge(qkT_done, 3 * (b + 1))
                if it.kind != "first":
                    pe.wait_ge(abs_done, 4 * b + (2 * o - 2))
                for k in range(4):
                    for half in range(2):
                        rows = slice(64 * half, 64 * half + 64)
                        last = nc.tensor.matmul(score_bank[2 * o + half][:, k, :], qk[rows, 4 * o + k, :],
                                                qk[rows, 8 + k, :], start=True, stop=True)
                last.then_inc(scores_done, 1)

            def turn_rows(it, g):
                bank = start(pe, it, f"tr{g}")
                pe.wait_ge(b_done, 4 * it.b + (g + 1))
                for k in range(4):
                    last = nc.tensor.transpose(bank[:, k * P:(k + 1) * P], r_sb[g][:, k, :], ident[:])
                last.then_inc(ring_filled, 1)

            def attend(it, g):
                bank = start(pe, it, f"AV{g}")
                pe.wait_ge(aT_done, 4 * it.b + (g + 1))
                if g == 0:
                    pe.wait_ge(v_done, it.b + 1)
                half = g % 2
                for k in range(4):
                    last = nc.tensor.matmul(bank[:, k * 65:(k + 1) * 65], aT[g % 2][:, k, :],
                                            v_sb[it.par][:, 4 * half + k, :], start=True, stop=True)
                last.then_inc(ring_filled, 1)

            def qk_cols(it, name, c0, n):
                bank = start(pe, it, name)
                project(bank[:, 0:n], xT_hi, xT_lo, wa_hi, wa_lo, slice(c0, c0 + n), KD).then_inc(ring_filled, 1)

            def qk_turn(it, j):
                bank = start(pe, it, f"QT{j}")
                pe.wait_ge(rope_added, 3 * it.b + (4 + j))
                for c in range(4):
                    last = nc.tensor.transpose(bank[:, c * P:(c + 1) * P], qr[j][:, c, :], ident[:])
                last.then_inc(ring_filled, 1)

            def decays(it, j):
                bank = start(pe, it, f"D{j}")
                pe.wait_ge(drhs_done, it.b + 2)
                nc.tensor.matmul(bank[:, :], until[:], d_rhs[:, 4 * j:4 * j + 4, :], start=True, stop=False)
                nc.tensor.matmul(bank[:, :], ident_b[:], hidden_b[:, :, :], start=False, stop=True).then_inc(ring_filled, 1)

            pe.wait_ge(ident_done, 1)
            pe.wait_ge(const_done, 1)
            pe.wait_ge(wa_done, KD)
            for it in turns(pe, B, 2):
                if it.kind == "first":
                    pe.wait_ge(wp_done, 1)
                if it.cur:
                    scores(it, 0)
                    scores(it, 1)
                if it.prev:
                    for j in range(2):
                        bank = start(pe, it, f"yT{j}")
                        pe.wait_ge(yn_done, it.b)
                        for c in range(4):
                            last = nc.tensor.transpose(bank[:, c * P:(c + 1) * P], yn[:, 4 * j + c, :], ident[:])
                        last.then_inc(ring_filled, 1)
                if it.nxt:
                    bank = start(pe, it, "xT")
                    pe.wait_ge(xn_done, it.b + 2)
                    for k in range(KD):
                        last = nc.tensor.transpose(bank[:, k * P:(k + 1) * P], xn[:, k * P:(k + 1) * P], ident[:])
                    last.then_inc(ring_filled, 1)
                if it.cur:
                    turn_rows(it, 0)
                if it.nxt:
                    pe.wait_ge(xT_done, it.b + 2)
                    qk_cols(it, "q0", 0, 512)
                    qk_cols(it, "q1", 512, 512)
                if it.prev:
                    bank = start(pe, it, "wproj")
                    pe.wait_ge(yT_done, 2 * it.b)
                    project(bank[:, 0:D], yT_hi, yT_lo, wp_hi, wp_lo, slice(0, D), 8).then_inc(ring_filled, 1)
                if it.cur:
                    turn_rows(it, 1)
                if it.nxt:
                    qk_cols(it, "g", G, 8)
                    qk_cols(it, "k", QC, 512)
                if it.cur:
                    attend(it, 0)
                if it.nxt:
                    qk_cols(it, "v", QC + KC, 512)
                if it.cur:
                    turn_rows(it, 2)
                    attend(it, 1)
                if it.nxt:
                    qk_turn(it, 0)
                if it.cur:
                    turn_rows(it, 3)
                if it.nxt:
                    qk_turn(it, 1)
                if it.cur:
                    attend(it, 2)
                if it.nxt:
                    decays(it, 0)
                    qk_turn(it, 2)
                    decays(it, 1)
                if it.cur:
                    attend(it, 3)

        @block.scalar
        def _(act):
            def take_turn(it, g):
                bank = filled(act, it, f"tr{g}")
                if it.kind != "first" or g >= 2:
                    if g >= 2:
                        jobs.wait_filled(act, it, f"AV{g - 2}")
                nc.scalar.activation(aT[g % 2][:, :, :].rearrange("p a b -> p (a b)"), bank[:, :], ACT.Square).then_inc(aT_done, 1)

            def take_rows(it, g):
                bank = filled(act, it, f"AV{g}")
                if it.kind != "first" and g == 0:
                    act.wait_ge(yn_done, it.b)
                nc.scalar.copy(y_sb[:, 4 * g:4 * g + 4, :].rearrange("p a b -> p (a b)"), bank[:, 0:260]).then_inc(y_done, 1)

            def take_qk(it, j):
                bank = filled(act, it, f"QT{j}")
                nc.scalar.copy(qkT[1 - it.par][:, 4 * j:4 * j + 4, :].rearrange("p a b -> p (a b)"), bank[:, :]).then_inc(qkT_done, 1)

            def take_decay(it, j):
                bank = filled(act, it, f"D{j}")
                if it.cur:
                    act.wait_ge(r_done, 4 * it.b)
                nc.scalar.activation(decay[1 - it.par][:, 4 * j:4 * j + 4, :].rearrange("p a b -> p (a b)"), bank[:, :],
                                     ACT.Exp, scale=0.5).then_inc(decay_done, 1)

            for k in range(KD):
                act.wait_ge(w_in, 16)
                act.wait_ge(vcent_done, 1)
                nc.scalar.copy(wa_hi[:, k, :], stage[:, k, :]).then_inc(wa_hi_done, 1)
            act.wait_ge(wp_scaled, 1)
            nc.scalar.copy(wp_hi[:], wp_stage).then_inc(wp_hi_done, 1)
            for it in turns(act, B, 2):
                if it.cur:
                    for g in range(4):
                        act.wait_ge(scores_done, 2 * it.b + (1 + g // 2))
                        if it.kind != "first":
                            act.wait_ge(r_done, 4 * it.b + (g - 3))
                        nc.scalar.activation(abs_s[g][:], score_bank[g][:], ACT.Abs, scale=HD ** -0.5).then_inc(abs_done, 1)
                if it.prev:
                    for j in range(2):
                        bank = filled(act, it, f"yT{j}")
                        nc.scalar.copy(yT_hi[:, 4 * j:4 * j + 4, :].rearrange("p a b -> p (a b)"), bank[:, :]).then_inc(yT_hi_done, 1)
                if it.nxt:
                    bank = filled(act, it, "xT")
                    nc.scalar.copy(xT_hi[:].rearrange("p a b -> p (a b)"), bank[:, 0:D]).then_inc(xT_hi_done, 1)
                if it.cur:
                    take_turn(it, 0)
                    take_turn(it, 1)
                if it.nxt:
                    act.wait_ge(z_done, it.b + 2)
                    nc.scalar.activation(az[:], z[:], ACT.Abs).then_inc(az_done, 1)
                    act.wait_ge(az_done, it.b + 2)
                    nc.scalar.activation(ez[:], az[:], ACT.Exp, scale=-1.0).then_inc(ez_done, 1)
                    act.wait_ge(ez_done, it.b + 2)
                    nc.scalar.activation(sp[:], ez[:], ACT.Ln, bias=1.0).then_inc(sp_done, 1)
                if it.cur:
                    take_rows(it, 0)
                if it.nxt:
                    bank = filled(act, it, "v")
                    nc.scalar.copy(v_sb[1 - it.par][:, :, 0:HD], bank[:, :].rearrange("p (h d) -> p h d", d=HD)).then_inc(v_done, 1)
                if it.cur:
                    take_turn(it, 2)
                    take_rows(it, 1)
                if it.nxt:
                    take_qk(it, 0)
                if it.cur:
                    take_turn(it, 3)
                if it.nxt:
                    take_qk(it, 1)
                if it.cur:
                    take_rows(it, 2)
                if it.nxt:
                    take_decay(it, 0)
                    take_qk(it, 2)
                    take_decay(it, 1)
                if it.cur:
                    take_rows(it, 3)

        @block.vector
        def _(dve):
            def rope(it, j, name):
                bank = filled(dve, it, name)
                if it.kind != "pro":
                    dve.wait_ge(rope_added, 3 * it.b + (1 + j))
                q = bank[:, :].rearrange("p (h e i) -> p h e i", e=2, i=32)
                cosb = cos_sb[:, :].rearrange("p (o n) -> p o n", o=1).to_broadcast([P, 8, HD])
                nc.vector.tensor_tensor(t1[j][:].rearrange("p h e i -> p h (e i)"), q.rearrange("p h e i -> p h (e i)"), cosb, ALU.mult)
                for e in range(2):
                    sinb = sin_sb[:, 32 * e:32 * e + 32].rearrange("p (o n) -> p o n", o=1).to_broadcast([P, 8, 32])
                    last = nc.vector.tensor_tensor(t2[j][:, :, e, :], q[:, :, 1 - e, :], sinb, ALU.mult)
                last.then_inc(rope_done, 1)

            def weigh(it, g):
                b, half = it.b, g % 2
                dve.wait_ge(abs_done, 4 * b + (g + 1))
                if g == 0:
                    dve.wait_ge(decay_done, 2 * b + 2)
                if it.kind != "first":
                    dve.wait_ge(aT_done, 4 * b + (g - 3))
                nc.vector.scalar_tensor_tensor(
                    out=r_sb[g][:], in0=abs_s[g][:], scalar=1e-30, in1=decay[it.par][:, 4 * half:4 * half + 4, :],
                    op0=ALU.add, op1=ALU.mult).then_inc(r_done, 1)
                dve.wait_ge(r_done, 4 * b + (g + 1))
                nc.vector.tensor_reduce(rmax[:, 4 * g:4 * g + 4], r_sb[g][:], AX.X, ALU.max).then_inc(rmax_done, 1)
                dve.wait_ge(rmax_done, 4 * b + (g + 1))
                nc.vector.reciprocal(rinv[:, 4 * g:4 * g + 4], rmax[:, 4 * g:4 * g + 4]).then_inc(rinv_done, 1)

            def square_sums(it, g):
                dve.wait_ge(sq_done, 4 * it.b + (g + 1))
                nc.vector.tensor_reduce(ms[:, 4 * g:4 * g + 4], sq[:, 4 * g:4 * g + 4, :], AX.X, ALU.add).then_inc(ms_done, 1)

            dve.wait_ge(w_in, 16)
            vv = stage[:, :, QC + KC:G].rearrange("p k (h d) -> p k h d", d=HD)
            for k in range(KD):
                last = nc.vector.tensor_reduce(vmean[:, k, :], vv[:, k, :, :], AX.X, ALU.add)
            last.then_inc(vmean_done, 1)
            dve.wait_ge(vmean_done, 1)
            last = nc.vector.tensor_scalar(vmean[:], vmean[:], 1.0 / HD, None, ALU.mult)
            last.then_inc(vmean_done, 1)
            dve.wait_ge(vmean_done, 2)
            for k in range(KD):
                last = nc.vector.tensor_tensor(vv[:, k, :, :], vv[:, k, :, :],
                                               vmean[:, k, :].rearrange("p (h o) -> p h o", o=1).to_broadcast([P, NKV, HD]),
                                               ALU.subtract)
            last.then_inc(vcent_done, 1)
            dve.wait_ge(vcent_done, 1)
            for k in range(KD):
                dve.wait_ge(wa_hi_done, k + 1)
                nc.vector.tensor_tensor(wa_lo[:, k, :], stage[:, k, :], wa_hi[:, k, :].bitcast(F32), ALU.subtract).then_inc(wa_done, 1)
            dve.wait_ge(wp_in, 16)
            dve.wait_ge(tab_in, 48)
            nc.vector.tensor_scalar(wp_stage, wp_stage, lnw_sb[:, 0:1], float(HD) ** 0.5, ALU.mult, ALU.mult).then_inc(wp_scaled, 1)
            dve.wait_ge(wp_scaled, 1)
            dve.wait_ge(wp_hi_done, 1)
            nc.vector.tensor_tensor(wp_lo[:], wp_stage, wp_hi[:].bitcast(F32), ALU.subtract).then_inc(wp_done, 1)

            for it in turns(dve, B, 2):
                if it.kind == "pro":
                    dve.wait_ge(x_in[0], 16)
                if it.kind == "first":
                    dve.wait_ge(x_in[1], 16)
                if it.nxt:
                    xb = x_sb[:, it.b + 1, :]
                    nc.vector.bn_stats(bn6[:], xb).then_inc(bn6_done, 1)
                    dve.wait_ge(bn6_done, it.b + 2)
                    dve.sem_inc(bn6_seen, 1)
                    nc.vector.bn_aggr(bn2[:], bn6[:]).then_inc(bn2_done, 1)
                    dve.wait_ge(bn2_done, it.b + 2)
                    nc.vector.tensor_scalar(vpe[:], bn2[:, 1:2], 1e-5, None, ALU.add).then_inc(vpe_done, 1)
                if it.cur:
                    weigh(it, 0)
                if it.nxt:
                    dve.wait_ge(rstd_done, it.b + 2)
                    nc.vector.tensor_scalar(xn[:], xb, bn2[:, 0:1], rstd[:, 0:1], ALU.subtract, ALU.mult).then_inc(xn_done, 1)
                if it.cur:
                    weigh(it, 1)
                if it.prev:
                    for j in range(2):
                        bank = filled(dve, it, f"yT{j}")
                        dve.wait_ge(yT_hi_done, 2 * it.b + (j - 1))
                        cols = slice(4 * j, 4 * j + 4)
                        nc.vector.tensor_tensor(yT_lo[:, cols, :].rearrange("p a b -> p (a b)"), bank[:, :],
                                                yT_hi[:, cols, :].bitcast(F32).rearrange("p a b -> p (a b)"), ALU.subtract).then_inc(yT_done, 1)
                if it.nxt:
                    bank = filled(dve, it, "xT")
                    dve.wait_ge(xT_hi_done, it.b + 2)
                    nc.vector.tensor_tensor(xT_lo[:].rearrange("p a b -> p (a b)"), bank[:, 0:D],
                                            xT_hi[:].bitcast(F32).rearrange("p a b -> p (a b)"), ALU.subtract).then_inc(xT_done, 1)
                if it.cur:
                    weigh(it, 2)
                    weigh(it, 3)
                if it.nxt:
                    rope(it, 0, "q0")
                    rope(it, 1, "q1")
                if it.prev:
                    bank = filled(dve, it, "wproj")
                    xp = x_sb[:, it.b - 1, :]
                    nc.vector.tensor_tensor(xp, xp, bank[:, 0:D], ALU.add).then_inc(x_added, 1)
                if it.nxt:
                    bank = filled(dve, it, "g")
                    nc.vector.tensor_scalar(z[:], bank[:, 0:8], 6.906768, None, ALU.add).then_inc(z_done, 1)
                    rope(it, 2, "k")
                    dve.wait_ge(sp_done, it.b + 2)
                    nc.vector.scalar_tensor_tensor(out=lg[:], in0=z[:], scalar=0.0, in1=sp[:], op0=ALU.min,
                                                   op1=ALU.subtract).then_inc(lg_done, 1)
                if it.cur:
                    dve.wait_ge(y_done, 4 * it.b + 4)
                    nc.vector.tensor_scalar(den[:].rearrange("p (h o) -> p h o", o=1), y_sb[:, :, HD:HD + 1], 1e-6,
                                            (1e-9 * HD) ** 0.5, ALU.add, ALU.mult).then_inc(den_done, 1)
                    dve.wait_ge(den_done, it.b + 1)
                    nc.vector.tensor_tensor(den2[:], den[:], den[:], ALU.mult).then_inc(den2_done, 1)
                    for g in range(4):
                        square_sums(it, g)
                    dve.wait_ge(den2_done, it.b + 1)
                    dve.wait_ge(ms_done, 4 * it.b + 4)
                    if it.kind != "first":
                        dve.wait_ge(f_done, it.b)
                    nc.vector.tensor_tensor(var_y[:], den2[:], ms[:], ALU.add).then_inc(var_done, 1)

        @block.gpsimd
        def _(pool):
            def scale_rows(it, g):
                pool.wait_ge(rinv_done, 4 * it.b + (g + 1))
                r = r_sb[g][:]
                nc.gpsimd.tensor_tensor(r, r, rinv[:, 4 * g:4 * g + 4].rearrange("p (h o) -> p h o", o=1).to_broadcast([P, 4, P]),
                                        ALU.mult).then_inc(b_done, 1)

            def rope_add(it, j):
                pool.wait_ge(rope_done, 3 * it.b + (4 + j))
                if it.kind != "pro":
                    pool.wait_ge(qkT_done, 3 * it.b + (1 + j))
                nc.gpsimd.tensor_tensor(qr[j][:].rearrange("p c n -> p (c n)"), t1[j][:].rearrange("p h e i -> p (h e i)"),
                                        t2[j][:].rearrange("p h e i -> p (h e i)"), ALU.add).then_inc(rope_added, 1)

            def squares(it, g):
                pool.wait_ge(y_done, 4 * it.b + (g + 1))
                ys = y_sb[:, 4 * g:4 * g + 4, 0:HD]
                if it.kind != "first":
                    pool.wait_ge(ms_done, 4 * it.b + (g - 3))
                nc.gpsimd.tensor_tensor(sq[:, 4 * g:4 * g + 4, :], ys, ys, ALU.mult).then_inc(sq_done, 1)

            nc.gpsimd.memset(ident[:], 0.0).then_inc(const_step, 1)
            nc.gpsimd.memset(zero_row[:], 0.0).then_inc(const_step, 1)
            nc.gpsimd.memset(until[:], 1.0).then_inc(const_step, 1)
            nc.gpsimd.memset(after[:], 1.0).then_inc(const_step, 1)
            nc.gpsimd.memset(hidden_b[:], 0.0).then_inc(const_step, 1)
            nc.gpsimd.memset(pow_half[:], -0.5).then_inc(const_step, 1)
            for v in v_sb:
                nc.gpsimd.memset(v[:], 1.0).then_inc(const_step, 1)
            pool.wait_ge(const_step, 8)
            nc.gpsimd.affine_select(out=ident[:], in_=ident[:], compare_op=ALU.not_equal, fill=1.0, base=0,
                                    pattern=[[-1, P]], channel_multiplier=1).then_inc(const_step, 1)
            nc.gpsimd.affine_select(out=until[:], in_=until[:], compare_op=ALU.is_ge, fill=0.0, base=0,
                                    pattern=[[1, P]], channel_multiplier=-1).then_inc(const_step, 1)
            nc.gpsimd.affine_select(out=after[:], in_=after[:], compare_op=ALU.is_ge, fill=0.0, base=-1,
                                    pattern=[[-1, P]], channel_multiplier=1).then_inc(const_step, 1)
            nc.gpsimd.affine_select(out=hidden_b[:], in_=hidden_b[:], compare_op=ALU.is_ge, fill=-30000.0, base=0,
                                    pattern=[[0, 4], [-1, P]], channel_multiplier=1).then_inc(const_step, 1)
            pool.wait_ge(const_step, 12)
            nc.gpsimd.tensor_copy(ident_b[:], ident[:]).then_inc(const_step, 1)
            pool.wait_ge(const_step, 13)
            pool.sem_inc(ident_done, 1)
            pool.sem_inc(const_done, 1)

            for it in turns(pool, B, 2):
                if it.nxt:
                    pool.wait_ge(vpe_done, it.b + 2)
                    nc.gpsimd.tensor_tensor(rstd[:], vpe[:], pow_half[:, 0:1], ALU.pow).then_inc(rstd_done, 1)
                if it.cur:
                    for g in range(4):
                        scale_rows(it, g)
                if it.nxt:
                    rope_add(it, 0)
                    rope_add(it, 1)
                    rope_add(it, 2)
                    pool.wait_ge(lg_done, it.b + 2)
                    if it.kind != "pro":
                        pool.wait_ge(decay_done, 2 * it.b + 2)
                    nc.gpsimd.tensor_tensor(d_rhs[:], after[:].rearrange("p (o n) -> p o n", o=1).to_broadcast([P, 8, P]),
                                            lg[:].rearrange("p (h o) -> p h o", o=1).to_broadcast([P, 8, P]),
                                            ALU.mult).then_inc(drhs_done, 1)
                if it.cur:
                    for g in range(4):
                        squares(it, g)
                    pool.wait_ge(var_done, it.b + 1)
                    nc.gpsimd.tensor_tensor(f_sb[:], var_y[:], pow_half[:], ALU.pow).then_inc(f_done, 1)
                    pool.wait_ge(f_done, it.b + 1)
                    if it.kind != "first":
                        pool.wait_ge(yT_hi_done, 2 * it.b)
                    nc.gpsimd.tensor_tensor(yn[:].rearrange("p c (h d) -> p (c h) d", d=HD), y_sb[:, :, 0:HD],
                                            f_sb[:].rearrange("p (h o) -> p h o", o=1).to_broadcast([P, 16, HD]),
                                            ALU.mult).then_inc(yn_done, 1)
    return jobs.end


def cross_attention(nc, sh, jobs_before, ctx_x, raw_in, w1, w1_in):
    B, x_sb, ident, pow_half, sem = sh.B, sh.x_sb, sh.ident, sh.pow_half, sh.sem
    ring, score_bank, ring_filled = sh.ring, sh.score_bank, sh.ring_filled
    PAIRS = B // 2
    KO = 8

    with ExitStack() as ctx:
        def sb(name, shape, dt=F32):
            return ctx.enter_context(nc.sbuf_tensor(name, shape, dt))

        w_raw = [sh.raw[:, 2048 * n:2048 * n + 2048] for n in range(4)]
        w_hi = [sb(f"cw_hi{n}", [P, 2048], F32R) for n in range(4)]
        w_lo = [sb(f"cw_lo{n}", [P, 2048], F32R) for n in range(4)]
        c_sb = sb("c_sb", [P, 2, D])
        bn6 = sb("c_bn6", [P, 2, 6])
        bn2 = sb("c_bn2", [P, 2, 2])
        vpe = sb("c_vpe", [P, 2])
        rstd = sb("c_rstd", [P, 2])
        xn = sb("c_xn", [P, 2, D])
        inT_hi = {n: sb(f"{n}T_hi2", [P, KD, 2, P], F32R) for n in "xc"}
        inT_lo = {n: sb(f"{n}T_lo2", [P, KD, 2, P], F32R) for n in "xc"}
        qT = sb("qT", [P, 8, 2 * P])
        kT = sb("kT", [P, 8, 2 * P])
        v_sb = [sb(f"c_v{u}", [P, 16 * HD]) for u in range(2)]
        p_sb = [sb(f"p_{i}", [P, 4, P]) for i in range(4)]
        smax = sb("smax", [P, 4, 4])
        den = sb("c_den", [P, 4, 4])
        rden = sb("rden", [P, 4, 4])
        pT = [sb(f"pT_{i}", [P, 4, P]) for i in range(2)]
        oT_hi = [sb(f"oT_hi{u}", [P, 8, P], F32R) for u in range(2)]
        oT_lo = [sb(f"oT_lo{u}", [P, 8, P], F32R) for u in range(2)]

        w_hi_done, w_done, c_in = sem("cw_hi_done"), sem("cw_done"), sem("c_in")
        bn6_done, bn6_seen, bn2_done, vpe_done, rstd_done, xn_done = (
            sem(f"c_{n}") for n in ("bn6_done", "bn6_seen", "bn2_done", "vpe_done", "rstd_done", "xn_done"))
        xT_hi_done, xT_done, cT_hi_done, cT_done = (sem(f"c_{n}") for n in ("xT_hi_done", "xT_done", "cT_hi_done", "cT_done"))
        q_done, k_done, v_done = (sem(f"c_{n}") for n in ("q_done", "k_done", "v_done"))
        scores_done, smax_done, sub_done, exp_done, den_done, rden_done, norm_done, pT_done = (
            sem(f"c_{n}") for n in ("scores_done", "smax_done", "sub_done", "exp_done", "den_done", "rden_done", "norm_done", "pT_done"))
        oT_hi_done, oT_done, x_added = (sem(f"c_{n}") for n in ("oT_hi_done", "oT_done", "x_added"))

        mid = ["trA3", "trB3", "q2", "q3", "AV3", "wo0",
               "trA0", "trB0", "k2", "k3", "AV0", "wo1", "v01", "v11",
               "xT", "cT", "trA1", "trB1", "q0", "q1", "AV1",
               "trA2", "trB2", "k0", "k1", "AV2", "v00", "v10"]
        last_turn = ("trA3", "trB3", "AV3", "wo0", "wo1")
        next_turn = ("xT", "cT", "q0", "q1", "k0", "k1", "v00", "v10")
        jobs = Ring(ring, ring_filled, {
            "pro": list(next_turn),
            "first": [n for n in mid if n not in last_turn],
            "mid": mid,
            "last": [n for n in mid if n not in next_turn],
            "tail": list(last_turn),
        }, {
            "xT": (xT_done, 1, 2), "cT": (cT_done, 1, 2),
            "q0": (q_done, 4, 5), "q1": (q_done, 4, 6), "q2": (q_done, 4, 3), "q3": (q_done, 4, 4),
            "k0": (k_done, 4, 5), "k1": (k_done, 4, 6), "k2": (k_done, 4, 3), "k3": (k_done, 4, 4),
            "v00": (v_done, 4, 5), "v10": (v_done, 4, 6), "v01": (v_done, 4, 3), "v11": (v_done, 4, 4),
            **{f"tr{'AB'[h]}{t}": (pT_done, 8, 2 * t + h + 1) for t in range(3) for h in range(2)},
            "trA3": (pT_done, 8, -1), "trB3": (pT_done, 8, 0),
            **{f"AV{t}": (oT_done, 4, t + 1) for t in range(3)}, "AV3": (oT_done, 4, 0),
            "wo0": (x_added, 2, -1), "wo1": (x_added, 2, 0),
        }, jobs_before, PAIRS - 2, 1)
        start, filled = jobs.start, jobs.filled

        block = ctx.enter_context(nc.Block())

        @block.sync
        def _(sync):
            def load(it):
                src = ctx_x.rearrange("(n two) t d -> n t two d", two=2)[it.b + 1]
                sync.dma_start(c_sb[:], src).then_inc(c_in, 16)

            for it in turns(sync, PAIRS, 1):
                if it.nxt:
                    if it.kind != "pro":
                        if it.kind == "first":
                            jobs.wait_filled(sync, Turn("pro", -1), "cT")
                        else:
                            sync.wait_ge(cT_hi_done, it.b + 1)
                    load(it)
                if it.kind == "first":
                    sync.wait_ge(w_done, 4)
                    sync.dma_start(sh.raw[:, :].rearrange("p (e k n) -> p e k n", e=w1.shape[0], k=KD),
                                   w1.rearrange("e (k p) n -> p e k n", p=P)).then_inc(w1_in, 16)

        @block.tensor
        def _(pe):
            def three(out, pairs):
                for n, ((a_hi, a_lo), (b_hi, b_lo)) in enumerate(pairs):
                    nc.tensor.matmul(out, a_hi, b_lo, start=(n == 0), stop=False)
                    nc.tensor.matmul(out, a_lo, b_hi, start=False, stop=False)
                    last = nc.tensor.matmul(out, a_hi, b_hi, start=False, stop=(n == len(pairs) - 1))
                return last

            def weight(n, k, c0, c1):
                cols = 1024 if n < 3 else D
                return tuple(w[n][:, k * cols + c0:k * cols + c1] for w in (w_hi, w_lo))

            def turn_in(it, name, tile, ready):
                bank = start(pe, it, f"{name}T")
                pe.wait_ge(ready, (it.b + 2) * (1 if name == "x" else 16))
                for k in range(KD):
                    for u in range(2):
                        last = nc.tensor.transpose(bank[:, (2 * k + u) * P:(2 * k + u + 1) * P],
                                                   tile[:, u, k * P:(k + 1) * P], ident[:])
                last.then_inc(ring_filled, 1)

            def project_T(it, which, j):
                bank = start(pe, it, f"{which}{j}")
                n, src = (0, "x") if which == "q" else (1, "c")
                for c in range(2):
                    last = three(bank[:, c * 2 * P:(c + 1) * 2 * P], [
                        (weight(n, k, (2 * j + c) * P, (2 * j + c + 1) * P),
                         tuple(t[src][:, k, :, :].rearrange("p u t -> p (u t)") for t in (inT_hi, inT_lo)))
                        for k in range(KD)])
                last.then_inc(ring_filled, 1)

            def project_v(it, u, o):
                bank = start(pe, it, f"v{u}{o}")
                three(bank[:, :], [(tuple(t["c"][:, k, u, :] for t in (inT_hi, inT_lo)), weight(2, k, 512 * o, 512 * o + 512))
                                   for k in range(KD)]).then_inc(ring_filled, 1)

            def scores(it, t):
                u, o = t % 2, t // 2
                if t == 0:
                    pe.wait_ge(q_done, 4 * it.b + 2)
                    pe.wait_ge(k_done, 4 * it.b + 2)
                if t == 2:
                    pe.wait_ge(q_done, 4 * it.b + 4)
                    pe.wait_ge(k_done, 4 * it.b + 4)
                if it.kind != "first" or t >= 2:
                    pe.wait_ge(sub_done, 8 * it.b + (2 * t - 2))
                for k in range(4):
                    for half in range(2):
                        rows = slice(64 * half, 64 * half + 64)
                        cols = slice(u * P, (u + 1) * P)
                        last = nc.tensor.matmul(score_bank[2 * (t % 2) + half][:, k, :], qT[rows, 4 * o + k, cols],
                                                kT[rows, 4 * o + k, cols], start=True, stop=True)
                last.then_inc(scores_done, 1)

            def turn_rows(it, t):
                b = it.b - 1 if t == 3 else it.b
                for half in range(2):
                    bank = start(pe, it, f"tr{'AB'[half]}{t}")
                    pe.wait_ge(norm_done, 8 * b + (2 * t + half + 1))
                    for k in range(4):
                        last = nc.tensor.transpose(bank[:, k * P:(k + 1) * P], p_sb[2 * (t % 2) + half][:, k, :], ident[:])
                    last.then_inc(ring_filled, 1)

            def attend(it, t):
                b, u, o = it.b - 1 if t == 3 else it.b, t % 2, t // 2
                bank = start(pe, it, f"AV{t}")
                pe.wait_ge(v_done, 4 * b + (2 if o == 0 else 4))
                pe.wait_ge(pT_done, 8 * b + (2 * t + 2))
                for k in range(4):
                    for half in range(2):
                        h = 8 * o + 2 * k + half
                        last = nc.tensor.matmul(bank[64 * half:64 * half + 64, k * P:(k + 1) * P],
                                                v_sb[u][:, h * HD:(h + 1) * HD], pT[half][:, k, :], start=True, stop=True,
                                                skip_group_check=True)
                last.then_inc(ring_filled, 1)

            def project_out(it, u):
                bank = start(pe, it, f"wo{u}")
                pe.wait_ge(oT_done, 4 * it.b + (-1 if u == 0 else 0))
                three(bank[:, 0:D], [((oT_hi[u][:, k, :], oT_lo[u][:, k, :]), weight(3, k, 0, D))
                                     for k in range(KO)]).then_inc(ring_filled, 1)

            for it in turns(pe, PAIRS, 1):
                if it.kind == "pro":
                    pe.wait_ge(w_done, 4)
                if it.cur:
                    scores(it, 0)
                if it.prev:
                    turn_rows(it, 3)
                if it.cur:
                    project_T(it, "q", 2)
                    project_T(it, "q", 3)
                if it.prev:
                    attend(it, 3)
                    project_out(it, 0)
                if it.cur:
                    scores(it, 1)
                    turn_rows(it, 0)
                    project_T(it, "k", 2)
                    project_T(it, "k", 3)
                    attend(it, 0)
                if it.prev:
                    project_out(it, 1)
                if it.cur:
                    project_v(it, 0, 1)
                    project_v(it, 1, 1)
                    scores(it, 2)
                if it.nxt:
                    turn_in(it, "x", xn, xn_done)
                    turn_in(it, "c", c_sb, c_in)
                if it.cur:
                    turn_rows(it, 1)
                if it.nxt:
                    pe.wait_ge(xT_done, it.b + 2)
                    project_T(it, "q", 0)
                    project_T(it, "q", 1)
                if it.cur:
                    attend(it, 1)
                    scores(it, 3)
                    turn_rows(it, 2)
                if it.nxt:
                    pe.wait_ge(cT_done, it.b + 2)
                    project_T(it, "k", 0)
                    project_T(it, "k", 1)
                if it.cur:
                    attend(it, 2)
                if it.nxt:
                    project_v(it, 0, 0)
                    project_v(it, 1, 0)

        @block.scalar
        def _(act):
            def expo(it, t):
                for half in range(2):
                    p = p_sb[2 * (t % 2) + half]
                    act.wait_ge(sub_done, 8 * it.b + (2 * t + half + 1))
                    nc.scalar.activation(p[:], p[:], ACT.Exp, scale=HD ** -0.5).then_inc(exp_done, 1)

            def take_turn(it, t):
                for half in range(2):
                    bank = filled(act, it, f"tr{'AB'[half]}{t}")
                    if t == 0 and it.kind != "first":
                        jobs.wait_filled(act, it, "AV3")
                    if t in (1, 2):
                        jobs.wait_filled(act, it, f"AV{t - 1}")
                    nc.scalar.copy(pT[half][:].rearrange("p a b -> p (a b)"), bank[:, :]).then_inc(pT_done, 1)

            def take_q(it, j):
                bank = filled(act, it, f"q{j}")
                nc.scalar.copy(qT[:, 2 * j:2 * j + 2, :].rearrange("p a b -> p (a b)"), bank[:, :]).then_inc(q_done, 1)

            def take_out(it, t):
                u, o = t % 2, t // 2
                bank = filled(act, it, f"AV{t}")
                if it.kind != "first" and t < 2:
                    jobs.wait_filled(act, it, f"wo{t}")
                nc.scalar.copy(oT_hi[u][:, 4 * o:4 * o + 4, :].rearrange("p a b -> p (a b)"), bank[:, :]).then_inc(oT_hi_done, 1)

            def take_v(it, u, o):
                bank = filled(act, it, f"v{u}{o}")
                nc.scalar.copy(v_sb[u][:, 512 * o:512 * o + 512], bank[:, :]).then_inc(v_done, 1)

            act.wait_ge(raw_in, 64)
            for n in range(4):
                nc.scalar.copy(w_hi[n][:], w_raw[n]).then_inc(w_hi_done, 1)
            for it in turns(act, PAIRS, 1):
                if it.cur:
                    expo(it, 0)
                if it.prev:
                    take_turn(it, 3)
                if it.cur:
                    take_q(it, 2)
                    take_q(it, 3)
                if it.prev:
                    take_out(it, 3)
                if it.cur:
                    expo(it, 1)
                    take_turn(it, 0)
                    take_out(it, 0)
                    take_v(it, 0, 1)
                    take_v(it, 1, 1)
                    expo(it, 2)
                if it.nxt:
                    for n, done in (("x", xT_hi_done), ("c", cT_hi_done)):
                        bank = filled(act, it, f"{n}T")
                        nc.scalar.copy(inT_hi[n][:].rearrange("p k u t -> p (k u t)"), bank[:, :]).then_inc(done, 1)
                if it.cur:
                    take_turn(it, 1)
                if it.nxt:
                    take_q(it, 0)
                    take_q(it, 1)
                if it.cur:
                    take_out(it, 1)
                    expo(it, 3)
                    take_turn(it, 2)
                    take_out(it, 2)
                if it.nxt:
                    take_v(it, 0, 0)
                    take_v(it, 1, 0)

        @block.vector
        def _(dve):
            def softmax_in(it, t):
                for half in range(2):
                    i = 2 * (t % 2) + half
                    n = 8 * it.b + (2 * t + half + 1)
                    if half == 0:
                        dve.wait_ge(scores_done, 4 * it.b + (t + 1))
                    nc.vector.tensor_reduce(smax[:, i, :], score_bank[i][:], AX.X, ALU.max).then_inc(smax_done, 1)
                    if t >= 2 or it.kind != "first":
                        dve.wait_ge(pT_done, 8 * it.b + (2 * t + half - 3))
                    dve.wait_ge(smax_done, n)
                    nc.vector.tensor_tensor(p_sb[i][:], score_bank[i][:],
                                            smax[:, i, :].rearrange("p (h o) -> p h o", o=1).to_broadcast([P, 4, P]),
                                            ALU.subtract).then_inc(sub_done, 1)

            def sums(it, t):
                for half in range(2):
                    i = 2 * (t % 2) + half
                    n = 8 * it.b + (2 * t + half + 1)
                    dve.wait_ge(exp_done, n)
                    nc.vector.tensor_reduce(den[:, i, :], p_sb[i][:], AX.X, ALU.add).then_inc(den_done, 1)
                    dve.wait_ge(den_done, n)
                    nc.vector.reciprocal(rden[:, i, :], den[:, i, :]).then_inc(rden_done, 1)

            def take_low(it, name, hi, lo, hi_done, n, done):
                bank = filled(dve, it, name)
                dve.wait_ge(hi_done, n)
                nc.vector.tensor_tensor(lo, bank[:, :], hi.bitcast(F32), ALU.subtract).then_inc(done, 1)

            def take_out(it, t):
                u, o = t % 2, t // 2
                hi, lo = (x[u][:, 4 * o:4 * o + 4, :].rearrange("p a b -> p (a b)") for x in (oT_hi, oT_lo))
                take_low(it, f"AV{t}", hi, lo, oT_hi_done, 4 * it.b + (0 if t == 3 else t + 1), oT_done)

            def take_k(it, j):
                bank = filled(dve, it, f"k{j}")
                nc.vector.tensor_copy(kT[:, 2 * j:2 * j + 2, :].rearrange("p a b -> p (a b)"), bank[:, :]).then_inc(k_done, 1)

            def add_out(it, u):
                bank = filled(dve, it, f"wo{u}")
                xp = x_sb[:, 2 * it.b - 2 + u, :]
                nc.vector.tensor_tensor(xp, xp, bank[:, 0:D], ALU.add).then_inc(x_added, 1)

            for n in range(4):
                dve.wait_ge(w_hi_done, n + 1)
                nc.vector.tensor_tensor(w_lo[n][:], w_raw[n], w_hi[n][:].bitcast(F32), ALU.subtract).then_inc(w_done, 1)
            for it in turns(dve, PAIRS, 1):
                if it.nxt:
                    xb = [x_sb[:, 2 * it.b + 2 + u, :] for u in range(2)]
                    for u in range(2):
                        last = nc.vector.bn_stats(bn6[:, u, :], xb[u])
                    last.then_inc(bn6_done, 1)
                    dve.wait_ge(bn6_done, it.b + 2)
                    dve.sem_inc(bn6_seen, 1)
                    for u in range(2):
                        last = nc.vector.bn_aggr(bn2[:, u, :], bn6[:, u, :])
                    last.then_inc(bn2_done, 1)
                    dve.wait_ge(bn2_done, it.b + 2)
                    nc.vector.tensor_scalar(vpe[:].rearrange("p (u o) -> p u o", o=1), bn2[:, :, 1:2], 1e-5, None,
                                            ALU.add).then_inc(vpe_done, 1)
                if it.cur:
                    softmax_in(it, 0)
                if it.prev:
                    take_out(it, 3)
                if it.cur:
                    sums(it, 0)
                if it.prev:
                    add_out(it, 0)
                if it.cur:
                    softmax_in(it, 1)
                    take_k(it, 2)
                    take_k(it, 3)
                    sums(it, 1)
                    take_out(it, 0)
                if it.prev:
                    add_out(it, 1)
                if it.nxt:
                    dve.wait_ge(rstd_done, it.b + 2)
                    if it.kind != "pro":
                        dve.wait_ge(xT_hi_done, it.b + 1)
                    for u in range(2):
                        last = nc.vector.tensor_scalar(xn[:, u, :], xb[u], bn2[:, u, 0:1], rstd[:, u:u + 1], ALU.subtract, ALU.mult)
                    last.then_inc(xn_done, 1)
                if it.cur:
                    softmax_in(it, 2)
                if it.nxt:
                    for n, a, b_ in (("x", xT_hi_done, xT_done), ("c", cT_hi_done, cT_done)):
                        hi, lo = (t[n][:].rearrange("p k u t -> p (k u t)") for t in (inT_hi, inT_lo))
                        take_low(it, f"{n}T", hi, lo, a, it.b + 2, b_)
                if it.cur:
                    sums(it, 2)
                    take_out(it, 1)
                    softmax_in(it, 3)
                if it.nxt:
                    take_k(it, 0)
                    take_k(it, 1)
                if it.cur:
                    sums(it, 3)
                    take_out(it, 2)

        @block.gpsimd
        def _(pool):
            def normalise(it, t):
                for half in range(2):
                    i = 2 * (t % 2) + half
                    pool.wait_ge(rden_done, 8 * it.b + (2 * t + half + 1))
                    nc.gpsimd.tensor_tensor(p_sb[i][:], p_sb[i][:],
                                            rden[:, i, :].rearrange("p (h o) -> p h o", o=1).to_broadcast([P, 4, P]),
                                            ALU.mult).then_inc(norm_done, 1)

            for it in turns(pool, PAIRS, 1):
                if it.nxt:
                    pool.wait_ge(vpe_done, it.b + 2)
                    nc.gpsimd.tensor_tensor(rstd[:], vpe[:], pow_half[:, 0:2], ALU.pow).then_inc(rstd_done, 1)
                if it.cur:
                    for t in range(4):
                        normalise(it, t)
    return jobs.end


class Plan:

    def __init__(self, banks, filled_sem, before, lo, hi, order, read_by):
        self.banks, self.filled_sem, self.lo, self.hi, self.order, self.read_by = banks, filled_sem, lo, hi, order, read_by
        self.number, self.last = {}, {}
        jobs = []
        for b in range(lo, hi + 1):
            for name in order(b):
                self.number[b, name] = before + len(jobs)
                self.last[b, name] = jobs[-RING] if len(jobs) >= RING else None
                jobs.append((b, name))
        self.end = before + len(jobs)

    def turns(self, eng, *loops):
        b = self.lo
        for first, last, unroll in [*loops, (self.hi + 1, self.hi, 1)]:
            for b in range(b, first):
                yield PlanTurn(self, b)
            b = max(b, first)
            if last >= first:
                assert (last - first + 1) % unroll == 0
                for c in range(first, last + 1):
                    rep = first + (c - first) % unroll
                    for name in self.order(rep):
                        p, q = self.last[rep, name], self.last[c, name]
                        assert p and q and p[1] == q[1] and rep - p[0] == c - q[0]
                        assert (self.number[c, name] - self.number[rep, name]) % RING == 0
                with eng.Fori(0, (last - first + 1) // unroll) as m:
                    for u in range(unroll):
                        yield PlanTurn(self, first + u, m, unroll)
                b = last + 1


class PlanTurn:

    def __init__(self, plan, rep, m=None, unroll=1):
        self.plan, self.rep, self.m, self.unroll = plan, rep, m, unroll

    def at(self, a, c):
        return self.rep * a + c if self.m is None else self.m * (a * self.unroll) + (self.rep * a + c)

    def has(self, name):
        return (self.rep, name) in self.plan.number

    def wait_filled(self, eng, name):
        n = self.plan.number[self.rep, name] + 1
        if self.m is not None:
            n = self.m * (self.unroll * len(self.plan.order(self.rep))) + n
        eng.wait_ge(self.plan.filled_sem, n)

    def filled(self, eng, name):
        self.wait_filled(eng, name)
        return self.plan.banks[self.plan.number[self.rep, name] % RING]

    def start(self, pe, name):
        last = self.plan.last[self.rep, name]
        if last:
            read, a, c = self.plan.read_by[last[1]]
            pe.wait_ge(read, self.at(a, c + a * (last[0] - self.rep)))
        return self.plan.banks[self.plan.number[self.rep, name] % RING]


def experts(nc, sh, raw1, jobs_before, gate_w, w2, raw1_in, xs_dram, xs_cleared, out):
    B, x_sb, ident, pow_half, sem = sh.B, sh.x_sb, sh.ident, sh.pow_half, sh.sem
    ring, ring_filled = sh.ring, sh.ring_filled
    E, F = 8, 512
    KF = F // P
    SEG = 2
    SB = B // SEG
    ST = SB * 2 + E - 1
    NT = SEG * ST
    EW = KD * F
    assert EW == KF * D

    xn_dram = nc.dram_tensor("xn_dram", (B, P, D), F32).ap()
    ys_dram = [nc.dram_tensor(f"ys_dram{s}", (ST * P, D), F32).ap() for s in range(SEG)]

    with ExitStack() as ctx:
        def sb(name, shape, dt=F32):
            return ctx.enter_context(nc.sbuf_tensor(name, shape, dt))

        w1_lo = sb("w1_lo", [P, E * EW], F32R)
        with nc.sbuf_tensor("raw2", [P, E * EW], F32) as raw2:
            pass
        w2_lo = sb("w2_lo", [P, E * EW], F32R)
        w1_hi = sb("w1_hi", [P, E * EW], F32R)
        w2_hi = sb("w2_hi", [P, E * EW], F32R)
        gate_sb = sb("gate_sb", [P, KD, E])
        bn6 = sb("r_bn6", [P, B, 6])
        mean = sb("r_mean", [P, B])
        diff = sb("r_diff", [P, B])
        var = sb("r_var", [P, B])
        half_col = sb("half_col", [P, B])
        rstd = sb("r_rstd", [P, B])
        xn = sb("r_xn", [P, 2, D])
        xnT = sb("r_xnT", [P, 2, D])
        logits = sb("logits", [P, B, E])
        rank_e = sb("rank_e", [P, E])
        top = sb("top", [P, 2, B])
        tmp = sb("tmp", [P, B, E])
        first_of = sb("first_of", [P, B])
        hot = [sb(f"hot{k}", [P, B, E]) for k in range(2)]
        hot_b = sb("hot_b", [P, B * E], BF16)
        before_b = sb("before_b", [P, P], BF16)
        ones_b = sb("ones_b", [P, P], BF16)
        pre = [sb(f"pre{i}", [P, SEG, SB, E]) for i in range(2)]
        count = sb("count", [P, SEG, E])
        count_i = sb("count_i", [P, SEG, E], mybir.dt.int32)
        padded = sb("padded", [P, SEG, E])
        begin = sb("begin", [P, SEG, E])
        slot_f = sb("slot_f", [P, 2, B])
        slot = sb("slot", [P, 2, B], mybir.dt.int32)
        share = sb("share", [P, 2, B])
        exp_d = sb("exp_d", [P, B])
        tile_row = sb("tile_row", [1, ST])
        tile_cmp = sb("tile_cmp", [1, ST, E])
        tile_e = sb("tile_e", [1, NT])
        tile_w = sb("tile_w", [1, NT], mybir.dt.int32)
        iota_i = sb("iota_i", [P, ST], mybir.dt.int32)
        send = [sb(f"send{i}", [P, D]) for i in range(2)]
        send_at = [sb(f"send_at{i}", [P, 1], mybir.dt.int32) for i in range(4)]
        xg = [sb(f"xg{i}", [P, D]) for i in range(2)]
        gT_hi = [sb(f"gT_hi{i}", [P, KD, P], F32R) for i in range(2)]
        gT_lo = [sb(f"gT_lo{i}", [P, KD, P], F32R) for i in range(2)]
        h_sb = [sb(f"h{i}", [P, F]) for i in range(2)]
        hT_hi = [sb(f"hT_hi{i}", [P, KF, P], F32R) for i in range(2)]
        hT_lo = [sb(f"hT_lo{i}", [P, KF, P], F32R) for i in range(2)]
        y_sb = [sb(f"y_out{i}", [P, D]) for i in range(2)]
        take_at = [sb(f"take_at{i}", [P, 1], mybir.dt.int32) for i in range(4)]
        yg = [sb(f"yg{i}", [P, D]) for i in range(4)]
        o_sb = [sb(f"o{i}", [P, D]) for i in range(2)]

        raw2_in, gate_in = sem("raw2_in"), sem("gate_in")
        w_hi_done, w_done = sem("ew_hi_done"), sem("ew_done")
        const_step, const_done = sem("e_const_step"), sem("e_const_done")
        stats_done, stat_step, var_done, rstd_done = sem("r_stats_done"), sem("r_stat_step"), sem("r_var_done"), sem("r_rstd_done")
        xn_done, xnT_done, logits_done = sem("r_xn_done"), sem("r_xnT_done"), sem("logits_done")
        xn_sent = [sem(f"xn_sent{i}") for i in range(2)]
        route_step, exp_in, exp_done, hot_done, ranks_done, slots_done, tiles_done = (
            sem(n) for n in ("route_step", "exp_in", "exp_done", "hot_done", "ranks_done", "slots_done", "tiles_done"))
        send_in = [sem(f"send_in{i}") for i in range(2)]
        send_at_done, scatter_ready, gather_ready = sem("send_at_done"), sem("scatter_ready"), sem("gather_ready")
        sent = [sem(f"sent{i}") for i in range(4)]
        seg_sent = sem("seg_sent")
        xg_in = [sem(f"xg_in{i}") for i in range(2)]
        gT_hi_done, gT_done, silu_done, hT_hi_done, hT_done, y_done = (
            sem(n) for n in ("gT_hi_done", "gT_done", "silu_done", "hT_hi_done", "hT_done", "y_out_done"))
        y_stored = [sem(f"y_stored{i}") for i in range(2)]
        seg_stored = sem("seg_stored")
        take_at_done = sem("take_at_done")
        taken = [sem(f"taken{i}") for i in range(4)]
        comb_step, comb_done = sem("comb_step"), sem("comb_done")
        out_sent = [sem(f"out_sent{i}") for i in range(2)]

        router = Plan(ring, ring_filled, jobs_before, 0, B,
                      lambda b: ["T"] * (b < B) + ["L"] * (b > 0),
                      {"T": (xnT_done, 1, 1), "L": (logits_done, 1, 0)})
        router_loop = (4, B - 1, 2)

        def tile_jobs(j):
            return (["h"] * (0 <= j < NT) + ["y"] * (0 <= j - 2 < NT) + ["hT"] * (0 <= j - 1 < NT)
                    + ["xT"] * (0 <= j + 1 < NT))

        tiles = Plan(ring, ring_filled, router.end + 2, -1, NT + 1, tile_jobs,
                     {"h": (silu_done, 1, 1), "y": (y_done, 1, -1), "hT": (hT_done, 1, 0), "xT": (gT_done, 1, 2)})
        tile_loop = (4, NT - 3 - NT % 2, 2)
        comb_from = ST + 3
        assert comb_from % 2 == 0
        comb_to = comb_from + 2 * SB - 1
        assert comb_to <= tile_loop[1]

        block = ctx.enter_context(nc.Block())

        @block.sync
        def _(sync):
            for u in range(2):
                sync.sem_inc(out_sent[u], 16)
            sync.dma_start(gate_sb[:], gate_w.rearrange("(k p) n -> p k n", p=P)).then_inc(gate_in, 16)
            sync.dma_start(raw2[:, :].rearrange("p (e k n) -> p e k n", e=E, k=KF),
                           w2.rearrange("e (k p) n -> p e k n", p=P)).then_inc(raw2_in, 16)
            with sync.Fori(0, B // 2) as m:
                for u in range(2):
                    sync.wait_ge(xn_done, m * 2 + (u + 1))
                    sync.dma_start(xn_dram[m * 2 + u], xn[:, u, :]).then_inc(xn_sent[u], 16)

            def load_rows(m, u, waits):
                if waits:
                    sync.wait_ge(sent[2 * u], m * 16)
                    sync.wait_ge(sent[2 * u + 1], m * 16)
                sync.dma_start(send[u][:], xn_dram[m * 2 + u]).then_inc(send_in[u], 16)

            for u in range(2):
                sync.wait_ge(xn_sent[u], 16 * (B // 2))
            for u in range(2):
                load_rows(0, u, False)
            with sync.Fori(1, SB // 2) as m:
                for u in range(2):
                    load_rows(m, u, True)

            def rows(dram, it, by):
                s = (it.rep + by) // ST
                return dram[s][bass.ts(it.at(1, by - s * ST), P), :]

            def load_tile(j, u, waits, src):
                if waits:
                    sync.wait_ge(gT_hi_done, j - 1)
                sync.dma_start(xg[u][:], src).then_inc(xg_in[u], 16)

            def store_tile(j, u, dst):
                sync.wait_ge(y_done, j + 1)
                sync.dma_start(dst, y_sb[u][:]).then_inc(y_stored[u], 16)

            sync.wait_ge(seg_sent, 1)
            for j in range(2):
                load_tile(j, j, False, xs_dram[0][j * P:(j + 1) * P, :])

            def store_out(m, u):
                sync.wait_ge(comb_done, m * 2 + (u + 1))
                sync.dma_start(out[m * 2 + u], o_sb[u][:]).then_inc(out_sent[u], 16)

            def store_all(tiles_of_half):
                for u in range(2):
                    sync.wait_ge(y_stored[u], 16 * ((tiles_of_half + 1 - u) // 2))
                sync.sem_inc(seg_stored, 1)

            for it in tiles.turns(sync, (4, 3 + SB, 2), (4 + SB, ST - 4, 2), (comb_from, comb_to, 4)):
                j, u = it.rep, it.rep % 2
                if j + 3 == ST:
                    sync.wait_ge(seg_sent, 2)
                if j + 3 < NT:
                    load_tile(it.at(1, 3), 1 - u, True, rows(xs_dram, it, 3))
                if j >= 2:
                    store_tile(it.at(1, -2), u, rows(ys_dram, it, -2))
                if it.m is not None and j < 4 + SB:
                    load_rows(it.m + SB // 2, u, True)
                if j == ST + 2:
                    store_all(ST)
                if it.m is not None and j == comb_from + 3:
                    for v in range(2):
                        store_out(it.m, v)
            store_all(NT)
            with sync.Fori(SB // 2, B // 2) as m:
                for u in range(2):
                    store_out(m, u)
            for u in range(2):
                sync.wait_ge(out_sent[u], 16 * (B // 2) + 16)

        @block.tensor
        def _(pe):
            pe.wait_ge(gate_in, 16)
            for it in router.turns(pe, router_loop):
                if it.has("T"):
                    bank = it.start(pe, "T")
                    pe.wait_ge(xn_done, it.at(1, 1))
                    for k in range(KD):
                        last = nc.tensor.transpose(bank[:, k * P:(k + 1) * P], xn[:, it.rep % 2, k * P:(k + 1) * P], ident[:])
                    last.then_inc(ring_filled, 1)
                if it.has("L"):
                    bank = it.start(pe, "L")
                    pe.wait_ge(xnT_done, it.at(1, 0))
                    for k in range(KD):
                        last = nc.tensor.matmul(bank[:, 0:E], xnT[:, (it.rep - 1) % 2, k * P:(k + 1) * P], gate_sb[:, k, :],
                                                start=(k == 0), stop=(k == KD - 1))
                    last.then_inc(ring_filled, 1)
            pe.wait_ge(hot_done, 1)
            pe.wait_ge(const_done, 1)
            pe.wait_ge(logits_done, B)
            nc.tensor.matmul(ring[router.end % RING][:, 0:B * E], before_b[:], hot_b[:], start=True, stop=True).then_inc(ring_filled, 1)
            nc.tensor.matmul(ring[(router.end + 1) % RING][:, 0:B * E], ones_b[:], hot_b[:], start=True, stop=True).then_inc(ring_filled, 1)

            pe.wait_ge(tiles_done, 1)
            pe.wait_ge(slots_done, 1)
            pe.wait_ge(w_done, 4)

            def expert_of(j):
                return pe.value_load(tile_w[0:1, bass.ds(j, 1)], min_val=0, max_val=(E - 1) * EW)

            for it in tiles.turns(pe, tile_loop):
                j, u = it.rep, it.rep % 2
                if it.has("h"):
                    bank = it.start(pe, "h")
                    pe.wait_ge(gT_done, it.at(1, 1))
                    at = expert_of(it.at(1, 0))
                    for k in range(KD):
                        hi, lo = (w[:, bass.ds(at + k * F, F)] for w in (w1_hi, w1_lo))
                        nc.tensor.matmul(bank[:, :], gT_hi[u][:, k, :], lo, start=(k == 0), stop=False)
                        nc.tensor.matmul(bank[:, :], gT_lo[u][:, k, :], hi, start=False, stop=False)
                        last = nc.tensor.matmul(bank[:, :], gT_hi[u][:, k, :], hi, start=False, stop=(k == KD - 1))
                    last.then_inc(ring_filled, 1)
                if it.has("y"):
                    bank = it.start(pe, "y")
                    pe.wait_ge(hT_done, it.at(1, -1))
                    at = expert_of(it.at(1, -2))
                    for k in range(KF):
                        hi, lo = (w[:, bass.ds(at + k * D, D)] for w in (w2_hi, w2_lo))
                        nc.tensor.matmul(bank[:, 0:D], hT_hi[u][:, k, :], lo, start=(k == 0), stop=False)
                        nc.tensor.matmul(bank[:, 0:D], hT_lo[u][:, k, :], hi, start=False, stop=False)
                        last = nc.tensor.matmul(bank[:, 0:D], hT_hi[u][:, k, :], hi, start=False, stop=(k == KF - 1))
                    last.then_inc(ring_filled, 1)
                if it.has("hT"):
                    bank = it.start(pe, "hT")
                    pe.wait_ge(silu_done, it.at(1, 0))
                    for k in range(KF):
                        last = nc.tensor.transpose(bank[:, k * P:(k + 1) * P], h_sb[1 - u][:, k * P:(k + 1) * P], ident[:])
                    last.then_inc(ring_filled, 1)
                if it.has("xT"):
                    bank = it.start(pe, "xT")
                    n = it.unroll * 8
                    v = 16 * ((j + 1) // 2 + 1)
                    pe.wait_ge(xg_in[1 - u], v if it.m is None else it.m * n + v)
                    for k in range(KD):
                        last = nc.tensor.transpose(bank[:, k * P:(k + 1) * P], xg[1 - u][:, k * P:(k + 1) * P], ident[:])
                    last.then_inc(ring_filled, 1)

        @block.scalar
        def _(act):
            for it in router.turns(act, router_loop):
                if it.has("T"):
                    bank = it.filled(act, "T")
                    if it.rep >= 2:
                        it2 = PlanTurn(router, it.rep - 1, it.m, it.unroll)
                        it2.wait_filled(act, "L")
                    nc.scalar.copy(xnT[:, it.rep % 2, :], bank[:, 0:D]).then_inc(xnT_done, 1)
            act.wait_ge(raw1_in, 16)
            act.wait_ge(raw2_in, 16)
            for raw, hi in ((raw1, w1_hi), (raw2, w2_hi)):
                for c in range(2):
                    cols = slice(c * 4 * EW, (c + 1) * 4 * EW)
                    nc.scalar.copy(hi[:, cols], raw[:, cols]).then_inc(w_hi_done, 1)
            act.wait_ge(exp_in, 1)
            nc.scalar.activation(exp_d[:], exp_d[:], ACT.Exp).then_inc(exp_done, 1)

            for it in tiles.turns(act, tile_loop):
                u = it.rep % 2
                if it.has("h"):
                    bank = it.filled(act, "h")
                    if it.rep >= 2:
                        PlanTurn(tiles, it.rep - 1, it.m, it.unroll).wait_filled(act, "hT")
                    nc.scalar.activation(h_sb[u][:], bank[:, :], ACT.Silu).then_inc(silu_done, 1)
                if it.has("y"):
                    bank = it.filled(act, "y")
                    if it.rep >= 4:
                        v = 16 * (it.rep // 2 - 1)
                        act.wait_ge(y_stored[u], v if it.m is None else it.m * (it.unroll * 8) + v)
                    nc.scalar.copy(y_sb[u][:], bank[:, 0:D]).then_inc(y_done, 1)
                if it.has("hT"):
                    bank = it.filled(act, "hT")
                    if it.rep >= 3:
                        PlanTurn(tiles, it.rep - 1, it.m, it.unroll).wait_filled(act, "y")
                    nc.scalar.copy(hT_hi[1 - u][:].rearrange("p k t -> p (k t)"), bank[:, :]).then_inc(hT_hi_done, 1)
                if it.has("xT"):
                    bank = it.filled(act, "xT")
                    if it.rep >= 1:
                        PlanTurn(tiles, it.rep - 1, it.m, it.unroll).wait_filled(act, "h")
                    nc.scalar.copy(gT_hi[1 - u][:].rearrange("p k t -> p (k t)"), bank[:, 0:D]).then_inc(gT_hi_done, 1)

        @block.vector
        def _(dve):
            step = [0]

            def link(ins):
                step[0] += 1
                ins.then_inc(route_step, 1)
                dve.wait_ge(route_step, step[0])

            def spread(ap, n):
                return ap.rearrange("p (m o) -> p m o", o=1).to_broadcast([ap.shape[0], ap.shape[1], n])

            with dve.Fori(0, B // 4) as m:
                for u in range(4):
                    last = nc.vector.bn_stats(bn6[:, m * 4 + u, :], x_sb[:, m * 4 + u, :])
                last.then_inc(stats_done, 1)
            dve.wait_ge(stats_done, B // 4)
            col = lambda c: bn6[:, :, c:c + 1].rearrange("p b o -> p (b o)")
            nc.vector.tensor_tensor(diff[:], col(1), col(4), ALU.subtract).then_inc(stat_step, 1)
            nc.vector.tensor_tensor(mean[:], col(1), col(4), ALU.add).then_inc(stat_step, 1)
            nc.vector.tensor_tensor(var[:], col(2), col(5), ALU.add).then_inc(stat_step, 1)
            dve.wait_ge(stat_step, 3)
            nc.vector.tensor_tensor(diff[:], diff[:], diff[:], ALU.mult).then_inc(stat_step, 1)
            nc.vector.tensor_scalar(mean[:], mean[:], 0.5, None, ALU.mult).then_inc(stat_step, 1)
            nc.vector.tensor_scalar(var[:], var[:], 1.0 / D, 1e-5, ALU.mult, ALU.add).then_inc(stat_step, 1)
            dve.wait_ge(stat_step, 6)
            nc.vector.scalar_tensor_tensor(out=var[:], in0=diff[:], scalar=0.25, in1=var[:], op0=ALU.mult,
                                           op1=ALU.add).then_inc(var_done, 1)
            dve.wait_ge(rstd_done, 1)

            for it in router.turns(dve, router_loop):
                u = it.rep % 2
                if it.has("T"):
                    if it.rep >= 2:
                        dve.wait_ge(xnT_done, it.at(1, -1))
                        v = 16 * (it.rep // 2)
                        dve.wait_ge(xn_sent[u], v if it.m is None else it.m * (it.unroll * 8) + v)
                    b = it.at(1, 0)
                    nc.vector.tensor_scalar(xn[:, u, :], x_sb[:, b, :], mean[:, bass.ds(b, 1)], rstd[:, bass.ds(b, 1)],
                                            ALU.subtract, ALU.mult).then_inc(xn_done, 1)
                if it.has("L"):
                    bank = it.filled(dve, "L")
                    nc.vector.tensor_copy(logits[:, it.at(1, -1), :], bank[:, 0:E]).then_inc(logits_done, 1)

            dve.wait_ge(logits_done, B)
            dve.wait_ge(const_done, 1)
            flat = lambda t: t[:].rearrange("p b e -> p (b e)")
            left = logits
            for k in range(2):
                link(nc.vector.tensor_reduce(top[:, k, :], left[:], AX.X, ALU.max))
                link(nc.vector.tensor_tensor(tmp[:], left[:], spread(top[:, k, :], E), ALU.is_equal))
                link(nc.vector.tensor_tensor(tmp[:], tmp[:], rank_e[:].rearrange("p (o e) -> p o e", o=1).to_broadcast([P, B, E]),
                                             ALU.mult))
                link(nc.vector.tensor_reduce(first_of[:], tmp[:], AX.X, ALU.max))
                link(nc.vector.tensor_tensor(hot[k][:], tmp[:], spread(first_of[:], E), ALU.is_equal))
                if k == 0:
                    link(nc.vector.scalar_tensor_tensor(out=flat(logits), in0=flat(hot[0]), scalar=-3e38, in1=flat(logits),
                                                        op0=ALU.mult, op1=ALU.add))
            nc.vector.tensor_tensor(hot_b[:], flat(hot[0]), flat(hot[1]), ALU.add).then_inc(hot_done, 1)
            nc.vector.tensor_tensor(exp_d[:], top[:, 1, :], top[:, 0, :], ALU.subtract).then_inc(exp_in, 1)

            n = router.end
            rank, total = (ring[(n + i) % RING][:, 0:B * E].rearrange("p (s b e) -> p s b e", s=SEG, e=E) for i in range(2))
            dve.wait_ge(ring_filled, n + 2)
            nc.vector.memset(pre[0][:, :, 0:1, :], 0.0)
            for s in range(SEG):
                last = nc.vector.tensor_copy(pre[0][:, s, 1:SB, :], total[:, s, 0:SB - 1, :])
            link(last)
            src, dst, by = pre[0], pre[1], 1
            while by < SB:
                for s in range(SEG):
                    nc.vector.tensor_copy(dst[:, s, 0:by, :], src[:, s, 0:by, :])
                    last = nc.vector.tensor_tensor(dst[:, s, by:SB, :], src[:, s, by:SB, :], src[:, s, 0:SB - by, :], ALU.add)
                link(last)
                src, dst, by = dst, src, 2 * by
            link(nc.vector.tensor_tensor(count[:], src[:, :, SB - 1, :], total[:, :, SB - 1, :], ALU.add))
            link(nc.vector.tensor_scalar(count_i[:], count[:], float(P - 1), None, ALU.add))
            link(nc.vector.tensor_scalar(count_i[:], count_i[:], 7, 7, ALU.logical_shift_right, ALU.logical_shift_left))
            link(nc.vector.tensor_copy(padded[:], count_i[:]))
            for s in range(SEG):
                last = nc.vector.memset(begin[:, s, 0:1], 0.0)
            link(last)
            for e in range(1, E):
                link(nc.vector.tensor_tensor(begin[:, :, e:e + 1], begin[:, :, e - 1:e], padded[:, :, e - 1:e], ALU.add))
            link(nc.vector.tensor_tensor(dst[:], rank, src[:], ALU.add))
            for s in range(SEG):
                last = nc.vector.tensor_tensor(dst[:, s, :, :], dst[:, s, :, :],
                                               begin[:, s, :].rearrange("p (o e) -> p o e", o=1).to_broadcast([P, SB, E]), ALU.add)
            link(last)
            at_slot = dst[:].rearrange("p s b e -> p (s b) e")
            for k in range(2):
                link(nc.vector.tensor_tensor(tmp[:], hot[k][:], at_slot, ALU.mult))
                link(nc.vector.tensor_reduce(slot_f[:, k, :], tmp[:], AX.X, ALU.add))
            nc.vector.tensor_copy(slot[:], slot_f[:]).then_inc(slots_done, 1)
            for s in range(SEG):
                link(nc.vector.tensor_tensor(tile_cmp[:], begin[0:1, s, :].rearrange("p (o e) -> p o e", o=1).to_broadcast([1, ST, E]),
                                             spread(tile_row[:], E), ALU.is_le))
                link(nc.vector.tensor_reduce(tile_e[:, s * ST:(s + 1) * ST], tile_cmp[:], AX.X, ALU.add))
            nc.vector.tensor_scalar(tile_w[:], tile_e[:], float(EW), float(-EW), ALU.mult, ALU.add).then_inc(tiles_done, 1)
            dve.wait_ge(exp_done, 1)
            link(nc.vector.tensor_scalar(first_of[:], exp_d[:], 1.0, None, ALU.add))
            link(nc.vector.reciprocal(share[:, 0, :], first_of[:]))
            link(nc.vector.tensor_tensor(share[:, 1, :], exp_d[:], share[:, 0, :], ALU.mult))
            for i, (raw, hi, lo) in enumerate(((raw1, w1_hi, w1_lo), (raw2, w2_hi, w2_lo))):
                for c in range(2):
                    cols = slice(c * 4 * EW, (c + 1) * 4 * EW)
                    dve.wait_ge(w_hi_done, 2 * i + c + 1)
                    nc.vector.tensor_tensor(lo[:, cols], raw[:, cols], hi[:, cols].bitcast(F32), ALU.subtract).then_inc(w_done, 1)

            def combine(m, u):
                b = m * 2 + u
                for k in range(2):
                    dve.wait_ge(taken[2 * u + k], m * 16 + 16)
                dve.wait_ge(out_sent[u], m * 16 + 16)
                col = lambda k: share[:, k, bass.ds(b, 1)]
                nc.vector.scalar_tensor_tensor(out=o_sb[u][:], in0=yg[2 * u][:], scalar=col(0), in1=x_sb[:, b, :], op0=ALU.mult,
                                               op1=ALU.add).then_inc(comb_step, 1)
                dve.wait_ge(comb_step, b + 1)
                nc.vector.scalar_tensor_tensor(out=o_sb[u][:], in0=yg[2 * u + 1][:], scalar=col(1), in1=o_sb[u][:],
                                               op0=ALU.mult, op1=ALU.add).then_inc(comb_done, 1)

            def low_halves(it):
                u = it.rep % 2
                if it.has("hT"):
                    bank = it.filled(dve, "hT")
                    dve.wait_ge(hT_hi_done, it.at(1, 0))
                    nc.vector.tensor_tensor(hT_lo[1 - u][:].rearrange("p k t -> p (k t)"), bank[:, :],
                                            hT_hi[1 - u][:].bitcast(F32).rearrange("p k t -> p (k t)"), ALU.subtract).then_inc(hT_done, 1)
                if it.has("xT"):
                    bank = it.filled(dve, "xT")
                    dve.wait_ge(gT_hi_done, it.at(1, 2))
                    nc.vector.tensor_tensor(gT_lo[1 - u][:].rearrange("p k t -> p (k t)"), bank[:, 0:D],
                                            gT_hi[1 - u][:].bitcast(F32).rearrange("p k t -> p (k t)"), ALU.subtract).then_inc(gT_done, 1)

            for it in tiles.turns(dve, (tile_loop[0], comb_from - 1, 2), (comb_from, comb_to, 4)):
                low_halves(it)
                if it.unroll == 4 and it.rep % 2 == 1:
                    combine(it.m, (it.rep - comb_from) // 2)
            with dve.Fori(SB // 2, B // 2) as m:
                for u in range(2):
                    combine(m, u)

        @block.gpsimd
        def _(pool):
            nc.gpsimd.memset(half_col[:], -0.5).then_inc(const_step, 1)
            nc.gpsimd.memset(ones_b[:], 1.0).then_inc(const_step, 1)
            nc.gpsimd.memset(before_b[:], 1.0).then_inc(const_step, 1)
            nc.gpsimd.iota(iota_i[:], [[P, ST]], base=0, channel_multiplier=0).then_inc(const_step, 1)
            pool.wait_ge(const_step, 4)
            nc.gpsimd.affine_select(out=before_b[:], in_=before_b[:], compare_op=ALU.is_ge, fill=0.0, base=-1,
                                    pattern=[[1, P]], channel_multiplier=-1).then_inc(const_step, 1)
            nc.gpsimd.tensor_copy(tile_row[:], iota_i[0:1, :]).then_inc(const_step, 1)
            pool.wait_ge(const_step, 6)
            nc.gpsimd.iota(iota_i[:, 0:E], [[-1, E]], base=E, channel_multiplier=0).then_inc(const_step, 1)
            pool.wait_ge(const_step, 7)
            nc.gpsimd.tensor_copy(rank_e[:], iota_i[:, 0:E]).then_inc(const_step, 1)
            pool.wait_ge(var_done, 1)
            nc.gpsimd.tensor_tensor(rstd[:], var[:], half_col[:], ALU.pow).then_inc(rstd_done, 1)
            pool.wait_ge(const_step, 8)
            pool.sem_inc(const_done, 1)

            def scatter(m, waits, dst):
                for u in range(2):
                    for k in range(2):
                        i = 2 * u + k
                        if waits:
                            pool.wait_ge(sent[i], m * 16)
                        nc.gpsimd.tensor_copy(send_at[i][:], slot[:, k, bass.ds(m * 2 + u, 1)]).then_inc(send_at_done, 1)
                for u in range(2):
                    pool.wait_ge(send_at_done, m * 4 + 4)
                    pool.wait_ge(send_in[u], m * 16 + 16)
                    pool.sem_inc(scatter_ready, 1)
                    for k in range(2):
                        i = 2 * u + k
                        pool.indirect_dma_start(out=dst, out_offset=bass.IndirectOffsetOnAxis(ap=send_at[i][:, 0:1], axis=0),
                                                in_=send[u][:], in_offset=None).then_inc(sent[i], 16)

            pool.wait_ge(slots_done, 1)
            pool.wait_ge(xs_cleared, 32)
            scatter(0, False, xs_dram[0])
            with pool.Fori(1, SB // 2) as m:
                scatter(m, True, xs_dram[0])
            for i in range(4):
                pool.wait_ge(sent[i], 16 * (SB // 2))
            pool.sem_inc(seg_sent, 1)
            with pool.Fori(SB // 2, B // 2) as m:
                scatter(m, True, xs_dram[1])
            for i in range(4):
                pool.wait_ge(sent[i], 16 * (B // 2))
            pool.sem_inc(seg_sent, 1)

            def gather(m, waits, src):
                for u in range(2):
                    if waits:
                        pool.wait_ge(comb_done, m * 2 + (u - 1))
                    for k in range(2):
                        i = 2 * u + k
                        nc.gpsimd.tensor_copy(take_at[i][:], slot[:, k, bass.ds(m * 2 + u, 1)]).then_inc(take_at_done, 1)
                for u in range(2):
                    pool.wait_ge(take_at_done, m * 4 + 4)
                    pool.sem_inc(gather_ready, 1)
                    for k in range(2):
                        i = 2 * u + k
                        pool.indirect_dma_start(out=yg[i][:], out_offset=None, in_=src,
                                                in_offset=bass.IndirectOffsetOnAxis(ap=take_at[i][:, 0:1], axis=0)).then_inc(taken[i], 16)

            pool.wait_ge(seg_stored, 1)
            gather(0, False, ys_dram[0])
            with pool.Fori(1, SB // 2) as m:
                gather(m, True, ys_dram[0])
            pool.wait_ge(seg_stored, 2)
            with pool.Fori(SB // 2, B // 2) as m:
                gather(m, True, ys_dram[1])


def bass_decoder_layer(nc, x, ctx_x, w_attn, w_proj, ln_w2, rope_cos, rope_sin, w_q, w_k, w_v, w_o, gate_w, w1, w2, out):
    B = x.shape[0]
    with ExitStack() as ctx:
        sh = Shared(nc, ctx, B)
        cross_raw_in, w1_in, xs_cleared = (sh.sem(n) for n in ("cross_raw_in", "w1_in", "xs_cleared"))
        xs_dram = [nc.dram_tensor(f"xs_dram{s}", ((B + 7) * P, D), F32).ap() for s in range(2)]
        with nc.sbuf_tensor("raw", [P, 8192], F32) as sh.raw:
            done = self_attention(nc, sh, x, w_attn, w_proj, ln_w2, rope_cos, rope_sin, (w_q, w_k, w_v, w_o), cross_raw_in,
                                  xs_dram, xs_cleared)
            done = cross_attention(nc, sh, done, ctx_x, cross_raw_in, w1, w1_in)
        experts(nc, sh, sh.raw, done, gate_w, w2, w1_in, xs_dram, xs_cleared, out)


def kernel(**inputs):
    import numpy as _np
    import concourse.bacc as _bacc
    from concourse import mybir as _mybir
    from concourse.bass_utils import run_bass_kernel_spmd as _run

    half_dims = _np.concatenate([_np.arange(0, HD, 2), _np.arange(1, HD, 2)])
    q_heads = [h + half for o in range(2) for k in range(4) for h in (2 * k + o,) for half in (0, 8)]
    k_heads = [k + half for k in range(4) for half in (0, 4)]
    cols = [h * HD + half_dims for h in q_heads] + [NQ * HD + h * HD + half_dims for h in k_heads]
    cols += [_np.arange((NQ + NKV) * HD, (NQ + 2 * NKV) * HD + 8)]
    cols = _np.concatenate(cols)
    slots = [8 * half + 2 * k + o for o in range(2) for half in range(2) for k in range(4)]
    rows = _np.concatenate([h * HD + _np.arange(HD) for h in slots])
    T = 128
    div = 2.0 * _np.pi / float(T) ** (_np.arange(0, HD, 2, dtype=_np.float32) / HD)
    ang = _np.arange(T, dtype=_np.float32)[:, None] * div.astype(_np.float32)[None, :]
    cos = _np.cos(ang.astype(_np.float64)).astype(_np.float32)
    sin = _np.sin(ang.astype(_np.float64)).astype(_np.float32)
    arrays = {
        "x": _np.ascontiguousarray(inputs["x"]),
        "ctx": _np.ascontiguousarray(inputs["ctx_1024"]),
        "w_attn": _np.ascontiguousarray(_np.asarray(inputs["L0_attn_w_attn"])[:, cols]),
        "w_proj": _np.ascontiguousarray(_np.asarray(inputs["L0_attn_w_proj"])[rows]),
        "ln_w2": _np.ascontiguousarray(_np.tile(_np.asarray(inputs["L0_attn_ln_w"]), 2).reshape(P, 1)),
        "rope_cos": _np.concatenate([cos, cos], axis=1),
        "rope_sin": _np.concatenate([-sin, sin], axis=1),
        **{n: _np.ascontiguousarray(inputs[f"L0_xattn_{n}"]) for n in ("w_q", "w_k", "w_v", "w_o")},
        **{n: _np.ascontiguousarray(inputs[f"L0_ffn_{n}"]) for n in ("gate_w", "w1", "w2")},
    }
    nc = _bacc.Bacc("TRN2", target_bir_lowering=False, num_devices=1)
    args = [nc.dram_tensor(f"in_{n}", a.shape, _mybir.dt.from_np(a.dtype), kind="ExternalInput").ap() for n, a in arrays.items()]
    out = nc.dram_tensor("out_0", (32, 128, 256), F32, kind="ExternalOutput").ap()
    bass_decoder_layer(nc, *args, out)
    r = _run(nc, [{f"in_{n}": a for n, a in arrays.items()}], core_ids=[0])
    return r.results[0]["out_0"]
```

```python
from contextlib import ExitStack

import concourse.bass as bass
import numpy as np
from concourse import mybir

ALU = mybir.AluOpType
ACT = mybir.ActivationFunctionType
AX = mybir.AxisListType
F32 = mybir.dt.float32
F32R = mybir.dt.float32r
BF16 = mybir.dt.bfloat16

P = 128
D = 256
KD = D // P
HD = 64
NQ, NKV = 16, 8
RING = 4


class Ring:

    def __init__(self, banks, filled_sem, orders, read_by, before, mids, unroll):
        self.banks, self.filled_sem, self.orders, self.read_by = banks, filled_sem, orders, read_by
        self.base, self.step = {}, unroll * len(orders["mid"])
        assert self.step % RING == 0 and orders["first"][-RING:] == orders["mid"][-RING:]
        n = before
        for kind, count in (("pro", 1), ("first", 1), ("mid", mids), ("last", 1), ("tail", 1)):
            self.base[kind] = n
            n += len(orders[kind]) * count
        self.end = n

    def number(self, it, name):
        return self.base[it.kind] + self.orders[it.kind].index(name) + it.u * len(self.orders[it.kind])

    def start(self, pe, it, name):
        kind, b, at = it.kind, it.b, self.orders[it.kind].index(name) - RING
        while at < 0 and kind != "pro":
            kind, b = {"first": "pro", "mid": "mid", "last": "mid", "tail": "last"}[kind], b - 1
            at += len(self.orders[kind])
        if at >= 0:
            read, a, c = self.read_by[self.orders[kind][at]]
            pe.wait_ge(read, b * a + c)
        return self.banks[self.number(it, name) % RING]

    def wait_filled(self, eng, it, name):
        n = self.number(it, name) + 1
        eng.wait_ge(self.filled_sem, n if it.kind != "mid" else it.m * self.step + n)

    def filled(self, eng, it, name):
        self.wait_filled(eng, it, name)
        return self.banks[self.number(it, name) % RING]


class Turn:

    def __init__(self, kind, b, u=0, m=None, unroll=1):
        self.kind, self.b, self.u, self.m = kind, b, u, m
        self.par = b % 2 if m is None else (1 + u) % 2
        self.cur = kind in ("first", "mid", "last")
        self.nxt = kind in ("pro", "first", "mid")
        self.prev = kind in ("mid", "last", "tail")


def turns(eng, n, unroll):
    yield Turn("pro", -1)
    yield Turn("first", 0)
    with eng.Fori(0, (n - 2) // unroll) as m:
        for u in range(unroll):
            yield Turn("mid", m * unroll + (1 + u), u, m)
    yield Turn("last", n - 1)
    yield Turn("tail", n)


class Shared:

    def __init__(self, nc, ctx, B):
        def sb(name, shape, dt=F32):
            return ctx.enter_context(nc.sbuf_tensor(name, shape, dt))

        self.B = B
        self.sem = lambda name: ctx.enter_context(nc.semaphore(name))
        self.ring = [ctx.enter_context(nc.psum_tensor(f"ring{i}", [P, 512], F32)) for i in range(RING)]
        self.score_bank = [ctx.enter_context(nc.psum_tensor(f"score{i}", [P, 4, P], F32)) for i in range(4)]
        self.ring_filled = self.sem("ring_filled")
        self.x_sb = sb("x_sb", [P, B, D])
        self.ident = sb("ident", [P, P])
        self.pow_half = sb("pow_half", [P, B])


def self_attention(nc, sh, x, w_attn, w_proj, ln_w2, rope_cos, rope_sin, cross_weights, cross_raw_in, xs_dram, xs_cleared):
    B, x_sb, ident, pow_half, sem = sh.B, sh.x_sb, sh.ident, sh.pow_half, sh.sem
    ring, score_bank, ring_filled = sh.ring, sh.score_bank, sh.ring_filled
    QC, KC = NQ * HD, NKV * HD
    G = QC + 2 * KC

    with ExitStack() as ctx:
        def sb(name, shape, dt=F32):
            return ctx.enter_context(nc.sbuf_tensor(name, shape, dt))

        ident_b = sb("ident_b", [P, P], BF16)
        until = sb("until", [P, P])
        after = sb("after", [P, P])
        hidden_b = sb("hidden_b", [P, 4, P], BF16)
        cos_sb = sb("cos_sb", [P, HD])
        sin_sb = sb("sin_sb", [P, HD])
        lnw_sb = sb("lnw_sb", [P, 1])
        stage = sh.raw[:, 0:KD * (G + 8)].rearrange("p (k n) -> p k n", k=KD)
        wa_hi = sb("wa_hi", [P, KD, G + 8], F32R)
        wa_lo = sb("wa_lo", [P, KD, G + 8], F32R)
        wp_stage = sh.raw[:, KD * (G + 8):KD * (G + 8) + 8 * D].rearrange("p (k n) -> p k n", k=8)
        wp_hi = sb("wp_hi", [P, 8, D], F32R)
        wp_lo = sb("wp_lo", [P, 8, D], F32R)
        vmean = sb("vmean", [P, KD, NKV])
        bn6 = sb("bn6", [P, B, 6])
        mean = sb("mean", [P, B])
        diff = sb("diff", [P, B])
        var = sb("var", [P, B])
        rstd = sb("rstd", [P, B])
        xn = sb("xn", [P, D])
        xT_hi = sb("xT_hi", [P, KD, P], F32R)
        xT_lo = sb("xT_lo", [P, KD, P], F32R)
        zero_row = sb("zero_row", [P, D])
        t1 = [sb(f"t1_{j}", [P, 8, 2, 32]) for j in range(3)]
        t2 = [sb(f"t2_{j}", [P, 8, 2, 32]) for j in range(3)]
        qr = [sb(f"qr_{j}", [P, 4, P]) for j in range(3)]
        qkT = [sb(f"qkT_{i}", [P, 12, P]) for i in range(2)]
        v_sb = [sb(f"v_{i}", [P, NKV, HD + 1]) for i in range(2)]
        z = sb("z", [P, 8])
        az = sb("az", [P, 8])
        ez = sb("ez", [P, 8])
        sp = sb("sp", [P, 8])
        lg = sb("lg", [P, 8])
        d_rhs = sb("d_rhs", [P, 8, P])
        decay = [sb(f"decay_{i}", [P, 8, P]) for i in range(2)]
        abs_s = [sb(f"abs_{g}", [P, 4, P]) for g in range(4)]
        r_sb = [sb(f"r_{g}", [P, 4, P]) for g in range(4)]
        rmax = sb("rmax", [P, 16])
        rinv = sb("rinv", [P, 16])
        aT = [sb(f"aT_{i}", [P, 4, P]) for i in range(2)]
        y_sb = sb("y_sb", [P, 16, HD + 1])
        sq = sb("sq", [P, 16, HD])
        ms = sb("ms", [P, 16])
        den = sb("den", [P, 16])
        den2 = sb("den2", [P, 16])
        var_y = sb("var_y", [P, 16])
        f_sb = sb("f_sb", [P, 16])
        yn = sb("yn", [P, 8, P])
        yT_hi = sb("yT_hi", [P, 8, P], F32R)
        yT_lo = sb("yT_lo", [P, 8, P], F32R)

        x_in = [sem("x_in0"), sem("x_in1")]
        w_in, wp_in, tab_in = sem("w_in"), sem("wp_in"), sem("tab_in")
        const_done, const_step = sem("const_done"), sem("const_step")
        ident_done = sem("ident_done")
        vmean_done, vcent_done, wa_hi_done, wa_done, wp_scaled, wp_hi_done, wp_done = (
            sem(n) for n in ("vmean_done", "vcent_done", "wa_hi_done", "wa_done", "wp_scaled", "wp_hi_done", "wp_done"))
        stats_done, stat_step, x_var_done, rstd_done, xn_done = (
            sem(n) for n in ("stats_done", "stat_step", "x_var_done", "rstd_done", "xn_done"))
        xT_hi_done, xT_done = sem("xT_hi_done"), sem("xT_done")
        rope_done, rope_added, qkT_done, v_done = (sem(n) for n in ("rope_done", "rope_added", "qkT_done", "v_done"))
        z_done, az_done, ez_done, sp_done, lg_done, drhs_done, decay_done = (
            sem(n) for n in ("z_done", "az_done", "ez_done", "sp_done", "lg_done", "drhs_done", "decay_done"))
        scores_done, abs_done, r_done, rmax_done, rinv_done, b_done, aT_done = (
            sem(n) for n in ("scores_done", "abs_done", "r_done", "rmax_done", "rinv_done", "b_done", "aT_done"))
        y_done, sq_done, ms_done, den_done, den2_done, var_done, f_done, yn_done = (
            sem(n) for n in ("y_done", "sq_done", "ms_done", "den_done", "den2_done", "var_done", "f_done", "yn_done"))
        yT_hi_done, yT_done, x_added = sem("yT_hi_done"), sem("yT_done"), sem("x_added")

        jobs = Ring(ring, ring_filled, {
            "pro": ["xT", "q0", "q1", "g", "k", "v", "QT0", "QT1", "D0", "QT2", "D1"],
            "first": ["xT", "tr0", "q0", "q1", "tr1", "g", "k", "AV0", "v", "tr2", "AV1", "QT0", "tr3", "QT1",
                      "AV2", "D0", "QT2", "D1", "AV3"],
            "mid": ["xT", "yT0", "yT1", "tr0", "q0", "q1", "wproj", "tr1", "g", "k", "AV0", "v", "tr2", "AV1", "QT0",
                    "tr3", "QT1", "AV2", "D0", "QT2", "D1", "AV3"],
            "last": ["yT0", "yT1", "tr0", "wproj", "tr1", "AV0", "tr2", "AV1", "tr3", "AV2", "AV3"],
            "tail": ["yT0", "yT1", "wproj"],
        }, {
            "yT0": (yT_done, 2, -1), "yT1": (yT_done, 2, 0), "wproj": (x_added, 1, 0), "xT": (xT_done, 1, 2),
            "q0": (rope_done, 3, 4), "q1": (rope_done, 3, 5), "k": (rope_done, 3, 6), "g": (z_done, 1, 2),
            "v": (v_done, 1, 2), "QT0": (qkT_done, 3, 4), "QT1": (qkT_done, 3, 5), "QT2": (qkT_done, 3, 6),
            "D0": (decay_done, 2, 3), "D1": (decay_done, 2, 4),
            **{f"tr{g}": (aT_done, 4, g + 1) for g in range(4)}, **{f"AV{g}": (y_done, 4, g + 1) for g in range(4)},
        }, 0, B - 2, 2)
        start, filled = jobs.start, jobs.filled

        block = ctx.enter_context(nc.Block())

        @block.sync
        def _(sp_):
            xv = x.rearrange("b t d -> t b d")
            sp_.dma_start(x_sb[:, 0:2, :], xv[:, 0:2, :]).then_inc(x_in[0], 16)
            sp_.dma_start(stage, w_attn.rearrange("(k p) n -> p k n", p=P)).then_inc(w_in, 16)
            sp_.dma_start(cos_sb[:], rope_cos).then_inc(tab_in, 16)
            sp_.dma_start(sin_sb[:], rope_sin).then_inc(tab_in, 16)
            sp_.dma_start(lnw_sb[:], ln_w2).then_inc(tab_in, 16)
            sp_.dma_start(wp_stage, w_proj.rearrange("(k p) n -> p k n", p=P)).then_inc(wp_in, 16)
            sp_.dma_start(x_sb[:, 2:B, :], xv[:, 2:B, :]).then_inc(x_in[1], 16)
            sp_.wait_ge(wa_done, KD)
            sp_.wait_ge(wp_done, 1)
            for n, w in enumerate(cross_weights):
                sp_.dma_start(sh.raw[:, 2048 * n:2048 * n + 2048].rearrange("p (k n) -> p k n", n=w.shape[1]),
                              w.rearrange("(k p) n -> p k n", p=P)).then_inc(cross_raw_in, 16)
            sp_.wait_ge(const_done, 1)
            for xs in xs_dram:
                sp_.dma_start(xs.rearrange("(n p) d -> p n d", p=P),
                              zero_row[:].rearrange("p (o d) -> p o d", o=1).to_broadcast([P, xs.shape[0] // P, D])).then_inc(xs_cleared, 16)
            sp_.wait_ge(xs_cleared, 32)

        @block.tensor
        def _(pe):
            def project(out, a_hi, a_lo, w_hi, w_lo, cols, K):
                for k in range(K):
                    nc.tensor.matmul(out, a_hi[:, k, :], w_lo[:, k, cols], start=(k == 0), stop=False)
                    nc.tensor.matmul(out, a_lo[:, k, :], w_hi[:, k, cols], start=False, stop=False)
                    last = nc.tensor.matmul(out, a_hi[:, k, :], w_hi[:, k, cols], start=False, stop=(k == K - 1))
                return last

            def scores(it, o):
                b, qk = it.b, qkT[it.par]
                if o == 0:
                    pe.wait_ge(qkT_done, 3 * (b + 1))
                if it.kind != "first":
                    pe.wait_ge(abs_done, 4 * b + (2 * o - 2))
                for k in range(4):
                    for half in range(2):
                        rows = slice(64 * half, 64 * half + 64)
                        last = nc.tensor.matmul(score_bank[2 * o + half][:, k, :], qk[rows, 4 * o + k, :],
                                                qk[rows, 8 + k, :], start=True, stop=True)
                last.then_inc(scores_done, 1)

            def turn_rows(it, g):
                bank = start(pe, it, f"tr{g}")
                pe.wait_ge(b_done, 4 * it.b + (g + 1))
                for k in range(4):
                    last = nc.tensor.transpose(bank[:, k * P:(k + 1) * P], r_sb[g][:, k, :], ident[:])
                last.then_inc(ring_filled, 1)

            def attend(it, g):
                bank = start(pe, it, f"AV{g}")
                pe.wait_ge(aT_done, 4 * it.b + (g + 1))
                if g == 0:
                    pe.wait_ge(v_done, it.b + 1)
                half = g % 2
                for k in range(4):
                    last = nc.tensor.matmul(bank[:, k * 65:(k + 1) * 65], aT[g % 2][:, k, :],
                                            v_sb[it.par][:, 4 * half + k, :], start=True, stop=True)
                last.then_inc(ring_filled, 1)

            def qk_cols(it, name, c0, n):
                bank = start(pe, it, name)
                project(bank[:, 0:n], xT_hi, xT_lo, wa_hi, wa_lo, slice(c0, c0 + n), KD).then_inc(ring_filled, 1)

            def qk_turn(it, j):
                bank = start(pe, it, f"QT{j}")
                pe.wait_ge(rope_added, 3 * it.b + (4 + j))
                for c in range(4):
                    last = nc.tensor.transpose(bank[:, c * P:(c + 1) * P], qr[j][:, c, :], ident[:])
                last.then_inc(ring_filled, 1)

            def decays(it, j):
                bank = start(pe, it, f"D{j}")
                pe.wait_ge(drhs_done, it.b + 2)
                nc.tensor.matmul(bank[:, :], until[:], d_rhs[:, 4 * j:4 * j + 4, :], start=True, stop=False)
                nc.tensor.matmul(bank[:, :], ident_b[:], hidden_b[:, :, :], start=False, stop=True).then_inc(ring_filled, 1)

            pe.wait_ge(ident_done, 1)
            pe.wait_ge(const_done, 1)
            pe.wait_ge(wa_done, KD)
            for it in turns(pe, B, 2):
                if it.kind == "first":
                    pe.wait_ge(wp_done, 1)
                if it.nxt:
                    bank = start(pe, it, "xT")
                    pe.wait_ge(xn_done, it.b + 2)
                    for k in range(KD):
                        last = nc.tensor.transpose(bank[:, k * P:(k + 1) * P], xn[:, k * P:(k + 1) * P], ident[:])
                    last.then_inc(ring_filled, 1)
                if it.cur:
                    scores(it, 0)
                    scores(it, 1)
                if it.prev:
                    for j in range(2):
                        bank = start(pe, it, f"yT{j}")
                        pe.wait_ge(yn_done, it.b * 4 + (2 * j - 2))
                        for c in range(4):
                            last = nc.tensor.transpose(bank[:, c * P:(c + 1) * P], yn[:, 4 * j + c, :], ident[:])
                        last.then_inc(ring_filled, 1)
                if it.cur:
                    turn_rows(it, 0)
                if it.nxt:
                    pe.wait_ge(xT_done, it.b + 2)
                    qk_cols(it, "q0", 0, 512)
                    qk_cols(it, "q1", 512, 512)
                if it.prev:
                    bank = start(pe, it, "wproj")
                    pe.wait_ge(yT_done, 2 * it.b)
                    project(bank[:, 0:D], yT_hi, yT_lo, wp_hi, wp_lo, slice(0, D), 8).then_inc(ring_filled, 1)
                if it.cur:
                    turn_rows(it, 1)
                if it.nxt:
                    qk_cols(it, "g", G, 8)
                    qk_cols(it, "k", QC, 512)
                if it.cur:
                    attend(it, 0)
                if it.nxt:
                    qk_cols(it, "v", QC + KC, 512)
                if it.cur:
                    turn_rows(it, 2)
                    attend(it, 1)
                if it.nxt:
                    qk_turn(it, 0)
                if it.cur:
                    turn_rows(it, 3)
                if it.nxt:
                    qk_turn(it, 1)
                if it.cur:
                    attend(it, 2)
                if it.nxt:
                    decays(it, 0)
                    qk_turn(it, 2)
                    decays(it, 1)
                if it.cur:
                    attend(it, 3)

        @block.scalar
        def _(act):
            def take_turn(it, g):
                bank = filled(act, it, f"tr{g}")
                if it.kind != "first" or g >= 2:
                    if g >= 2:
                        jobs.wait_filled(act, it, f"AV{g - 2}")
                nc.scalar.activation(aT[g % 2][:, :, :].rearrange("p a b -> p (a b)"), bank[:, :], ACT.Square).then_inc(aT_done, 1)

            def take_rows(it, g):
                bank = filled(act, it, f"AV{g}")
                if it.kind != "first" and g == 0:
                    act.wait_ge(yn_done, it.b * 4)
                rows = bank[:, 0:260].rearrange("p (h d) -> p h d", d=HD + 1)
                nc.scalar.activation(sq[:, 4 * g:4 * g + 4, :], rows[:, :, 0:HD], ACT.Square).then_inc(sq_done, 1)
                nc.scalar.copy(y_sb[:, 4 * g:4 * g + 4, :].rearrange("p a b -> p (a b)"), bank[:, 0:260]).then_inc(y_done, 1)

            def take_qk(it, j):
                bank = filled(act, it, f"QT{j}")
                nc.scalar.copy(qkT[1 - it.par][:, 4 * j:4 * j + 4, :].rearrange("p a b -> p (a b)"), bank[:, :]).then_inc(qkT_done, 1)

            def take_decay(it, j):
                bank = filled(act, it, f"D{j}")
                if it.cur:
                    act.wait_ge(r_done, 4 * it.b)
                nc.scalar.activation(decay[1 - it.par][:, 4 * j:4 * j + 4, :].rearrange("p a b -> p (a b)"), bank[:, :],
                                     ACT.Exp, scale=0.5).then_inc(decay_done, 1)

            for k in range(KD):
                act.wait_ge(w_in, 16)
                act.wait_ge(vcent_done, 1)
                nc.scalar.copy(wa_hi[:, k, :], stage[:, k, :]).then_inc(wa_hi_done, 1)
            act.wait_ge(wp_scaled, 1)
            nc.scalar.copy(wp_hi[:], wp_stage).then_inc(wp_hi_done, 1)
            for it in turns(act, B, 2):
                if it.nxt:
                    bank = filled(act, it, "xT")
                    nc.scalar.copy(xT_hi[:].rearrange("p a b -> p (a b)"), bank[:, 0:D]).then_inc(xT_hi_done, 1)
                if it.cur:
                    for g in range(4):
                        act.wait_ge(scores_done, 2 * it.b + (1 + g // 2))
                        if it.kind != "first":
                            act.wait_ge(r_done, 4 * it.b + (g - 3))
                        nc.scalar.activation(abs_s[g][:], score_bank[g][:], ACT.Abs, scale=HD ** -0.5).then_inc(abs_done, 1)
                if it.prev:
                    for j in range(2):
                        bank = filled(act, it, f"yT{j}")
                        nc.scalar.copy(yT_hi[:, 4 * j:4 * j + 4, :].rearrange("p a b -> p (a b)"), bank[:, :]).then_inc(yT_hi_done, 1)
                if it.cur:
                    take_turn(it, 0)
                    take_turn(it, 1)
                if it.nxt:
                    act.wait_ge(z_done, it.b + 2)
                    nc.scalar.activation(az[:], z[:], ACT.Abs).then_inc(az_done, 1)
                    act.wait_ge(az_done, it.b + 2)
                    nc.scalar.activation(ez[:], az[:], ACT.Exp, scale=-1.0).then_inc(ez_done, 1)
                    act.wait_ge(ez_done, it.b + 2)
                    nc.scalar.activation(sp[:], ez[:], ACT.Ln, bias=1.0).then_inc(sp_done, 1)
                if it.cur:
                    take_rows(it, 0)
                if it.nxt:
                    bank = filled(act, it, "v")
                    nc.scalar.copy(v_sb[1 - it.par][:, :, 0:HD], bank[:, :].rearrange("p (h d) -> p h d", d=HD)).then_inc(v_done, 1)
                if it.cur:
                    take_turn(it, 2)
                    take_rows(it, 1)
                if it.nxt:
                    take_qk(it, 0)
                if it.cur:
                    take_turn(it, 3)
                if it.nxt:
                    take_qk(it, 1)
                if it.cur:
                    take_rows(it, 2)
                if it.nxt:
                    take_decay(it, 0)
                    take_qk(it, 2)
                    take_decay(it, 1)
                if it.cur:
                    take_rows(it, 3)

        @block.vector
        def _(dve):
            def rope(it, j, name):
                bank = filled(dve, it, name)
                if it.kind != "pro":
                    dve.wait_ge(rope_added, 3 * it.b + (1 + j))
                q = bank[:, :].rearrange("p (h e i) -> p h e i", e=2, i=32)
                cosb = cos_sb[:, :].rearrange("p (o n) -> p o n", o=1).to_broadcast([P, 8, HD])
                nc.vector.tensor_tensor(t1[j][:].rearrange("p h e i -> p h (e i)"), q.rearrange("p h e i -> p h (e i)"), cosb, ALU.mult)
                for e in range(2):
                    sinb = sin_sb[:, 32 * e:32 * e + 32].rearrange("p (o n) -> p o n", o=1).to_broadcast([P, 8, 32])
                    last = nc.vector.tensor_tensor(t2[j][:, :, e, :], q[:, :, 1 - e, :], sinb, ALU.mult)
                last.then_inc(rope_done, 1)

            def weigh(it, g):
                b, half = it.b, g % 2
                dve.wait_ge(abs_done, 4 * b + (g + 1))
                if g == 0:
                    dve.wait_ge(decay_done, 2 * b + 2)
                if it.kind != "first":
                    dve.wait_ge(aT_done, 4 * b + (g - 3))
                nc.vector.scalar_tensor_tensor(
                    out=r_sb[g][:], in0=abs_s[g][:], scalar=1e-30, in1=decay[it.par][:, 4 * half:4 * half + 4, :],
                    op0=ALU.add, op1=ALU.mult).then_inc(r_done, 1)
                dve.wait_ge(r_done, 4 * b + (g + 1))
                nc.vector.tensor_reduce(rmax[:, 4 * g:4 * g + 4], r_sb[g][:], AX.X, ALU.max).then_inc(rmax_done, 1)
                dve.wait_ge(rmax_done, 4 * b + (g + 1))
                nc.vector.reciprocal(rinv[:, 4 * g:4 * g + 4], rmax[:, 4 * g:4 * g + 4]).then_inc(rinv_done, 1)

            def spreads(b, g):
                n, cols = 4 * b + (g + 1), slice(4 * g, 4 * g + 4)
                dve.wait_ge(sq_done, n)
                dve.wait_ge(y_done, n)
                nc.vector.tensor_scalar(den[:, cols].rearrange("p (h o) -> p h o", o=1), y_sb[:, cols, HD:HD + 1], 1e-6,
                                        (1e-9 * HD) ** 0.5, ALU.add, ALU.mult).then_inc(den_done, 1)
                dve.wait_ge(den_done, n)
                nc.vector.tensor_tensor(den2[:, cols], den[:, cols], den[:, cols], ALU.mult).then_inc(den2_done, 1)
                nc.vector.tensor_reduce(ms[:, cols], sq[:, cols, :], AX.X, ALU.add).then_inc(ms_done, 1)
                dve.wait_ge(den2_done, n)
                dve.wait_ge(ms_done, n)
                nc.vector.tensor_tensor(var_y[:, cols], den2[:, cols], ms[:, cols], ALU.add).then_inc(var_done, 1)

            def statistics(lo, hi, unroll, steps):
                with dve.Fori(lo // unroll, hi // unroll) as m:
                    for u in range(unroll):
                        last = nc.vector.bn_stats(bn6[:, m * unroll + u, :], x_sb[:, m * unroll + u, :])
                    last.then_inc(stats_done, 1)
                dve.wait_ge(stats_done, hi // unroll)
                sl = slice(lo, hi)
                col = lambda c: bn6[:, sl, c:c + 1].rearrange("p b o -> p (b o)")
                nc.vector.tensor_tensor(diff[:, sl], col(1), col(4), ALU.subtract).then_inc(stat_step, 1)
                nc.vector.tensor_tensor(mean[:, sl], col(1), col(4), ALU.add).then_inc(stat_step, 1)
                nc.vector.tensor_tensor(var[:, sl], col(2), col(5), ALU.add).then_inc(stat_step, 1)
                dve.wait_ge(stat_step, steps + 3)
                nc.vector.tensor_tensor(diff[:, sl], diff[:, sl], diff[:, sl], ALU.mult).then_inc(stat_step, 1)
                nc.vector.tensor_scalar(mean[:, sl], mean[:, sl], 0.5, None, ALU.mult).then_inc(stat_step, 1)
                nc.vector.tensor_scalar(var[:, sl], var[:, sl], 1.0 / D, 1e-5, ALU.mult, ALU.add).then_inc(stat_step, 1)
                dve.wait_ge(stat_step, steps + 6)
                nc.vector.scalar_tensor_tensor(out=var[:, sl], in0=diff[:, sl], scalar=0.25, in1=var[:, sl], op0=ALU.mult,
                                               op1=ALU.add).then_inc(x_var_done, 1)

            dve.wait_ge(x_in[0], 16)
            statistics(0, 2, 2, 0)
            dve.wait_ge(w_in, 16)
            vv = stage[:, :, QC + KC:G].rearrange("p k (h d) -> p k h d", d=HD)
            for k in range(KD):
                last = nc.vector.tensor_reduce(vmean[:, k, :], vv[:, k, :, :], AX.X, ALU.add)
            last.then_inc(vmean_done, 1)
            dve.wait_ge(vmean_done, 1)
            last = nc.vector.tensor_scalar(vmean[:], vmean[:], 1.0 / HD, None, ALU.mult)
            last.then_inc(vmean_done, 1)
            dve.wait_ge(vmean_done, 2)
            for k in range(KD):
                last = nc.vector.tensor_tensor(vv[:, k, :, :], vv[:, k, :, :],
                                               vmean[:, k, :].rearrange("p (h o) -> p h o", o=1).to_broadcast([P, NKV, HD]),
                                               ALU.subtract)
            last.then_inc(vcent_done, 1)
            dve.wait_ge(vcent_done, 1)
            for k in range(KD):
                dve.wait_ge(wa_hi_done, k + 1)
                nc.vector.tensor_tensor(wa_lo[:, k, :], stage[:, k, :], wa_hi[:, k, :].bitcast(F32), ALU.subtract).then_inc(wa_done, 1)
            dve.wait_ge(wp_in, 16)
            dve.wait_ge(tab_in, 48)
            nc.vector.tensor_scalar(wp_stage, wp_stage, lnw_sb[:, 0:1], float(HD) ** 0.5, ALU.mult, ALU.mult).then_inc(wp_scaled, 1)
            dve.wait_ge(wp_scaled, 1)
            dve.wait_ge(wp_hi_done, 1)
            nc.vector.tensor_tensor(wp_lo[:], wp_stage, wp_hi[:].bitcast(F32), ALU.subtract).then_inc(wp_done, 1)

            dve.wait_ge(rstd_done, 1)
            for it in turns(dve, B, 2):
                if it.nxt:
                    col = bass.ds(it.b + 1, 1)
                    nc.vector.tensor_scalar(xn[:], x_sb[:, it.b + 1, :], mean[:, col], rstd[:, col], ALU.subtract,
                                            ALU.mult).then_inc(xn_done, 1)
                if it.prev:
                    spreads(it.b - 1, 2)
                if it.nxt:
                    bank = filled(dve, it, "xT")
                    dve.wait_ge(xT_hi_done, it.b + 2)
                    nc.vector.tensor_tensor(xT_lo[:].rearrange("p a b -> p (a b)"), bank[:, 0:D],
                                            xT_hi[:].bitcast(F32).rearrange("p a b -> p (a b)"), ALU.subtract).then_inc(xT_done, 1)
                if it.prev:
                    spreads(it.b - 1, 3)
                if it.cur:
                    weigh(it, 0)
                    weigh(it, 1)
                if it.prev:
                    for j in range(2):
                        bank = filled(dve, it, f"yT{j}")
                        dve.wait_ge(yT_hi_done, 2 * it.b + (j - 1))
                        cols = slice(4 * j, 4 * j + 4)
                        nc.vector.tensor_tensor(yT_lo[:, cols, :].rearrange("p a b -> p (a b)"), bank[:, :],
                                                yT_hi[:, cols, :].bitcast(F32).rearrange("p a b -> p (a b)"), ALU.subtract).then_inc(yT_done, 1)
                if it.nxt:
                    rope(it, 0, "q0")
                if it.cur:
                    weigh(it, 2)
                if it.nxt:
                    rope(it, 1, "q1")
                if it.cur:
                    weigh(it, 3)
                if it.prev:
                    bank = filled(dve, it, "wproj")
                    xp = x_sb[:, it.b - 1, :]
                    nc.vector.tensor_tensor(xp, xp, bank[:, 0:D], ALU.add).then_inc(x_added, 1)
                if it.nxt:
                    bank = filled(dve, it, "g")
                    nc.vector.tensor_scalar(z[:], bank[:, 0:8], 6.906768, None, ALU.add).then_inc(z_done, 1)
                    rope(it, 2, "k")
                    dve.wait_ge(sp_done, it.b + 2)
                    nc.vector.scalar_tensor_tensor(out=lg[:], in0=z[:], scalar=0.0, in1=sp[:], op0=ALU.min,
                                                   op1=ALU.subtract).then_inc(lg_done, 1)
                if it.cur:
                    spreads(it.b, 0)
                    spreads(it.b, 1)
                if it.kind == "first":
                    dve.wait_ge(x_in[1], 16)
                    statistics(2, B, 2, 6)
                    dve.wait_ge(rstd_done, 2)

        @block.gpsimd
        def _(pool):
            def scale_rows(it, g):
                pool.wait_ge(rinv_done, 4 * it.b + (g + 1))
                r = r_sb[g][:]
                nc.gpsimd.tensor_tensor(r, r, rinv[:, 4 * g:4 * g + 4].rearrange("p (h o) -> p h o", o=1).to_broadcast([P, 4, P]),
                                        ALU.mult).then_inc(b_done, 1)

            def rope_add(it, j):
                pool.wait_ge(rope_done, 3 * it.b + (4 + j))
                if it.kind != "pro":
                    pool.wait_ge(qkT_done, 3 * it.b + (1 + j))
                nc.gpsimd.tensor_tensor(qr[j][:].rearrange("p c n -> p (c n)"), t1[j][:].rearrange("p h e i -> p (h e i)"),
                                        t2[j][:].rearrange("p h e i -> p (h e i)"), ALU.add).then_inc(rope_added, 1)

            def normalise(b, g):
                cols = slice(4 * g, 4 * g + 4)
                pool.wait_ge(var_done, 4 * b + (g + 1))
                nc.gpsimd.tensor_tensor(f_sb[:, cols], var_y[:, cols], pow_half[:, 0:4], ALU.pow).then_inc(f_done, 1)
                pool.wait_ge(f_done, 4 * b + (g + 1))
                nc.gpsimd.tensor_tensor(yn[:, 2 * g:2 * g + 2, :].rearrange("p c (h d) -> p (c h) d", d=HD), y_sb[:, cols, 0:HD],
                                        f_sb[:, cols].rearrange("p (h o) -> p h o", o=1).to_broadcast([P, 4, HD]),
                                        ALU.mult).then_inc(yn_done, 1)

            nc.gpsimd.memset(ident[:], 0.0).then_inc(const_step, 1)
            nc.gpsimd.memset(zero_row[:], 0.0).then_inc(const_step, 1)
            nc.gpsimd.memset(until[:], 1.0).then_inc(const_step, 1)
            nc.gpsimd.memset(after[:], 1.0).then_inc(const_step, 1)
            nc.gpsimd.memset(hidden_b[:], 0.0).then_inc(const_step, 1)
            nc.gpsimd.memset(pow_half[:], -0.5).then_inc(const_step, 1)
            for v in v_sb:
                nc.gpsimd.memset(v[:], 1.0).then_inc(const_step, 1)
            pool.wait_ge(const_step, 8)
            nc.gpsimd.affine_select(out=ident[:], in_=ident[:], compare_op=ALU.not_equal, fill=1.0, base=0,
                                    pattern=[[-1, P]], channel_multiplier=1).then_inc(const_step, 1)
            nc.gpsimd.affine_select(out=until[:], in_=until[:], compare_op=ALU.is_ge, fill=0.0, base=0,
                                    pattern=[[1, P]], channel_multiplier=-1).then_inc(const_step, 1)
            nc.gpsimd.affine_select(out=after[:], in_=after[:], compare_op=ALU.is_ge, fill=0.0, base=-1,
                                    pattern=[[-1, P]], channel_multiplier=1).then_inc(const_step, 1)
            nc.gpsimd.affine_select(out=hidden_b[:], in_=hidden_b[:], compare_op=ALU.is_ge, fill=-30000.0, base=0,
                                    pattern=[[0, 4], [-1, P]], channel_multiplier=1).then_inc(const_step, 1)
            pool.wait_ge(const_step, 12)
            nc.gpsimd.tensor_copy(ident_b[:], ident[:]).then_inc(const_step, 1)
            pool.wait_ge(const_step, 13)
            pool.sem_inc(ident_done, 1)
            pool.sem_inc(const_done, 1)

            pool.wait_ge(x_var_done, 1)
            nc.gpsimd.tensor_tensor(rstd[:, 0:2], var[:, 0:2], pow_half[:, 0:2], ALU.pow).then_inc(rstd_done, 1)
            for it in turns(pool, B, 2):
                if it.prev:
                    normalise(it.b - 1, 2)
                    normalise(it.b - 1, 3)
                if it.cur:
                    scale_rows(it, 0)
                    scale_rows(it, 1)
                if it.nxt:
                    rope_add(it, 0)
                if it.cur:
                    scale_rows(it, 2)
                if it.nxt:
                    rope_add(it, 1)
                if it.cur:
                    scale_rows(it, 3)
                if it.nxt:
                    rope_add(it, 2)
                    pool.wait_ge(lg_done, it.b + 2)
                    if it.kind != "pro":
                        pool.wait_ge(decay_done, 2 * it.b + 2)
                    nc.gpsimd.tensor_tensor(d_rhs[:], after[:].rearrange("p (o n) -> p o n", o=1).to_broadcast([P, 8, P]),
                                            lg[:].rearrange("p (h o) -> p h o", o=1).to_broadcast([P, 8, P]),
                                            ALU.mult).then_inc(drhs_done, 1)
                if it.cur:
                    if it.kind != "first":
                        pool.wait_ge(yT_hi_done, 2 * it.b)
                    normalise(it.b, 0)
                    normalise(it.b, 1)
                if it.kind == "first":
                    pool.wait_ge(x_var_done, 2)
                    nc.gpsimd.tensor_tensor(rstd[:, 2:B], var[:, 2:B], pow_half[:, 2:B], ALU.pow).then_inc(rstd_done, 1)
    return jobs.end


def cross_attention(nc, sh, jobs_before, ctx_x, raw_in, w1, w1_in):
    B, x_sb, ident, pow_half, sem = sh.B, sh.x_sb, sh.ident, sh.pow_half, sh.sem
    ring, score_bank, ring_filled = sh.ring, sh.score_bank, sh.ring_filled
    PAIRS = B // 2
    KO = 8

    with ExitStack() as ctx:
        def sb(name, shape, dt=F32):
            return ctx.enter_context(nc.sbuf_tensor(name, shape, dt))

        w_raw = [sh.raw[:, 2048 * n:2048 * n + 2048] for n in range(4)]
        w_hi = [sb(f"cw_hi{n}", [P, 2048], F32R) for n in range(4)]
        w_lo = [sb(f"cw_lo{n}", [P, 2048], F32R) for n in range(4)]
        c_sb = sb("c_sb", [P, 2, D])
        bn6 = sb("c_bn6", [P, 2, 6])
        bn2 = sb("c_bn2", [P, 2, 2])
        vpe = sb("c_vpe", [P, 2])
        rstd = sb("c_rstd", [P, 2])
        xn = sb("c_xn", [P, 2, D])
        inT_hi = {n: sb(f"{n}T_hi2", [P, KD, 2, P], F32R) for n in "xc"}
        inT_lo = {n: sb(f"{n}T_lo2", [P, KD, 2, P], F32R) for n in "xc"}
        qT = sb("qT", [P, 8, 2 * P])
        kT = sb("kT", [P, 8, 2 * P])
        v_sb = [sb(f"c_v{u}", [P, 16 * HD]) for u in range(2)]
        p_sb = [sb(f"p_{i}", [P, 4, P]) for i in range(4)]
        smax = sb("smax", [P, 4, 4])
        den = sb("c_den", [P, 4, 4])
        rden = sb("rden", [P, 4, 4])
        pT = [sb(f"pT_{i}", [P, 4, P]) for i in range(2)]
        oT_hi = [sb(f"oT_hi{u}", [P, 8, P], F32R) for u in range(2)]
        oT_lo = [sb(f"oT_lo{u}", [P, 8, P], F32R) for u in range(2)]

        w_hi_done, w_done, c_in = sem("cw_hi_done"), sem("cw_done"), sem("c_in")
        bn6_done, bn6_seen, bn2_done, vpe_done, rstd_done, xn_done = (
            sem(f"c_{n}") for n in ("bn6_done", "bn6_seen", "bn2_done", "vpe_done", "rstd_done", "xn_done"))
        xT_hi_done, xT_done, cT_hi_done, cT_done = (sem(f"c_{n}") for n in ("xT_hi_done", "xT_done", "cT_hi_done", "cT_done"))
        q_done, k_done, v_done = (sem(f"c_{n}") for n in ("q_done", "k_done", "v_done"))
        scores_done, smax_done, sub_done, exp_done, den_done, rden_done, norm_done, pT_done = (
            sem(f"c_{n}") for n in ("scores_done", "smax_done", "sub_done", "exp_done", "den_done", "rden_done", "norm_done", "pT_done"))
        oT_hi_done, oT_done, x_added = (sem(f"c_{n}") for n in ("oT_hi_done", "oT_done", "x_added"))

        mid = ["trA3", "trB3", "q2", "q3", "AV3", "wo0",
               "trA0", "trB0", "k2", "k3", "AV0", "wo1", "xT", "v01", "v11",
               "cT", "trA1", "trB1", "q0", "q1", "AV1",
               "trA2", "trB2", "k0", "k1", "AV2", "v00", "v10"]
        last_turn = ("trA3", "trB3", "AV3", "wo0", "wo1")
        next_turn = ("xT", "cT", "q0", "q1", "k0", "k1", "v00", "v10")
        jobs = Ring(ring, ring_filled, {
            "pro": list(next_turn),
            "first": [n for n in mid if n not in last_turn],
            "mid": mid,
            "last": [n for n in mid if n not in next_turn],
            "tail": list(last_turn),
        }, {
            "xT": (xT_done, 1, 2), "cT": (cT_done, 1, 2),
            "q0": (q_done, 4, 5), "q1": (q_done, 4, 6), "q2": (q_done, 4, 3), "q3": (q_done, 4, 4),
            "k0": (k_done, 4, 5), "k1": (k_done, 4, 6), "k2": (k_done, 4, 3), "k3": (k_done, 4, 4),
            "v00": (v_done, 4, 5), "v10": (v_done, 4, 6), "v01": (v_done, 4, 3), "v11": (v_done, 4, 4),
            **{f"tr{'AB'[h]}{t}": (pT_done, 8, 2 * t + h + 1) for t in range(3) for h in range(2)},
            "trA3": (pT_done, 8, -1), "trB3": (pT_done, 8, 0),
            **{f"AV{t}": (oT_done, 4, t + 1) for t in range(3)}, "AV3": (oT_done, 4, 0),
            "wo0": (x_added, 2, -1), "wo1": (x_added, 2, 0),
        }, jobs_before, PAIRS - 2, 1)
        start, filled = jobs.start, jobs.filled

        block = ctx.enter_context(nc.Block())

        @block.sync
        def _(sync):
            def load(it):
                src = ctx_x.rearrange("(n two) t d -> n t two d", two=2)[it.b + 1]
                sync.dma_start(c_sb[:], src).then_inc(c_in, 16)

            for it in turns(sync, PAIRS, 1):
                if it.nxt:
                    if it.kind != "pro":
                        if it.kind == "first":
                            jobs.wait_filled(sync, Turn("pro", -1), "cT")
                        else:
                            sync.wait_ge(cT_hi_done, it.b + 1)
                    load(it)
                if it.kind == "first":
                    sync.wait_ge(w_done, 4)
                    sync.dma_start(sh.raw[:, :].rearrange("p (e k n) -> p e k n", e=w1.shape[0], k=KD),
                                   w1.rearrange("e (k p) n -> p e k n", p=P)).then_inc(w1_in, 16)

        @block.tensor
        def _(pe):
            def three(out, pairs):
                for n, ((a_hi, a_lo), (b_hi, b_lo)) in enumerate(pairs):
                    nc.tensor.matmul(out, a_hi, b_lo, start=(n == 0), stop=False)
                    nc.tensor.matmul(out, a_lo, b_hi, start=False, stop=False)
                    last = nc.tensor.matmul(out, a_hi, b_hi, start=False, stop=(n == len(pairs) - 1))
                return last

            def weight(n, k, c0, c1):
                cols = 1024 if n < 3 else D
                return tuple(w[n][:, k * cols + c0:k * cols + c1] for w in (w_hi, w_lo))

            def turn_in(it, name, tile, ready):
                bank = start(pe, it, f"{name}T")
                pe.wait_ge(ready, (it.b + 2) * (1 if name == "x" else 16))
                for k in range(KD):
                    for u in range(2):
                        last = nc.tensor.transpose(bank[:, (2 * k + u) * P:(2 * k + u + 1) * P],
                                                   tile[:, u, k * P:(k + 1) * P], ident[:])
                last.then_inc(ring_filled, 1)

            def project_T(it, which, j):
                bank = start(pe, it, f"{which}{j}")
                n, src = (0, "x") if which == "q" else (1, "c")
                for c in range(2):
                    last = three(bank[:, c * 2 * P:(c + 1) * 2 * P], [
                        (weight(n, k, (2 * j + c) * P, (2 * j + c + 1) * P),
                         tuple(t[src][:, k, :, :].rearrange("p u t -> p (u t)") for t in (inT_hi, inT_lo)))
                        for k in range(KD)])
                last.then_inc(ring_filled, 1)

            def project_v(it, u, o):
                bank = start(pe, it, f"v{u}{o}")
                three(bank[:, :], [(tuple(t["c"][:, k, u, :] for t in (inT_hi, inT_lo)), weight(2, k, 512 * o, 512 * o + 512))
                                   for k in range(KD)]).then_inc(ring_filled, 1)

            def scores(it, t):
                u, o = t % 2, t // 2
                if t == 0:
                    pe.wait_ge(q_done, 4 * it.b + 2)
                    pe.wait_ge(k_done, 4 * it.b + 2)
                if t == 2:
                    pe.wait_ge(q_done, 4 * it.b + 4)
                    pe.wait_ge(k_done, 4 * it.b + 4)
                if it.kind != "first" or t >= 2:
                    pe.wait_ge(sub_done, 8 * it.b + (2 * t - 2))
                for k in range(4):
                    for half in range(2):
                        rows = slice(64 * half, 64 * half + 64)
                        cols = slice(u * P, (u + 1) * P)
                        last = nc.tensor.matmul(score_bank[2 * (t % 2) + half][:, k, :], qT[rows, 4 * o + k, cols],
                                                kT[rows, 4 * o + k, cols], start=True, stop=True)
                last.then_inc(scores_done, 1)

            def turn_rows(it, t):
                b = it.b - 1 if t == 3 else it.b
                for half in range(2):
                    bank = start(pe, it, f"tr{'AB'[half]}{t}")
                    pe.wait_ge(norm_done, 8 * b + (2 * t + half + 1))
                    for k in range(4):
                        last = nc.tensor.transpose(bank[:, k * P:(k + 1) * P], p_sb[2 * (t % 2) + half][:, k, :], ident[:])
                    last.then_inc(ring_filled, 1)

            def attend(it, t):
                b, u, o = it.b - 1 if t == 3 else it.b, t % 2, t // 2
                bank = start(pe, it, f"AV{t}")
                pe.wait_ge(v_done, 4 * b + (2 if o == 0 else 4))
                pe.wait_ge(pT_done, 8 * b + (2 * t + 2))
                for k in range(4):
                    for half in range(2):
                        h = 8 * o + 2 * k + half
                        last = nc.tensor.matmul(bank[64 * half:64 * half + 64, k * P:(k + 1) * P],
                                                v_sb[u][:, h * HD:(h + 1) * HD], pT[half][:, k, :], start=True, stop=True,
                                                skip_group_check=True)
                last.then_inc(ring_filled, 1)

            def project_out(it, u):
                bank = start(pe, it, f"wo{u}")
                pe.wait_ge(oT_done, 4 * it.b + (-1 if u == 0 else 0))
                three(bank[:, 0:D], [((oT_hi[u][:, k, :], oT_lo[u][:, k, :]), weight(3, k, 0, D))
                                     for k in range(KO)]).then_inc(ring_filled, 1)

            for it in turns(pe, PAIRS, 1):
                if it.kind == "pro":
                    pe.wait_ge(w_done, 4)
                if it.cur:
                    scores(it, 0)
                if it.prev:
                    turn_rows(it, 3)
                if it.cur:
                    project_T(it, "q", 2)
                    project_T(it, "q", 3)
                if it.prev:
                    attend(it, 3)
                    project_out(it, 0)
                if it.cur:
                    scores(it, 1)
                    turn_rows(it, 0)
                    project_T(it, "k", 2)
                    project_T(it, "k", 3)
                    attend(it, 0)
                if it.prev:
                    project_out(it, 1)
                if it.nxt:
                    turn_in(it, "x", xn, xn_done)
                if it.cur:
                    project_v(it, 0, 1)
                    project_v(it, 1, 1)
                    scores(it, 2)
                if it.nxt:
                    turn_in(it, "c", c_sb, c_in)
                if it.cur:
                    turn_rows(it, 1)
                if it.nxt:
                    pe.wait_ge(xT_done, it.b + 2)
                    project_T(it, "q", 0)
                    project_T(it, "q", 1)
                if it.cur:
                    attend(it, 1)
                    scores(it, 3)
                    turn_rows(it, 2)
                if it.nxt:
                    pe.wait_ge(cT_done, it.b + 2)
                    project_T(it, "k", 0)
                    project_T(it, "k", 1)
                if it.cur:
                    attend(it, 2)
                if it.nxt:
                    project_v(it, 0, 0)
                    project_v(it, 1, 0)

        @block.scalar
        def _(act):
            def expo(it, t):
                for half in range(2):
                    p = p_sb[2 * (t % 2) + half]
                    act.wait_ge(sub_done, 8 * it.b + (2 * t + half + 1))
                    nc.scalar.activation(p[:], p[:], ACT.Exp, scale=HD ** -0.5).then_inc(exp_done, 1)

            def take_turn(it, t):
                for half in range(2):
                    bank = filled(act, it, f"tr{'AB'[half]}{t}")
                    if t == 0 and it.kind != "first":
                        jobs.wait_filled(act, it, "AV3")
                    if t in (1, 2):
                        jobs.wait_filled(act, it, f"AV{t - 1}")
                    nc.scalar.copy(pT[half][:].rearrange("p a b -> p (a b)"), bank[:, :]).then_inc(pT_done, 1)

            def take_q(it, j):
                bank = filled(act, it, f"q{j}")
                nc.scalar.copy(qT[:, 2 * j:2 * j + 2, :].rearrange("p a b -> p (a b)"), bank[:, :]).then_inc(q_done, 1)

            def take_out(it, t):
                u, o = t % 2, t // 2
                bank = filled(act, it, f"AV{t}")
                if it.kind != "first" and t < 2:
                    jobs.wait_filled(act, it, f"wo{t}")
                nc.scalar.copy(oT_hi[u][:, 4 * o:4 * o + 4, :].rearrange("p a b -> p (a b)"), bank[:, :]).then_inc(oT_hi_done, 1)

            def take_in(it, n, done):
                bank = filled(act, it, f"{n}T")
                nc.scalar.copy(inT_hi[n][:].rearrange("p k u t -> p (k u t)"), bank[:, :]).then_inc(done, 1)

            def take_v(it, u, o):
                bank = filled(act, it, f"v{u}{o}")
                nc.scalar.copy(v_sb[u][:, 512 * o:512 * o + 512], bank[:, :]).then_inc(v_done, 1)

            act.wait_ge(raw_in, 64)
            for n in range(4):
                nc.scalar.copy(w_hi[n][:], w_raw[n]).then_inc(w_hi_done, 1)
            for it in turns(act, PAIRS, 1):
                if it.prev:
                    take_turn(it, 3)
                if it.cur:
                    expo(it, 0)
                    take_q(it, 2)
                    take_q(it, 3)
                if it.prev:
                    take_out(it, 3)
                if it.cur:
                    take_turn(it, 0)
                    expo(it, 1)
                    take_out(it, 0)
                if it.nxt:
                    take_in(it, "x", xT_hi_done)
                if it.cur:
                    take_v(it, 0, 1)
                    take_v(it, 1, 1)
                if it.nxt:
                    take_in(it, "c", cT_hi_done)
                if it.cur:
                    take_turn(it, 1)
                    expo(it, 2)
                if it.nxt:
                    take_q(it, 0)
                    take_q(it, 1)
                if it.cur:
                    take_out(it, 1)
                    take_turn(it, 2)
                    expo(it, 3)
                    take_out(it, 2)
                if it.nxt:
                    take_v(it, 0, 0)
                    take_v(it, 1, 0)

        @block.vector
        def _(dve):
            def softmax_in(it, t):
                for half in range(2):
                    i = 2 * (t % 2) + half
                    n = 8 * it.b + (2 * t + half + 1)
                    if half == 0:
                        dve.wait_ge(scores_done, 4 * it.b + (t + 1))
                    nc.vector.tensor_reduce(smax[:, i, :], score_bank[i][:], AX.X, ALU.max).then_inc(smax_done, 1)
                    if t >= 2 or it.kind != "first":
                        dve.wait_ge(pT_done, 8 * it.b + (2 * t + half - 3))
                    dve.wait_ge(smax_done, n)
                    nc.vector.tensor_tensor(p_sb[i][:], score_bank[i][:],
                                            smax[:, i, :].rearrange("p (h o) -> p h o", o=1).to_broadcast([P, 4, P]),
                                            ALU.subtract).then_inc(sub_done, 1)

            def sums(it, t):
                for half in range(2):
                    i = 2 * (t % 2) + half
                    n = 8 * it.b + (2 * t + half + 1)
                    dve.wait_ge(exp_done, n)
                    nc.vector.tensor_reduce(den[:, i, :], p_sb[i][:], AX.X, ALU.add).then_inc(den_done, 1)
                    dve.wait_ge(den_done, n)
                    nc.vector.reciprocal(rden[:, i, :], den[:, i, :]).then_inc(rden_done, 1)

            def take_low(it, name, hi, lo, hi_done, n, done):
                bank = filled(dve, it, name)
                dve.wait_ge(hi_done, n)
                nc.vector.tensor_tensor(lo, bank[:, :], hi.bitcast(F32), ALU.subtract).then_inc(done, 1)

            def take_out(it, t):
                u, o = t % 2, t // 2
                hi, lo = (x[u][:, 4 * o:4 * o + 4, :].rearrange("p a b -> p (a b)") for x in (oT_hi, oT_lo))
                take_low(it, f"AV{t}", hi, lo, oT_hi_done, 4 * it.b + (0 if t == 3 else t + 1), oT_done)

            def take_in(it, n, hi_done, done):
                hi, lo = (t[n][:].rearrange("p k u t -> p (k u t)") for t in (inT_hi, inT_lo))
                take_low(it, f"{n}T", hi, lo, hi_done, it.b + 2, done)

            def take_k(it, j):
                bank = filled(dve, it, f"k{j}")
                nc.vector.tensor_copy(kT[:, 2 * j:2 * j + 2, :].rearrange("p a b -> p (a b)"), bank[:, :]).then_inc(k_done, 1)

            def add_out(it, u):
                bank = filled(dve, it, f"wo{u}")
                xp = x_sb[:, 2 * it.b - 2 + u, :]
                nc.vector.tensor_tensor(xp, xp, bank[:, 0:D], ALU.add).then_inc(x_added, 1)

            for n in range(4):
                dve.wait_ge(w_hi_done, n + 1)
                nc.vector.tensor_tensor(w_lo[n][:], w_raw[n], w_hi[n][:].bitcast(F32), ALU.subtract).then_inc(w_done, 1)
            for it in turns(dve, PAIRS, 1):
                if it.nxt:
                    xb = [x_sb[:, 2 * it.b + 2 + u, :] for u in range(2)]
                    for u in range(2):
                        last = nc.vector.bn_stats(bn6[:, u, :], xb[u])
                    last.then_inc(bn6_done, 1)
                    dve.wait_ge(bn6_done, it.b + 2)
                    dve.sem_inc(bn6_seen, 1)
                    for u in range(2):
                        last = nc.vector.bn_aggr(bn2[:, u, :], bn6[:, u, :])
                    last.then_inc(bn2_done, 1)
                    dve.wait_ge(bn2_done, it.b + 2)
                    nc.vector.tensor_scalar(vpe[:].rearrange("p (u o) -> p u o", o=1), bn2[:, :, 1:2], 1e-5, None,
                                            ALU.add).then_inc(vpe_done, 1)
                if it.cur:
                    softmax_in(it, 0)
                if it.prev:
                    take_out(it, 3)
                if it.cur:
                    sums(it, 0)
                if it.prev:
                    add_out(it, 0)
                if it.nxt:
                    dve.wait_ge(rstd_done, it.b + 2)
                    if it.kind != "pro":
                        dve.wait_ge(xT_hi_done, it.b + 1)
                    for u in range(2):
                        last = nc.vector.tensor_scalar(xn[:, u, :], xb[u], bn2[:, u, 0:1], rstd[:, u:u + 1], ALU.subtract, ALU.mult)
                    last.then_inc(xn_done, 1)
                if it.cur:
                    softmax_in(it, 1)
                    take_k(it, 2)
                    take_k(it, 3)
                    sums(it, 1)
                    take_out(it, 0)
                if it.prev:
                    add_out(it, 1)
                if it.nxt:
                    take_in(it, "x", xT_hi_done, xT_done)
                if it.cur:
                    softmax_in(it, 2)
                if it.nxt:
                    take_in(it, "c", cT_hi_done, cT_done)
                if it.cur:
                    sums(it, 2)
                    take_out(it, 1)
                    softmax_in(it, 3)
                if it.nxt:
                    take_k(it, 0)
                    take_k(it, 1)
                if it.cur:
                    sums(it, 3)
                    take_out(it, 2)

        @block.gpsimd
        def _(pool):
            def normalise(it, t):
                for half in range(2):
                    i = 2 * (t % 2) + half
                    pool.wait_ge(rden_done, 8 * it.b + (2 * t + half + 1))
                    nc.gpsimd.tensor_tensor(p_sb[i][:], p_sb[i][:],
                                            rden[:, i, :].rearrange("p (h o) -> p h o", o=1).to_broadcast([P, 4, P]),
                                            ALU.mult).then_inc(norm_done, 1)

            for it in turns(pool, PAIRS, 1):
                if it.nxt:
                    pool.wait_ge(vpe_done, it.b + 2)
                    nc.gpsimd.tensor_tensor(rstd[:], vpe[:], pow_half[:, 0:2], ALU.pow).then_inc(rstd_done, 1)
                if it.cur:
                    for t in range(4):
                        normalise(it, t)
    return jobs.end


class Plan:

    def __init__(self, banks, filled_sem, before, lo, hi, order, read_by):
        self.banks, self.filled_sem, self.lo, self.hi, self.order, self.read_by = banks, filled_sem, lo, hi, order, read_by
        self.number, self.last = {}, {}
        jobs = []
        for b in range(lo, hi + 1):
            for name in order(b):
                self.number[b, name] = before + len(jobs)
                self.last[b, name] = jobs[-RING] if len(jobs) >= RING else None
                jobs.append((b, name))
        self.end = before + len(jobs)

    def turns(self, eng, *loops):
        b = self.lo
        for first, last, unroll in [*loops, (self.hi + 1, self.hi, 1)]:
            for b in range(b, first):
                yield PlanTurn(self, b)
            b = max(b, first)
            if last >= first:
                assert (last - first + 1) % unroll == 0
                for c in range(first, last + 1):
                    rep = first + (c - first) % unroll
                    for name in self.order(rep):
                        p, q = self.last[rep, name], self.last[c, name]
                        assert p and q and p[1] == q[1] and rep - p[0] == c - q[0]
                        assert (self.number[c, name] - self.number[rep, name]) % RING == 0
                with eng.Fori(0, (last - first + 1) // unroll) as m:
                    for u in range(unroll):
                        yield PlanTurn(self, first + u, m, unroll)
                b = last + 1


class PlanTurn:

    def __init__(self, plan, rep, m=None, unroll=1):
        self.plan, self.rep, self.m, self.unroll = plan, rep, m, unroll

    def at(self, a, c):
        return self.rep * a + c if self.m is None else self.m * (a * self.unroll) + (self.rep * a + c)

    def has(self, name):
        return (self.rep, name) in self.plan.number

    def wait_filled(self, eng, name):
        n = self.plan.number[self.rep, name] + 1
        if self.m is not None:
            n = self.m * (self.unroll * len(self.plan.order(self.rep))) + n
        eng.wait_ge(self.plan.filled_sem, n)

    def filled(self, eng, name):
        self.wait_filled(eng, name)
        return self.plan.banks[self.plan.number[self.rep, name] % RING]

    def start(self, pe, name):
        last = self.plan.last[self.rep, name]
        if last:
            read, a, c = self.plan.read_by[last[1]]
            pe.wait_ge(read, self.at(a, c + a * (last[0] - self.rep)))
        return self.plan.banks[self.plan.number[self.rep, name] % RING]


def experts(nc, sh, raw1, jobs_before, gate_w, w2, raw1_in, xs_dram, xs_cleared, out):
    B, x_sb, ident, pow_half, sem = sh.B, sh.x_sb, sh.ident, sh.pow_half, sh.sem
    ring, ring_filled = sh.ring, sh.ring_filled
    E, F = 8, 512
    KF = F // P
    SEG = 2
    SB = B // SEG
    ST = SB * 2 + E - 1
    NT = SEG * ST
    XG = 4
    CS = 4
    EW = KD * F
    assert EW == KF * D

    ys_dram = [nc.dram_tensor(f"ys_dram{s}", (ST * P, D), F32).ap() for s in range(SEG)]

    with ExitStack() as ctx:
        def sb(name, shape, dt=F32):
            return ctx.enter_context(nc.sbuf_tensor(name, shape, dt))

        w1_lo = sb("w1_lo", [P, E * EW], F32R)
        with nc.sbuf_tensor("raw2", [P, E * EW], F32) as raw2:
            pass
        w2_lo = sb("w2_lo", [P, E * EW], F32R)
        w1_hi = sb("w1_hi", [P, E * EW], F32R)
        w2_hi = sb("w2_hi", [P, E * EW], F32R)
        gate_sb = sb("gate_sb", [P, KD, E])
        bn6 = sb("r_bn6", [P, B, 6])
        mean = sb("r_mean", [P, B])
        diff = sb("r_diff", [P, B])
        var = sb("r_var", [P, B])
        half_col = sb("half_col", [P, B])
        rstd = sb("r_rstd", [P, B])
        shift = sb("r_shift", [P, B])
        with nc.sbuf_tensor("r_xn", [P, 2, 2, D], F32) as xn, nc.sbuf_tensor("r_xnT", [P, 2, 2, D], F32) as xnT:
            pass
        yg = [sb(f"yg{i}", [P, D]) for i in range(2 * CS)]
        logits = sb("logits", [P, B, E])
        rank_e = sb("rank_e", [P, E])
        top = sb("top", [P, 2, B])
        tmp = sb("tmp", [P, B, E])
        first_of = sb("first_of", [P, B])
        hot = [sb(f"hot{k}", [P, B, E]) for k in range(2)]
        hot_b = sb("hot_b", [P, B * E], BF16)
        before_b = sb("before_b", [P, P], BF16)
        ones_b = sb("ones_b", [P, P], BF16)
        pre = [sb(f"pre{i}", [P, SEG, SB, E]) for i in range(2)]
        count = sb("count", [P, SEG, E])
        count_i = sb("count_i", [P, SEG, E], mybir.dt.int32)
        padded = sb("padded", [P, SEG, E])
        begin = sb("begin", [P, SEG, E])
        slot_f = sb("slot_f", [P, 2, B])
        slot = sb("slot", [P, 2, B], mybir.dt.int32)
        share = sb("share", [P, 2, B])
        exp_d = sb("exp_d", [P, B])
        tile_row = sb("tile_row", [1, ST])
        tile_cmp = sb("tile_cmp", [1, ST, E])
        tile_e = sb("tile_e", [1, NT])
        tile_w = sb("tile_w", [1, NT], mybir.dt.int32)
        iota_i = sb("iota_i", [P, ST], mybir.dt.int32)
        send = [sb(f"send{i}", [P, D]) for i in range(2)]
        send_at = [sb(f"send_at{i}", [P, 1], mybir.dt.int32) for i in range(4)]
        xg = [sb(f"xg{i}", [P, D]) for i in range(XG)]
        gT_hi = [sb(f"gT_hi{i}", [P, KD, P], F32R) for i in range(2)]
        gT_lo = [sb(f"gT_lo{i}", [P, KD, P], F32R) for i in range(2)]
        h_sb = [sb(f"h{i}", [P, F]) for i in range(2)]
        hT_hi = [sb(f"hT_hi{i}", [P, KF, P], F32R) for i in range(2)]
        hT_lo = [sb(f"hT_lo{i}", [P, KF, P], F32R) for i in range(2)]
        y_sb = [sb(f"y_out{i}", [P, D]) for i in range(2)]
        take_at = [sb(f"take_at{i}", [P, 1], mybir.dt.int32) for i in range(2 * CS)]

        raw2_in, gate_in = sem("raw2_in"), sem("gate_in")
        w_hi_done, w_done = sem("ew_hi_done"), sem("ew_done")
        const_step, const_done = sem("e_const_step"), sem("e_const_done")
        stats_done, stat_step, var_done, rstd_done = sem("r_stats_done"), sem("r_stat_step"), sem("r_var_done"), sem("r_rstd_done")
        xn_done, xnT_done, logits_done = sem("r_xn_done"), sem("r_xnT_done"), sem("logits_done")
        shift_done = sem("r_shift_done")
        route_step, exp_in, exp_done, hot_done, ranks_done, slots_done, tiles_done = (
            sem(n) for n in ("route_step", "exp_in", "exp_done", "hot_done", "ranks_done", "slots_done", "tiles_done"))
        send_in = sem("send_in")
        send_at_done, scatter_ready, gather_ready = sem("send_at_done"), sem("scatter_ready"), sem("gather_ready")
        sent = [sem(f"sent{i}") for i in range(4)]
        seg_sent = sem("seg_sent")
        xg_in = [sem(f"xg_in{i}") for i in range(XG)]
        gT_hi_done, gT_done, silu_done, hT_hi_done, hT_done, y_done = (
            sem(n) for n in ("gT_hi_done", "gT_done", "silu_done", "hT_hi_done", "hT_done", "y_out_done"))
        y_stored = [sem(f"y_stored{i}") for i in range(2)]
        seg_stored = sem("seg_stored")
        take_at_done = sem("take_at_done")
        taken = [sem(f"taken{i}") for i in range(2 * CS)]
        comb_step, comb_done = sem("comb_step"), sem("comb_done")
        out_sent = [sem(f"out_sent{i}") for i in range(CS)]

        PAIRS = B // 2
        router = Plan(ring, ring_filled, jobs_before, 0, PAIRS + 1,
                      lambda g: ["T"] * (g < PAIRS) + ["L"] * (g > 1),
                      {"T": (xnT_done, 1, 1), "L": (logits_done, 1, -1)})
        router_loop = (4, PAIRS - 1, 2)

        def tile_jobs(j):
            return (["h"] * (0 <= j < NT) + ["hT"] * (0 <= j - 1 < NT) + ["xT"] * (0 <= j + 2 < NT)
                    + ["y"] * (0 <= j - 2 < NT))

        tiles = Plan(ring, ring_filled, router.end + 2, -2, NT + 1, tile_jobs,
                     {"h": (silu_done, 1, 1), "y": (y_done, 1, -1), "hT": (hT_done, 1, 0), "xT": (gT_done, 1, 3)})
        tile_loop_end = 4 + (NT - 6) // 4 * 4 - 1
        send_to = 4 + SB - 1
        comb_from = ST + 3
        assert comb_from % 2 == 0
        comb_to = comb_from + 2 * SB - 1
        assert comb_to <= tile_loop_end

        block = ctx.enter_context(nc.Block())

        @block.sync
        def _(sync):
            sync.dma_start(gate_sb[:], gate_w.rearrange("(k p) n -> p k n", p=P)).then_inc(gate_in, 16)
            sync.dma_start(raw2[:, :].rearrange("p (e k n) -> p e k n", e=E, k=KF),
                           w2.rearrange("e (k p) n -> p e k n", p=P)).then_inc(raw2_in, 16)

            def rows(dram, it, by):
                s = (it.rep + by) // ST
                return dram[s][bass.ts(it.at(1, by - s * ST), P), :]

            def store_out(m, u):
                sync.wait_ge(comb_done, m * CS + (u + 1))
                sync.dma_start(out[m * CS + u], yg[2 * u][:]).then_inc(out_sent[u], 16)

            def store_all(tiles_of_half):
                for u in range(2):
                    sync.wait_ge(y_stored[u], 16 * ((tiles_of_half + 1 - u) // 2))
                sync.sem_inc(seg_stored, 1)

            sync.wait_ge(seg_sent, 1)
            for j in range(XG):
                sync.dma_start(xg[j][:], xs_dram[0][j * P:(j + 1) * P, :]).then_inc(xg_in[j], 16)
            for it in tiles.turns(sync, (4, 4 + (ST - XG - 4) // 4 * 4 - 1, 4), (comb_from, comb_to, 2 * CS)):
                j = it.rep
                if j + XG == ST:
                    sync.wait_ge(seg_sent, 2)
                if 0 <= j and j + XG < NT:
                    sync.wait_ge(gT_hi_done, it.at(1, 1))
                    sync.dma_start(xg[j % XG][:], rows(xs_dram, it, XG)).then_inc(xg_in[j % XG], 16)
                if j >= 2:
                    sync.wait_ge(y_done, it.at(1, -1))
                    sync.dma_start(rows(ys_dram, it, -2), y_sb[j % 2][:]).then_inc(y_stored[j % 2], 16)
                if j == ST + 2:
                    store_all(ST)
                if it.unroll == 2 * CS and j % 2 == 1:
                    store_out(it.m, (j - comb_from) // 2)
            store_all(NT)
            with sync.Fori(SB // CS, B // CS) as m:
                for u in range(CS):
                    store_out(m, u)
            for u in range(CS):
                sync.wait_ge(out_sent[u], 16 * (B // CS))

        @block.tensor
        def _(pe):
            pe.wait_ge(gate_in, 16)
            for it in router.turns(pe, router_loop):
                u = it.rep % 2
                if it.has("T"):
                    bank = it.start(pe, "T")
                    pe.wait_ge(xn_done, it.at(1, 1))
                    for i in range(2):
                        for k in range(KD):
                            last = nc.tensor.transpose(bank[:, i * D + k * P:i * D + (k + 1) * P], xn[:, u, i, k * P:(k + 1) * P], ident[:])
                    last.then_inc(ring_filled, 1)
                if it.has("L"):
                    bank = it.start(pe, "L")
                    pe.wait_ge(xnT_done, it.at(1, -1))
                    for i in range(2):
                        for k in range(KD):
                            last = nc.tensor.matmul(bank[:, i * E:(i + 1) * E], xnT[:, u, i, k * P:(k + 1) * P], gate_sb[:, k, :],
                                                    start=(k == 0), stop=(k == KD - 1))
                    last.then_inc(ring_filled, 1)
            pe.wait_ge(hot_done, 1)
            pe.wait_ge(const_done, 1)
            pe.wait_ge(logits_done, PAIRS)
            nc.tensor.matmul(ring[router.end % RING][:, 0:B * E], before_b[:], hot_b[:], start=True, stop=True).then_inc(ring_filled, 1)
            nc.tensor.matmul(ring[(router.end + 1) % RING][:, 0:B * E], ones_b[:], hot_b[:], start=True, stop=True).then_inc(ring_filled, 1)

            pe.wait_ge(tiles_done, 1)
            pe.wait_ge(slots_done, 1)
            pe.wait_ge(w_done, 4)

            def expert_of(j):
                return pe.value_load(tile_w[0:1, bass.ds(j, 1)], min_val=0, max_val=(E - 1) * EW)

            for it in tiles.turns(pe, (4, tile_loop_end, 4)):
                j, u = it.rep, it.rep % 2
                if it.has("h"):
                    at_h = expert_of(it.at(1, 0))
                if it.has("y"):
                    at_y = expert_of(it.at(1, -2))
                if it.has("h"):
                    bank = it.start(pe, "h")
                    pe.wait_ge(gT_done, it.at(1, 1))
                    for k in range(KD):
                        hi, lo = (w[:, bass.ds(at_h + k * F, F)] for w in (w1_hi, w1_lo))
                        nc.tensor.matmul(bank[:, :], gT_hi[u][:, k, :], lo, start=(k == 0), stop=False)
                        nc.tensor.matmul(bank[:, :], gT_lo[u][:, k, :], hi, start=False, stop=False)
                        last = nc.tensor.matmul(bank[:, :], gT_hi[u][:, k, :], hi, start=False, stop=(k == KD - 1))
                    last.then_inc(ring_filled, 1)
                if it.has("hT"):
                    bank = it.start(pe, "hT")
                    pe.wait_ge(silu_done, it.at(1, 0))
                    for k in range(KF):
                        last = nc.tensor.transpose(bank[:, k * P:(k + 1) * P], h_sb[1 - u][:, k * P:(k + 1) * P], ident[:])
                    last.then_inc(ring_filled, 1)
                if it.has("xT"):
                    bank = it.start(pe, "xT")
                    v = 16 * ((j + 2) // XG + 1)
                    pe.wait_ge(xg_in[(j + 2) % XG], v if it.m is None else it.m * 16 + v)
                    for k in range(KD):
                        last = nc.tensor.transpose(bank[:, k * P:(k + 1) * P], xg[(j + 2) % XG][:, k * P:(k + 1) * P], ident[:])
                    last.then_inc(ring_filled, 1)
                if it.has("y"):
                    bank = it.start(pe, "y")
                    pe.wait_ge(hT_done, it.at(1, -1))
                    for k in range(KF):
                        hi, lo = (w[:, bass.ds(at_y + k * D, D)] for w in (w2_hi, w2_lo))
                        nc.tensor.matmul(bank[:, 0:D], hT_hi[u][:, k, :], lo, start=(k == 0), stop=False)
                        nc.tensor.matmul(bank[:, 0:D], hT_lo[u][:, k, :], hi, start=False, stop=False)
                        last = nc.tensor.matmul(bank[:, 0:D], hT_hi[u][:, k, :], hi, start=False, stop=(k == KF - 1))
                    last.then_inc(ring_filled, 1)

        @block.scalar
        def _(act):
            def split_high(raw, hi):
                for c in range(2):
                    cols = slice(c * 4 * EW, (c + 1) * 4 * EW)
                    nc.scalar.copy(hi[:, cols], raw[:, cols]).then_inc(w_hi_done, 1)

            act.wait_ge(raw1_in, 16)
            split_high(raw1, w1_hi)
            for it in router.turns(act, router_loop):
                if it.has("T"):
                    bank = it.filled(act, "T")
                    if it.rep >= 2:
                        it.wait_filled(act, "L")
                    nc.scalar.copy(xnT[:, it.rep % 2, :, :].rearrange("p i d -> p (i d)"), bank[:, :]).then_inc(xnT_done, 1)
            act.wait_ge(raw2_in, 16)
            split_high(raw2, w2_hi)
            act.wait_ge(exp_in, 1)
            nc.scalar.activation(exp_d[:], exp_d[:], ACT.Exp).then_inc(exp_done, 1)

            def normalise(b, u, sends):
                if sends is not None:
                    act.wait_ge(sent[2 * u], sends)
                    act.wait_ge(sent[2 * u + 1], sends)
                nc.scalar.activation(send[u][:], x_sb[:, b, :], ACT.Identity, bias=shift[:, bass.ds(b, 1)],
                                     scale=rstd[:, bass.ds(b, 1)]).then_inc(send_in, 1)

            act.wait_ge(shift_done, 1)
            for u in range(2):
                normalise(u, u, None)
            with act.Fori(1, SB // 2) as m:
                for u in range(2):
                    normalise(m * 2 + u, u, m * 16)

            for it in tiles.turns(act, (4, send_to, 2), (send_to + 1, tile_loop_end, 2)):
                u = it.rep % 2
                if it.has("h"):
                    bank = it.filled(act, "h")
                    if it.rep >= 2:
                        PlanTurn(tiles, it.rep - 1, it.m, it.unroll).wait_filled(act, "hT")
                    nc.scalar.activation(h_sb[u][:], bank[:, :], ACT.Silu).then_inc(silu_done, 1)
                if it.has("hT"):
                    bank = it.filled(act, "hT")
                    if it.rep >= 3:
                        PlanTurn(tiles, it.rep - 1, it.m, it.unroll).wait_filled(act, "y")
                    nc.scalar.copy(hT_hi[1 - u][:].rearrange("p k t -> p (k t)"), bank[:, :]).then_inc(hT_hi_done, 1)
                if it.has("xT"):
                    bank = it.filled(act, "xT")
                    nc.scalar.copy(gT_hi[u][:].rearrange("p k t -> p (k t)"), bank[:, 0:D]).then_inc(gT_hi_done, 1)
                if it.has("y"):
                    bank = it.filled(act, "y")
                    if it.rep >= 4:
                        v = 16 * (it.rep // 2 - 1)
                        act.wait_ge(y_stored[u], v if it.m is None else it.m * (it.unroll * 8) + v)
                    nc.scalar.copy(y_sb[u][:], bank[:, 0:D]).then_inc(y_done, 1)
                if it.m is not None and it.rep <= send_to:
                    normalise(it.m * 2 + (SB + u), u, it.m * 16 + SB * 8)

        @block.vector
        def _(dve):
            step = [0]

            def link(ins):
                step[0] += 1
                ins.then_inc(route_step, 1)
                dve.wait_ge(route_step, step[0])

            def spread(ap, n):
                return ap.rearrange("p (m o) -> p m o", o=1).to_broadcast([ap.shape[0], ap.shape[1], n])

            with dve.Fori(0, B // 4) as m:
                for u in range(4):
                    last = nc.vector.bn_stats(bn6[:, m * 4 + u, :], x_sb[:, m * 4 + u, :])
                last.then_inc(stats_done, 1)
            dve.wait_ge(stats_done, B // 4)
            col = lambda c: bn6[:, :, c:c + 1].rearrange("p b o -> p (b o)")
            nc.vector.tensor_tensor(diff[:], col(1), col(4), ALU.subtract).then_inc(stat_step, 1)
            nc.vector.tensor_tensor(mean[:], col(1), col(4), ALU.add).then_inc(stat_step, 1)
            nc.vector.tensor_tensor(var[:], col(2), col(5), ALU.add).then_inc(stat_step, 1)
            dve.wait_ge(stat_step, 3)
            nc.vector.tensor_tensor(diff[:], diff[:], diff[:], ALU.mult).then_inc(stat_step, 1)
            nc.vector.tensor_scalar(mean[:], mean[:], 0.5, None, ALU.mult).then_inc(stat_step, 1)
            nc.vector.tensor_scalar(var[:], var[:], 1.0 / D, 1e-5, ALU.mult, ALU.add).then_inc(stat_step, 1)
            dve.wait_ge(stat_step, 6)
            nc.vector.scalar_tensor_tensor(out=var[:], in0=diff[:], scalar=0.25, in1=var[:], op0=ALU.mult,
                                           op1=ALU.add).then_inc(var_done, 1)
            dve.wait_ge(rstd_done, 1)
            nc.vector.scalar_tensor_tensor(out=shift[:], in0=mean[:], scalar=-1.0, in1=rstd[:], op0=ALU.mult,
                                           op1=ALU.mult).then_inc(shift_done, 1)

            def take_logits(it):
                bank = it.filled(dve, "L")
                nc.vector.tensor_copy(logits[:, bass.ds(it.at(2, -4), 2), :],
                                      bank[:, 0:2 * E].rearrange("p (i e) -> p i e", e=E)).then_inc(logits_done, 1)

            for it in router.turns(dve, router_loop):
                u = it.rep % 2
                if it.has("T"):
                    if it.rep >= 2:
                        PlanTurn(router, it.rep - 2, it.m, it.unroll).wait_filled(dve, "T")
                    for i in range(2):
                        b = it.at(2, i)
                        last = nc.vector.tensor_scalar(xn[:, u, i, :], x_sb[:, b, :], mean[:, bass.ds(b, 1)],
                                                       rstd[:, bass.ds(b, 1)], ALU.subtract, ALU.mult)
                    last.then_inc(xn_done, 1)
                before = PlanTurn(router, it.rep - 1, it.m, it.unroll)
                if before.has("L"):
                    take_logits(before)
                if it.rep == router.hi:
                    take_logits(it)

            dve.wait_ge(logits_done, PAIRS)
            dve.wait_ge(const_done, 1)
            flat = lambda t: t[:].rearrange("p b e -> p (b e)")
            left = logits
            for k in range(2):
                link(nc.vector.tensor_reduce(top[:, k, :], left[:], AX.X, ALU.max))
                link(nc.vector.tensor_tensor(tmp[:], left[:], spread(top[:, k, :], E), ALU.is_equal))
                link(nc.vector.tensor_tensor(tmp[:], tmp[:], rank_e[:].rearrange("p (o e) -> p o e", o=1).to_broadcast([P, B, E]),
                                             ALU.mult))
                link(nc.vector.tensor_reduce(first_of[:], tmp[:], AX.X, ALU.max))
                link(nc.vector.tensor_tensor(hot[k][:], tmp[:], spread(first_of[:], E), ALU.is_equal))
                if k == 0:
                    link(nc.vector.scalar_tensor_tensor(out=flat(logits), in0=flat(hot[0]), scalar=-3e38, in1=flat(logits),
                                                        op0=ALU.mult, op1=ALU.add))
            nc.vector.tensor_tensor(hot_b[:], flat(hot[0]), flat(hot[1]), ALU.add).then_inc(hot_done, 1)
            nc.vector.tensor_tensor(exp_d[:], top[:, 1, :], top[:, 0, :], ALU.subtract).then_inc(exp_in, 1)

            n = router.end
            rank, total = (ring[(n + i) % RING][:, 0:B * E].rearrange("p (s b e) -> p s b e", s=SEG, e=E) for i in range(2))
            dve.wait_ge(ring_filled, n + 2)
            nc.vector.memset(pre[0][:, :, 0:1, :], 0.0)
            for s in range(SEG):
                last = nc.vector.tensor_copy(pre[0][:, s, 1:SB, :], total[:, s, 0:SB - 1, :])
            link(last)
            src, dst, by = pre[0], pre[1], 1
            while by < SB:
                for s in range(SEG):
                    nc.vector.tensor_copy(dst[:, s, 0:by, :], src[:, s, 0:by, :])
                    last = nc.vector.tensor_tensor(dst[:, s, by:SB, :], src[:, s, by:SB, :], src[:, s, 0:SB - by, :], ALU.add)
                link(last)
                src, dst, by = dst, src, 2 * by
            link(nc.vector.tensor_tensor(count[:], src[:, :, SB - 1, :], total[:, :, SB - 1, :], ALU.add))
            link(nc.vector.tensor_scalar(count_i[:], count[:], float(P - 1), None, ALU.add))
            link(nc.vector.tensor_scalar(count_i[:], count_i[:], 7, 7, ALU.logical_shift_right, ALU.logical_shift_left))
            link(nc.vector.tensor_copy(padded[:], count_i[:]))
            for s in range(SEG):
                last = nc.vector.memset(begin[:, s, 0:1], 0.0)
            link(last)
            for e in range(1, E):
                link(nc.vector.tensor_tensor(begin[:, :, e:e + 1], begin[:, :, e - 1:e], padded[:, :, e - 1:e], ALU.add))
            link(nc.vector.tensor_tensor(dst[:], rank, src[:], ALU.add))
            for s in range(SEG):
                last = nc.vector.tensor_tensor(dst[:, s, :, :], dst[:, s, :, :],
                                               begin[:, s, :].rearrange("p (o e) -> p o e", o=1).to_broadcast([P, SB, E]), ALU.add)
            link(last)
            at_slot = dst[:].rearrange("p s b e -> p (s b) e")
            for k in range(2):
                link(nc.vector.tensor_tensor(tmp[:], hot[k][:], at_slot, ALU.mult))
                link(nc.vector.tensor_reduce(slot_f[:, k, :], tmp[:], AX.X, ALU.add))
            nc.vector.tensor_copy(slot[:], slot_f[:]).then_inc(slots_done, 1)
            for s in range(SEG):
                link(nc.vector.tensor_tensor(tile_cmp[:], begin[0:1, s, :].rearrange("p (o e) -> p o e", o=1).to_broadcast([1, ST, E]),
                                             spread(tile_row[:], E), ALU.is_le))
                link(nc.vector.tensor_reduce(tile_e[:, s * ST:(s + 1) * ST], tile_cmp[:], AX.X, ALU.add))
            nc.vector.tensor_scalar(tile_w[:], tile_e[:], float(EW), float(-EW), ALU.mult, ALU.add).then_inc(tiles_done, 1)
            dve.wait_ge(exp_done, 1)
            link(nc.vector.tensor_scalar(first_of[:], exp_d[:], 1.0, None, ALU.add))
            link(nc.vector.reciprocal(share[:, 0, :], first_of[:]))
            link(nc.vector.tensor_tensor(share[:, 1, :], exp_d[:], share[:, 0, :], ALU.mult))
            for i, (raw, hi, lo) in enumerate(((raw1, w1_hi, w1_lo), (raw2, w2_hi, w2_lo))):
                for c in range(2):
                    cols = slice(c * 4 * EW, (c + 1) * 4 * EW)
                    dve.wait_ge(w_hi_done, 2 * i + c + 1)
                    nc.vector.tensor_tensor(lo[:, cols], raw[:, cols], hi[:, cols].bitcast(F32), ALU.subtract).then_inc(w_done, 1)

            def combine(m, u):
                b = m * CS + u
                for k in range(2):
                    dve.wait_ge(taken[2 * u + k], m * 16 + 16)
                col = lambda k: share[:, k, bass.ds(b, 1)]
                nc.vector.scalar_tensor_tensor(out=yg[2 * u][:], in0=yg[2 * u][:], scalar=col(0), in1=x_sb[:, b, :], op0=ALU.mult,
                                               op1=ALU.add).then_inc(comb_step, 1)
                dve.wait_ge(comb_step, b + 1)
                nc.vector.scalar_tensor_tensor(out=yg[2 * u][:], in0=yg[2 * u + 1][:], scalar=col(1), in1=yg[2 * u][:],
                                               op0=ALU.mult, op1=ALU.add).then_inc(comb_done, 1)

            def low_halves(it):
                u = it.rep % 2
                if it.has("hT"):
                    bank = it.filled(dve, "hT")
                    dve.wait_ge(hT_hi_done, it.at(1, 0))
                    nc.vector.tensor_tensor(hT_lo[1 - u][:].rearrange("p k t -> p (k t)"), bank[:, :],
                                            hT_hi[1 - u][:].bitcast(F32).rearrange("p k t -> p (k t)"), ALU.subtract).then_inc(hT_done, 1)
                if it.has("xT"):
                    bank = it.filled(dve, "xT")
                    dve.wait_ge(gT_hi_done, it.at(1, 3))
                    nc.vector.tensor_tensor(gT_lo[u][:].rearrange("p k t -> p (k t)"), bank[:, 0:D],
                                            gT_hi[u][:].bitcast(F32).rearrange("p k t -> p (k t)"), ALU.subtract).then_inc(gT_done, 1)

            for it in tiles.turns(dve, (4, comb_from - 1, 2), (comb_from, comb_to, 2 * CS)):
                low_halves(it)
                if it.unroll == 2 * CS and it.rep % 2 == 1:
                    combine(it.m, (it.rep - comb_from) // 2)
            with dve.Fori(SB // CS, B // CS) as m:
                for u in range(CS):
                    combine(m, u)

        @block.gpsimd
        def _(pool):
            nc.gpsimd.memset(half_col[:], -0.5).then_inc(const_step, 1)
            nc.gpsimd.memset(ones_b[:], 1.0).then_inc(const_step, 1)
            nc.gpsimd.memset(before_b[:], 1.0).then_inc(const_step, 1)
            nc.gpsimd.iota(iota_i[:], [[P, ST]], base=0, channel_multiplier=0).then_inc(const_step, 1)
            pool.wait_ge(const_step, 4)
            nc.gpsimd.affine_select(out=before_b[:], in_=before_b[:], compare_op=ALU.is_ge, fill=0.0, base=-1,
                                    pattern=[[1, P]], channel_multiplier=-1).then_inc(const_step, 1)
            nc.gpsimd.tensor_copy(tile_row[:], iota_i[0:1, :]).then_inc(const_step, 1)
            pool.wait_ge(const_step, 6)
            nc.gpsimd.iota(iota_i[:, 0:E], [[-1, E]], base=E, channel_multiplier=0).then_inc(const_step, 1)
            pool.wait_ge(const_step, 7)
            nc.gpsimd.tensor_copy(rank_e[:], iota_i[:, 0:E]).then_inc(const_step, 1)
            pool.wait_ge(var_done, 1)
            nc.gpsimd.tensor_tensor(rstd[:], var[:], half_col[:], ALU.pow).then_inc(rstd_done, 1)
            pool.wait_ge(const_step, 8)
            pool.sem_inc(const_done, 1)

            def scatter(m, waits, dst):
                for u in range(2):
                    for k in range(2):
                        i = 2 * u + k
                        if waits:
                            pool.wait_ge(sent[i], m * 16)
                        nc.gpsimd.tensor_copy(send_at[i][:], slot[:, k, bass.ds(m * 2 + u, 1)]).then_inc(send_at_done, 1)
                for u in range(2):
                    pool.wait_ge(send_at_done, m * 4 + 4)
                    pool.wait_ge(send_in, m * 2 + (u + 1))
                    pool.sem_inc(scatter_ready, 1)
                    for k in range(2):
                        i = 2 * u + k
                        pool.indirect_dma_start(out=dst, out_offset=bass.IndirectOffsetOnAxis(ap=send_at[i][:, 0:1], axis=0),
                                                in_=send[u][:], in_offset=None).then_inc(sent[i], 16)

            pool.wait_ge(slots_done, 1)
            pool.wait_ge(xs_cleared, 32)
            scatter(0, False, xs_dram[0])
            with pool.Fori(1, SB // 2) as m:
                scatter(m, True, xs_dram[0])
            for i in range(4):
                pool.wait_ge(sent[i], 16 * (SB // 2))
            pool.sem_inc(seg_sent, 1)
            with pool.Fori(SB // 2, B // 2) as m:
                scatter(m, True, xs_dram[1])
            for i in range(4):
                pool.wait_ge(sent[i], 16 * (B // 2))
            pool.sem_inc(seg_sent, 1)

            def gather(m, waits, src):
                for u in range(CS):
                    if waits:
                        pool.wait_ge(out_sent[u], m * 16)
                    for k in range(2):
                        nc.gpsimd.tensor_copy(take_at[2 * u + k][:], slot[:, k, bass.ds(m * CS + u, 1)]).then_inc(take_at_done, 1)
                    pool.wait_ge(take_at_done, m * (2 * CS) + (2 * u + 2))
                    pool.sem_inc(gather_ready, 1)
                    for k in range(2):
                        i = 2 * u + k
                        pool.indirect_dma_start(out=yg[i][:], out_offset=None, in_=src,
                                                in_offset=bass.IndirectOffsetOnAxis(ap=take_at[i][:, 0:1], axis=0)).then_inc(taken[i], 16)

            pool.wait_ge(seg_stored, 1)
            gather(0, False, ys_dram[0])
            with pool.Fori(1, SB // CS) as m:
                gather(m, True, ys_dram[0])
            pool.wait_ge(seg_stored, 2)
            with pool.Fori(SB // CS, B // CS) as m:
                gather(m, True, ys_dram[1])


def bass_decoder_layer(nc, x, ctx_x, w_attn, w_proj, ln_w2, rope_cos, rope_sin, w_q, w_k, w_v, w_o, gate_w, w1, w2, out):
    B = x.shape[0]
    with ExitStack() as ctx:
        sh = Shared(nc, ctx, B)
        cross_raw_in, w1_in, xs_cleared = (sh.sem(n) for n in ("cross_raw_in", "w1_in", "xs_cleared"))
        xs_dram = [nc.dram_tensor(f"xs_dram{s}", ((B + 7) * P, D), F32).ap() for s in range(2)]
        with nc.sbuf_tensor("raw", [P, 8192], F32) as sh.raw:
            done = self_attention(nc, sh, x, w_attn, w_proj, ln_w2, rope_cos, rope_sin, (w_q, w_k, w_v, w_o), cross_raw_in,
                                  xs_dram, xs_cleared)
            done = cross_attention(nc, sh, done, ctx_x, cross_raw_in, w1, w1_in)
        experts(nc, sh, sh.raw, done, gate_w, w2, w1_in, xs_dram, xs_cleared, out)


def kernel(**inputs):
    import numpy as _np
    import concourse.bacc as _bacc
    from concourse import mybir as _mybir
    from concourse.bass_utils import run_bass_kernel_spmd as _run

    half_dims = _np.concatenate([_np.arange(0, HD, 2), _np.arange(1, HD, 2)])
    q_heads = [h + half for o in range(2) for k in range(4) for h in (2 * k + o,) for half in (0, 8)]
    k_heads = [k + half for k in range(4) for half in (0, 4)]
    cols = [h * HD + half_dims for h in q_heads] + [NQ * HD + h * HD + half_dims for h in k_heads]
    cols += [_np.arange((NQ + NKV) * HD, (NQ + 2 * NKV) * HD + 8)]
    cols = _np.concatenate(cols)
    slots = [8 * half + 2 * k + o for o in range(2) for half in range(2) for k in range(4)]
    rows = _np.concatenate([h * HD + _np.arange(HD) for h in slots])
    T = 128
    div = 2.0 * _np.pi / float(T) ** (_np.arange(0, HD, 2, dtype=_np.float32) / HD)
    ang = _np.arange(T, dtype=_np.float32)[:, None] * div.astype(_np.float32)[None, :]
    cos = _np.cos(ang.astype(_np.float64)).astype(_np.float32)
    sin = _np.sin(ang.astype(_np.float64)).astype(_np.float32)
    arrays = {
        "x": _np.ascontiguousarray(inputs["x"]),
        "ctx": _np.ascontiguousarray(inputs["ctx_1024"]),
        "w_attn": _np.ascontiguousarray(_np.asarray(inputs["L0_attn_w_attn"])[:, cols]),
        "w_proj": _np.ascontiguousarray(_np.asarray(inputs["L0_attn_w_proj"])[rows]),
        "ln_w2": _np.ascontiguousarray(_np.tile(_np.asarray(inputs["L0_attn_ln_w"]), 2).reshape(P, 1)),
        "rope_cos": _np.concatenate([cos, cos], axis=1),
        "rope_sin": _np.concatenate([-sin, sin], axis=1),
        **{n: _np.ascontiguousarray(inputs[f"L0_xattn_{n}"]) for n in ("w_q", "w_k", "w_v", "w_o")},
        **{n: _np.ascontiguousarray(inputs[f"L0_ffn_{n}"]) for n in ("gate_w", "w1", "w2")},
    }
    nc = _bacc.Bacc("TRN2", target_bir_lowering=False, num_devices=1)
    args = [nc.dram_tensor(f"in_{n}", a.shape, _mybir.dt.from_np(a.dtype), kind="ExternalInput").ap() for n, a in arrays.items()]
    out = nc.dram_tensor("out_0", (32, 128, 256), F32, kind="ExternalOutput").ap()
    bass_decoder_layer(nc, *args, out)
    r = _run(nc, [{f"in_{n}": a for n, a in arrays.items()}], core_ids=[0])
    return r.results[0]["out_0"]
```

```python
from contextlib import ExitStack

import concourse.bass as bass
import numpy as np
from concourse import mybir

ALU = mybir.AluOpType
ACT = mybir.ActivationFunctionType
AX = mybir.AxisListType
F32 = mybir.dt.float32
F32R = mybir.dt.float32r
BF16 = mybir.dt.bfloat16

P = 128
F = 512
D = 256
KD = D // P
EW = KD * F
HD = 64
NQ, NKV = 16, 8
E = 8
CS = 4
RING = 4


class Ring:

    def __init__(self, banks, filled_sem, orders, read_by, before, mids, unroll):
        self.banks, self.filled_sem, self.orders, self.read_by = banks, filled_sem, orders, read_by
        self.base, self.step = {}, unroll * len(orders["mid"])
        assert self.step % RING == 0 and orders["first"][-RING:] == orders["mid"][-RING:]
        n = before
        for kind, count in (("pro", 1), ("first", 1), ("mid", mids), ("last", 1), ("tail", 1)):
            self.base[kind] = n
            n += len(orders[kind]) * count
        self.end = n

    def number(self, it, name):
        return self.base[it.kind] + self.orders[it.kind].index(name) + it.u * len(self.orders[it.kind])

    def start(self, pe, it, name):
        kind, b, at = it.kind, it.b, self.orders[it.kind].index(name) - RING
        while at < 0 and kind != "pro":
            kind, b = {"first": "pro", "mid": "mid", "last": "mid", "tail": "last"}[kind], b - 1
            at += len(self.orders[kind])
        if at >= 0:
            read, a, c = self.read_by[self.orders[kind][at]]
            pe.wait_ge(read, b * a + c)
        return self.banks[self.number(it, name) % RING]

    def wait_filled(self, eng, it, name):
        n = self.number(it, name) + 1
        eng.wait_ge(self.filled_sem, n if it.m is None else it.m * self.step + n)

    def filled(self, eng, it, name):
        self.wait_filled(eng, it, name)
        return self.banks[self.number(it, name) % RING]


class Turn:

    def __init__(self, kind, b, u=0, m=None, unroll=1):
        self.kind, self.b, self.u, self.m = kind, b, u, m
        self.par = b % 2 if m is None else (1 + u) % 2
        self.cur = kind in ("first", "mid", "last")
        self.nxt = kind in ("pro", "first", "mid")
        self.prev = kind in ("mid", "last", "tail")


def turns(eng, n, unroll, peel=0, late=0):
    yield Turn("pro", -1)
    yield Turn("first", 0)
    for u in range(peel):
        yield Turn("mid", 1 + u, u)
    with eng.Fori(0, (n - 2 - peel - late) // unroll) as m:
        for u in range(peel, peel + unroll):
            yield Turn("mid", m * unroll + (1 + u), u, m)
    for u in range(n - 2 - late, n - 2):
        yield Turn("mid", 1 + u, u)
    yield Turn("last", n - 1)
    yield Turn("tail", n)


class Shared:

    def __init__(self, nc, ctx, B):
        def sb(name, shape, dt=F32):
            return ctx.enter_context(nc.sbuf_tensor(name, shape, dt))

        self.B = B
        self.sem = lambda name: ctx.enter_context(nc.semaphore(name))
        self.ring = [ctx.enter_context(nc.psum_tensor(f"ring{i}", [P, 512], F32)) for i in range(RING)]
        self.score_bank = [ctx.enter_context(nc.psum_tensor(f"score{i}", [P, 4, P], F32)) for i in range(4)]
        self.ring_filled = self.sem("ring_filled")
        self.sort_sems = [self.sem(f"sort_{n}") for n in ("const_step", "const_done", "step_done", "hot_done", "slots_done",
                                                          "tiles_done")]
        self.sort_steps = 0
        self.x_sb = sb("x_sb", [P, B, D])
        self.ident = sb("ident", [P, P])
        self.pow_half = sb("pow_half", [P, B])
        self.e_rstd = sb("e_rstd", [P, B])
        self.e_shift = sb("e_shift", [P, B])
        self.logits = sb("logits", [P, B, E])
        self.top = sb("top", [P, 2, B])
        self.slot = sb("slot", [P, 2, B + CS], mybir.dt.int32)
        self.seqs = [5 * B // 8, 3 * B // 8]
        self.first_seq = [0, self.seqs[0]]
        self.tiles = [2 * n + E - 1 for n in self.seqs]
        self.first_tile = [0, self.tiles[0]]
        self.tile_w = sb("tile_w", [1, sum(self.tiles)], mybir.dt.int32)


class Sorting:

    def __init__(self, nc, sh, ctx, s):
        def sb(name, shape, dt=F32):
            return ctx.enter_context(nc.sbuf_tensor(f"sort{s}_{name}", shape, dt))

        self.nc, self.sh, self.s, self.SB, self.ST = nc, sh, s, sh.seqs[s], sh.tiles[s]
        SB, ST = self.SB, self.ST
        self.seqs = slice(sh.first_seq[s], sh.first_seq[s] + SB)
        self.logits = sh.logits[:, self.seqs, :]
        self.rank_e = sb("rank_e", [P, E])
        work = sb("work", [P, 3 * SB * E])
        self.tmp, *self.pre = (work[:, i * SB * E:(i + 1) * SB * E].rearrange("p (b e) -> p b e", e=E) for i in range(3))
        self.first_of = sb("first_of", [P, SB])
        self.hot = [sb(f"hot{k}", [P, SB, E]) for k in range(2)]
        self.hot_b = sb("hot_b", [P, SB * E], BF16)
        self.before_b = sb("before_b", [P, P], BF16)
        self.ones_b = sb("ones_b", [P, P], BF16)
        self.counts = sb("counts", [P, 2, SB, E])
        self.count_i = sb("count_i", [P, E], mybir.dt.int32)
        self.padded = sb("padded", [P, E])
        self.begin = sb("begin", [P, E])
        self.slot_f = sb("slot_f", [P, 2, SB])
        self.tile_row = sb("tile_row", [1, ST])
        self.tile_cmp = work[0:1, 0:ST * E].rearrange("p (b e) -> p b e", e=E)
        self.tile_e = sb("tile_e", [1, ST])
        self.iota_i = sb("iota_i", [P, ST], mybir.dt.int32)
        self.const_step, self.const_done, self.step_done, self.hot_done, self.slots_done, self.tiles_done = sh.sort_sems
        self.done = s + 1

    def link(self, dve, ins):
        self.sh.sort_steps += 1
        ins.then_inc(self.step_done, 1)
        dve.wait_ge(self.step_done, self.sh.sort_steps)

    @staticmethod
    def spread(ap, n):
        return ap.rearrange("p (m o) -> p m o", o=1).to_broadcast([ap.shape[0], ap.shape[1], n])

    @staticmethod
    def repeat(ap, n):
        return ap.rearrange("p (o m) -> p o m", o=1).to_broadcast([ap.shape[0], n, ap.shape[1]])

    def constants(self, pool):
        nc, step = self.nc, self.const_step
        nc.gpsimd.memset(self.ones_b[:], 1.0).then_inc(step, 1)
        nc.gpsimd.memset(self.before_b[:], 1.0).then_inc(step, 1)
        nc.gpsimd.iota(self.iota_i[:], [[P, self.ST]], base=0, channel_multiplier=0).then_inc(step, 1)
        pool.wait_ge(step, 7 * self.s + 3)
        nc.gpsimd.affine_select(out=self.before_b[:], in_=self.before_b[:], compare_op=ALU.is_ge, fill=0.0, base=-1,
                                pattern=[[1, P]], channel_multiplier=-1).then_inc(step, 1)
        nc.gpsimd.tensor_copy(self.tile_row[:], self.iota_i[0:1, :]).then_inc(step, 1)
        pool.wait_ge(step, 7 * self.s + 5)
        nc.gpsimd.iota(self.iota_i[:, 0:E], [[-1, E]], base=E, channel_multiplier=0).then_inc(step, 1)
        pool.wait_ge(step, 7 * self.s + 6)
        nc.gpsimd.tensor_copy(self.rank_e[:], self.iota_i[:, 0:E]).then_inc(step, 1)
        pool.wait_ge(step, 7 * self.s + 7)
        pool.sem_inc(self.const_done, 1)

    def choose(self, dve):
        nc, left, tmp, SB = self.nc, self.logits, self.tmp, self.SB
        dve.wait_ge(self.const_done, self.done)
        for k in range(2):
            top = self.sh.top[:, k, self.seqs]
            self.link(dve, nc.vector.tensor_reduce(top, left, AX.X, ALU.max))
            self.link(dve, nc.vector.tensor_tensor(tmp, left, self.spread(top, E), ALU.is_equal))
            self.link(dve, nc.vector.tensor_tensor(tmp, tmp, self.repeat(self.rank_e[:], SB), ALU.mult))
            self.link(dve, nc.vector.tensor_reduce(self.first_of[:], tmp, AX.X, ALU.max))
            self.link(dve, nc.vector.tensor_tensor(self.hot[k][:], tmp, self.spread(self.first_of[:], E), ALU.is_equal))
            if k == 0:
                self.link(dve, nc.vector.scalar_tensor_tensor(out=left, in0=self.hot[0][:], scalar=-3e38, in1=left,
                                                              op0=ALU.mult, op1=ALU.add))
        nc.vector.tensor_tensor(self.hot_b[:].rearrange("p (b e) -> p b e", e=E), self.hot[0][:], self.hot[1][:],
                                ALU.add).then_inc(self.hot_done, 1)

    def banks(self, bank):
        n = self.SB * E
        return bank[:, 2 * E:2 * E + n], bank[:, 4 * E + n:4 * E + 2 * n]

    def count(self, pe, bank):
        pe.wait_ge(self.hot_done, self.done)
        for out, weights in zip(self.banks(bank), (self.before_b, self.ones_b)):
            last = self.nc.tensor.matmul(out, weights[:], self.hot_b[:], start=True, stop=True)
        return last

    def take_counts(self, dve, bank):
        for i, src in enumerate(self.banks(bank)):
            last = self.nc.vector.tensor_copy(self.counts[:, i, :, :].rearrange("p b e -> p (b e)"), src)
        self.link(dve, last)

    def add_up(self, dve):
        nc, SB, total = self.nc, self.SB, self.counts[:, 1]
        nc.vector.memset(self.pre[0][:, 0:1, :], 0.0)
        self.link(dve, nc.vector.tensor_copy(self.pre[0][:, 1:SB, :], total[:, 0:SB - 1, :]))
        src, dst, by = self.pre[0], self.pre[1], 1
        while by < SB:
            nc.vector.tensor_copy(dst[:, 0:by, :], src[:, 0:by, :])
            self.link(dve, nc.vector.tensor_tensor(dst[:, by:SB, :], src[:, by:SB, :], src[:, 0:SB - by, :], ALU.add))
            src, dst, by = dst, src, 2 * by
        self.before, self.free = src, dst

    def place(self, dve):
        nc, SB, ST, begin, padded, count_i = self.nc, self.SB, self.ST, self.begin, self.padded, self.count_i
        self.link(dve, nc.vector.tensor_tensor(padded[:], self.before[:, SB - 1, :], self.counts[:, 1, SB - 1, :], ALU.add))
        self.link(dve, nc.vector.tensor_scalar(count_i[:], padded[:], float(P - 1), None, ALU.add))
        self.link(dve, nc.vector.tensor_scalar(count_i[:], count_i[:], 7, 7, ALU.logical_shift_right, ALU.logical_shift_left))
        self.link(dve, nc.vector.tensor_copy(padded[:], count_i[:]))
        self.link(dve, nc.vector.memset(begin[:, 0:1], 0.0))
        for e in range(1, E):
            self.link(dve, nc.vector.tensor_tensor(begin[:, e:e + 1], begin[:, e - 1:e], padded[:, e - 1:e], ALU.add))
        at = self.free
        self.link(dve, nc.vector.tensor_tensor(at, self.counts[:, 0], self.before, ALU.add))
        self.link(dve, nc.vector.tensor_tensor(at, at, self.repeat(begin[:], SB), ALU.add))
        for k in range(2):
            self.link(dve, nc.vector.tensor_tensor(self.tmp, self.hot[k][:], at, ALU.mult))
            self.link(dve, nc.vector.tensor_reduce(self.slot_f[:, k, :], self.tmp, AX.X, ALU.add))
        nc.vector.tensor_copy(self.sh.slot[:, :, self.seqs], self.slot_f[:]).then_inc(self.slots_done, 1)
        self.link(dve, nc.vector.tensor_tensor(self.tile_cmp, self.repeat(begin[0:1, :], ST), self.spread(self.tile_row[:], E),
                                               ALU.is_le))
        self.link(dve, nc.vector.tensor_reduce(self.tile_e[:], self.tile_cmp, AX.X, ALU.add))
        first = self.sh.first_tile[self.s]
        nc.vector.tensor_scalar(self.sh.tile_w[:, first:first + ST], self.tile_e[:], float(EW), float(-EW), ALU.mult,
                                ALU.add).then_inc(self.tiles_done, 1)


class Dispatch:

    def __init__(self, nc, sh, ctx, name, buffers):
        self.nc, self.sh, self.buffers = nc, sh, buffers
        self.send = [ctx.enter_context(nc.sbuf_tensor(f"{name}_send{i}", [P, D], F32)) for i in range(buffers)]
        self.send_at = [ctx.enter_context(nc.sbuf_tensor(f"{name}_send_at{i}", [P, 2, 1], mybir.dt.int32)) for i in range(buffers)]
        self.send_in, self.scatter_ready = sh.sem(f"{name}_send_in"), sh.sem(f"{name}_scatter_ready")
        self.sent = [sh.sem(f"{name}_sent{i}") for i in range(2 * buffers)]

    def lay_out(self, act, b, u, sends):
        nc, sh, col = self.nc, self.sh, bass.ds(b, 1)
        if sends is not None:
            act.wait_ge(self.sent[2 * u], sends)
            act.wait_ge(self.sent[2 * u + 1], sends)
        nc.scalar.activation(self.send[u][:], sh.x_sb[:, b, :], ACT.Identity, bias=sh.e_shift[:, col], scale=sh.e_rstd[:, col])
        nc.scalar.copy(self.send_at[u][:], sh.slot[:, :, col]).then_inc(self.send_in, 1)

    def scatter(self, pool, n, u, dst):
        pool.wait_ge(self.send_in, n)
        pool.sem_inc(self.scatter_ready, 1)
        for k in range(2):
            pool.indirect_dma_start(out=dst, out_offset=bass.IndirectOffsetOnAxis(ap=self.send_at[u][:, k, 0:1], axis=0),
                                    in_=self.send[u][:], in_offset=None).then_inc(self.sent[2 * u + k], 16)

    def finish(self, pool, sequences):
        for sent in self.sent:
            pool.wait_ge(sent, 16 * (sequences // self.buffers))


def self_attention(nc, sh, x, w_attn, w_proj, ln_w2, rope_cos, rope_sin, cross_weights, cross_raw_in, xs_dram, xs_cleared):
    B, x_sb, ident, pow_half, sem = sh.B, sh.x_sb, sh.ident, sh.pow_half, sh.sem
    ring, score_bank, ring_filled = sh.ring, sh.score_bank, sh.ring_filled
    QC, KC = NQ * HD, NKV * HD
    G = QC + 2 * KC

    with ExitStack() as ctx:
        def sb(name, shape, dt=F32):
            return ctx.enter_context(nc.sbuf_tensor(name, shape, dt))

        ident_b = sb("ident_b", [P, P], BF16)
        until_r = sb("until_r", [P, P], F32R)
        after = sb("after", [P, P])
        hidden_b = sb("hidden_b", [P, 4, P], BF16)
        cos_sb = sb("cos_sb", [P, HD])
        sin_sb = sb("sin_sb", [P, HD])
        lnw_sb = sb("lnw_sb", [P, 1])
        stage = sh.raw[:, 0:KD * (G + 8)].rearrange("p (k n) -> p k n", k=KD)
        wa_hi = sb("wa_hi", [P, KD, G + 8], F32R)
        wa_lo = sb("wa_lo", [P, KD, G + 8], F32R)
        wp_stage = sh.raw[:, KD * (G + 8):KD * (G + 8) + 8 * D].rearrange("p (k n) -> p k n", k=8)
        wp_hi = sb("wp_hi", [P, 8, D], F32R)
        wp_lo = sb("wp_lo", [P, 8, D], F32R)
        vmean = sb("vmean", [P, KD, NKV])
        bn6 = sb("bn6", [P, B, 6])
        mean = sb("mean", [P, B])
        diff = sb("diff", [P, B])
        var = sb("var", [P, B])
        rstd = sb("rstd", [P, B])
        xn = sb("xn", [P, D])
        xT_hi = sb("xT_hi", [P, KD, P], F32R)
        xT_lo = sb("xT_lo", [P, KD, P], F32R)
        zero_row = sb("zero_row", [P, D])
        t1 = [sb(f"t1_{j}", [P, 8, 2, 32]) for j in range(3)]
        t2 = [sb(f"t2_{j}", [P, 8, 2, 32]) for j in range(3)]
        until = t1[0][:].rearrange("p h e i -> p (h e i)")[:, 0:P]
        qkT = [sb(f"qkT_{i}", [P, 12, P]) for i in range(2)]
        v_sb = [sb(f"v_{i}", [P, NKV, HD + 1]) for i in range(2)]
        z = sb("z", [P, 8])
        az = sb("az", [P, 8])
        ez = sb("ez", [P, 8])
        sp = sb("sp", [P, 8])
        lg = sb("lg", [P, 8])
        lg_hi = sb("lg_hi", [P, 8], F32R)
        lg_lo = sb("lg_lo", [P, 8], F32R)
        d_hi = sb("d_hi", [P, 8, P], F32R)
        d_lo = sb("d_lo", [P, 8, P], F32R)
        decay = [sb(f"decay_{i}", [P, 8, P]) for i in range(2)]
        abs_s = [sb(f"abs_{g}", [P, 4, P]) for g in range(4)]
        r_sb = [sb(f"r_{g}", [P, 4, P]) for g in range(4)]
        rmax = sb("rmax", [P, 16])
        rinv = sb("rinv", [P, 16])
        aT = [sb(f"aT_{i}", [P, 4, P]) for i in range(2)]
        y_sb = sb("y_sb", [P, 16, HD + 1])
        sq = sb("sq", [P, 16, HD])
        ms = sb("ms", [P, 16])
        den = sb("den", [P, 16])
        den2 = sb("den2", [P, 16])
        var_y = sb("var_y", [P, 16])
        f_sb = sb("f_sb", [P, 16])
        yn = sb("yn", [P, 8, P])
        yT_hi = sb("yT_hi", [P, 8, P], F32R)
        yT_lo = sb("yT_lo", [P, 8, P], F32R)

        x_in = [sem("x_in0"), sem("x_in1")]
        wq_in, wkv_in, wp_in, tab_in = sem("wq_in"), sem("wkv_in"), sem("wp_in"), sem("tab_in")
        const_done, const_step = sem("const_done"), sem("const_step")
        ident_done = sem("ident_done")
        vmean_done, vcent_done, wa_hi_done, wa_done, wp_scaled, wp_hi_done, wp_done = (
            sem(n) for n in ("vmean_done", "vcent_done", "wa_hi_done", "wa_done", "wp_scaled", "wp_hi_done", "wp_done"))
        stats_done, stat_step, x_var_done, rstd_done, xn_done = (
            sem(n) for n in ("stats_done", "stat_step", "x_var_done", "rstd_done", "xn_done"))
        xT_hi_done, xT_done = sem("xT_hi_done"), sem("xT_done")
        rope_done, rope_added, qkT_done, v_done = (sem(n) for n in ("rope_done", "rope_added", "qkT_done", "v_done"))
        z_done, az_done, ez_done, sp_done, lg_done, lg_hi_done, lg_lo_done, d_hi_done, d_lo_done, decay_done = (
            sem(n) for n in ("z_done", "az_done", "ez_done", "sp_done", "lg_done", "lg_hi_done", "lg_lo_done", "d_hi_done",
                             "d_lo_done", "decay_done"))
        scores_done, abs_done, r_done, rmax_done, rinv_done, b_done, aT_done = (
            sem(n) for n in ("scores_done", "abs_done", "r_done", "rmax_done", "rinv_done", "b_done", "aT_done"))
        y_done, sq_done, ms_done, den_done, den2_done, var_done, f_done, yn_done = (
            sem(n) for n in ("y_done", "sq_done", "ms_done", "den_done", "den2_done", "var_done", "f_done", "yn_done"))
        yT_hi_done, yT_done, x_added = sem("yT_hi_done"), sem("yT_done"), sem("x_added")

        x_parts = [(0, 2), (2, 10), (10, 20), (20, B)]
        w_parts = [slice(0, QC), slice(QC, QC + KC), slice(QC + KC, G + 8)]

        jobs = Ring(ring, ring_filled, {
            "pro": ["xT", "q0", "q1", "g", "k", "v", "QT0", "QT1", "QT2", "D0", "D1"],
            "first": ["xT", "q0", "tr0", "q1", "tr1", "g", "k", "AV0", "v", "tr2", "AV1", "QT0", "tr3", "QT1",
                      "AV2", "QT2", "D0", "D1", "AV3"],
            "mid": ["xT", "yT0", "yT1", "q0", "tr0", "q1", "wproj", "tr1", "g", "k", "AV0", "v", "tr2", "AV1", "QT0",
                    "tr3", "QT1", "AV2", "QT2", "D0", "D1", "AV3"],
            "last": ["yT0", "yT1", "tr0", "wproj", "tr1", "AV0", "tr2", "AV1", "tr3", "AV2", "AV3"],
            "tail": ["yT0", "yT1", "wproj"],
        }, {
            "yT0": (yT_done, 2, -1), "yT1": (yT_done, 2, 0), "wproj": (x_added, 1, 0), "xT": (xT_done, 1, 2),
            "q0": (rope_done, 3, 4), "q1": (rope_done, 3, 5), "k": (rope_done, 3, 6), "g": (z_done, 1, 2),
            "v": (v_done, 1, 2), "QT0": (qkT_done, 3, 4), "QT1": (qkT_done, 3, 5), "QT2": (qkT_done, 3, 6),
            "D0": (decay_done, 2, 3), "D1": (decay_done, 2, 4),
            **{f"tr{g}": (aT_done, 4, g + 1) for g in range(4)}, **{f"AV{g}": (y_done, 4, g + 1) for g in range(4)},
        }, 0, B - 2, 2)
        start, filled = jobs.start, jobs.filled

        def spread_decay(eng, out, lg_half):
            return eng.tensor_tensor(out[:], after[:].rearrange("p (o n) -> p o n", o=1).to_broadcast([P, 8, P]),
                                     lg_half[:].bitcast(F32).rearrange("p (h o) -> p h o", o=1).to_broadcast([P, 8, P]), ALU.mult)

        block = ctx.enter_context(nc.Block())

        @block.sync
        def _(sp_):
            xv = x.rearrange("b t d -> t b d")
            sp_.dma_start(x_sb[:, 0:2, :], xv[:, 0:2, :]).then_inc(x_in[0], 16)
            w_cols = w_attn.rearrange("(k p) n -> p k n", p=P)
            sp_.dma_start(stage[:, :, 0:QC], w_cols[:, :, 0:QC]).then_inc(wq_in, 16)
            sp_.dma_start(stage[:, :, QC:G + 8], w_cols[:, :, QC:G + 8]).then_inc(wkv_in, 16)
            sp_.dma_start(cos_sb[:], rope_cos).then_inc(tab_in, 16)
            sp_.dma_start(sin_sb[:], rope_sin).then_inc(tab_in, 16)
            sp_.dma_start(lnw_sb[:], ln_w2).then_inc(tab_in, 16)
            sp_.dma_start(wp_stage, w_proj.rearrange("(k p) n -> p k n", p=P)).then_inc(wp_in, 16)
            sp_.dma_start(x_sb[:, 2:B, :], xv[:, 2:B, :]).then_inc(x_in[1], 16)
            sp_.wait_ge(wa_done, 3)
            sp_.wait_ge(wp_done, 1)
            for n, w in enumerate(cross_weights):
                sp_.dma_start(sh.raw[:, 2048 * n:2048 * n + 2048].rearrange("p (k n) -> p k n", n=w.shape[1]),
                              w.rearrange("(k p) n -> p k n", p=P)).then_inc(cross_raw_in, 16)
            sp_.wait_ge(const_done, 1)
            for xs in xs_dram:
                sp_.dma_start(xs.rearrange("(n p) d -> p n d", p=P),
                              zero_row[:].rearrange("p (o d) -> p o d", o=1).to_broadcast([P, xs.shape[0] // P, D])).then_inc(xs_cleared, 16)
            sp_.wait_ge(xs_cleared, 32)

        @block.tensor
        def _(pe):
            def project(out, a_hi, a_lo, w_hi, w_lo, cols, K):
                for k in range(K):
                    nc.tensor.matmul(out, a_hi[:, k, :], w_lo[:, k, cols], start=(k == 0), stop=False)
                    nc.tensor.matmul(out, a_lo[:, k, :], w_hi[:, k, cols], start=False, stop=False)
                    last = nc.tensor.matmul(out, a_hi[:, k, :], w_hi[:, k, cols], start=False, stop=(k == K - 1))
                return last

            def scores(it, o):
                b, qk = it.b, qkT[it.par]
                if o == 0:
                    pe.wait_ge(qkT_done, 3 * (b + 1))
                if it.kind != "first":
                    pe.wait_ge(abs_done, 4 * b + (2 * o - 2))
                for k in range(4):
                    for half in range(2):
                        rows = slice(64 * half, 64 * half + 64)
                        last = nc.tensor.matmul(score_bank[2 * o + half][:, k, :], qk[rows, 4 * o + k, :],
                                                qk[rows, 8 + k, :], start=True, stop=True)
                last.then_inc(scores_done, 1)

            def turn_rows(it, g):
                bank = start(pe, it, f"tr{g}")
                pe.wait_ge(b_done, 4 * it.b + (g + 1))
                for k in range(4):
                    last = nc.tensor.transpose(bank[:, k * P:(k + 1) * P], r_sb[g][:, k, :], ident[:])
                last.then_inc(ring_filled, 1)

            def attend(it, g):
                bank = start(pe, it, f"AV{g}")
                pe.wait_ge(aT_done, 4 * it.b + (g + 1))
                if g == 0:
                    pe.wait_ge(v_done, it.b + 1)
                half = g % 2
                for k in range(4):
                    last = nc.tensor.matmul(bank[:, k * 65:(k + 1) * 65], aT[g % 2][:, k, :],
                                            v_sb[it.par][:, 4 * half + k, :], start=True, stop=True)
                last.then_inc(ring_filled, 1)

            def qk_cols(it, name, c0, n):
                bank = start(pe, it, name)
                project(bank[:, 0:n], xT_hi, xT_lo, wa_hi, wa_lo, slice(c0, c0 + n), KD).then_inc(ring_filled, 1)

            def qk_turn(it, j):
                bank = start(pe, it, f"QT{j}")
                pe.wait_ge(rope_added, 3 * it.b + (4 + j))
                for c in range(4):
                    last = nc.tensor.transpose(bank[:, c * P:(c + 1) * P], t1[j][:, 2 * c:2 * c + 2, :, :].rearrange("p h e i -> p (h e i)"),
                                               ident[:])
                last.then_inc(ring_filled, 1)

            def decays(it, j):
                bank = start(pe, it, f"D{j}")
                pe.wait_ge(d_hi_done, it.b + 2)
                pe.wait_ge(d_lo_done, it.b + 2)
                nc.tensor.matmul(bank[:, :], until_r[:], d_lo[:, 4 * j:4 * j + 4, :], start=True, stop=False)
                nc.tensor.matmul(bank[:, :], until_r[:], d_hi[:, 4 * j:4 * j + 4, :], start=False, stop=False)
                nc.tensor.matmul(bank[:, :], ident_b[:], hidden_b[:, :, :], start=False, stop=True).then_inc(ring_filled, 1)

            pe.wait_ge(ident_done, 1)
            pe.wait_ge(const_done, 1)
            for it in turns(pe, B, 2, 2):
                if it.nxt:
                    bank = start(pe, it, "xT")
                    pe.wait_ge(xn_done, it.b + 2)
                    for k in range(KD):
                        last = nc.tensor.transpose(bank[:, k * P:(k + 1) * P], xn[:, k * P:(k + 1) * P], ident[:])
                    last.then_inc(ring_filled, 1)
                if it.cur:
                    scores(it, 0)
                    scores(it, 1)
                if it.prev:
                    for j in range(2):
                        bank = start(pe, it, f"yT{j}")
                        pe.wait_ge(yn_done, it.b * 4 + (2 * j - 2))
                        for c in range(4):
                            last = nc.tensor.transpose(bank[:, c * P:(c + 1) * P], yn[:, 4 * j + c, :], ident[:])
                        last.then_inc(ring_filled, 1)
                if it.kind == "pro":
                    pe.wait_ge(wa_done, 1)
                if it.nxt:
                    pe.wait_ge(xT_done, it.b + 2)
                    qk_cols(it, "q0", 0, 512)
                if it.cur:
                    turn_rows(it, 0)
                if it.nxt:
                    qk_cols(it, "q1", 512, 512)
                if it.prev:
                    bank = start(pe, it, "wproj")
                    pe.wait_ge(yT_done, 2 * it.b)
                    project(bank[:, 0:D], yT_hi, yT_lo, wp_hi, wp_lo, slice(0, D), 8).then_inc(ring_filled, 1)
                if it.cur:
                    turn_rows(it, 1)
                if it.kind == "pro":
                    pe.wait_ge(wa_done, 3)
                if it.nxt:
                    qk_cols(it, "g", G, 8)
                    qk_cols(it, "k", QC, 512)
                if it.cur:
                    attend(it, 0)
                if it.nxt:
                    qk_cols(it, "v", QC + KC, 512)
                if it.cur:
                    turn_rows(it, 2)
                    attend(it, 1)
                if it.nxt:
                    qk_turn(it, 0)
                if it.cur:
                    turn_rows(it, 3)
                if it.nxt:
                    qk_turn(it, 1)
                if it.cur:
                    attend(it, 2)
                if it.nxt:
                    qk_turn(it, 2)
                    decays(it, 0)
                    decays(it, 1)
                if it.cur:
                    attend(it, 3)
                if it.kind == "first":
                    pe.wait_ge(wp_done, 1)

        @block.scalar
        def _(act):
            def take_turn(it, g):
                bank = filled(act, it, f"tr{g}")
                if g >= 2:
                    jobs.wait_filled(act, it, f"AV{g - 2}")
                nc.scalar.activation(aT[g % 2][:, :, :].rearrange("p a b -> p (a b)"), bank[:, :], ACT.Square).then_inc(aT_done, 1)

            def take_rows(it, g):
                bank = filled(act, it, f"AV{g}")
                if it.kind != "first" and g == 0:
                    act.wait_ge(yn_done, it.b * 4)
                rows = bank[:, 0:260].rearrange("p (h d) -> p h d", d=HD + 1)
                nc.scalar.activation(sq[:, 4 * g:4 * g + 4, :], rows[:, :, 0:HD], ACT.Square).then_inc(sq_done, 1)
                nc.scalar.copy(y_sb[:, 4 * g:4 * g + 4, :].rearrange("p a b -> p (a b)"), bank[:, 0:260]).then_inc(y_done, 1)

            def take_qk(it, j):
                bank = filled(act, it, f"QT{j}")
                nc.scalar.copy(qkT[1 - it.par][:, 4 * j:4 * j + 4, :].rearrange("p a b -> p (a b)"), bank[:, :]).then_inc(qkT_done, 1)

            def take_decay(it, j):
                bank = filled(act, it, f"D{j}")
                if it.cur:
                    act.wait_ge(r_done, 4 * it.b)
                nc.scalar.activation(decay[1 - it.par][:, 4 * j:4 * j + 4, :].rearrange("p a b -> p (a b)"), bank[:, :],
                                     ACT.Exp, scale=0.5).then_inc(decay_done, 1)

            for it in turns(act, B, 2, 2):
                if it.nxt:
                    bank = filled(act, it, "xT")
                    nc.scalar.copy(xT_hi[:].rearrange("p a b -> p (a b)"), bank[:, 0:D]).then_inc(xT_hi_done, 1)
                if it.kind == "pro":
                    for n, cols in enumerate(w_parts):
                        if n == 0:
                            act.wait_ge(wq_in, 16)
                        if n == 1:
                            act.wait_ge(wkv_in, 16)
                        if n == 2:
                            act.wait_ge(vcent_done, 1)
                        nc.scalar.copy(wa_hi[:, :, cols], stage[:, :, cols]).then_inc(wa_hi_done, 1)
                if it.cur:
                    for g in range(4):
                        act.wait_ge(scores_done, 2 * it.b + (1 + g // 2))
                        if it.kind != "first":
                            act.wait_ge(r_done, 4 * it.b + (g - 3))
                        nc.scalar.activation(abs_s[g][:], score_bank[g][:], ACT.Abs, scale=HD ** -0.5).then_inc(abs_done, 1)
                if it.prev:
                    for j in range(2):
                        bank = filled(act, it, f"yT{j}")
                        nc.scalar.copy(yT_hi[:, 4 * j:4 * j + 4, :].rearrange("p a b -> p (a b)"), bank[:, :]).then_inc(yT_hi_done, 1)
                if it.kind == "first":
                    act.wait_ge(wp_scaled, 1)
                    nc.scalar.copy(wp_hi[:], wp_stage).then_inc(wp_hi_done, 1)
                if it.cur:
                    take_turn(it, 0)
                    take_turn(it, 1)
                if it.nxt:
                    act.wait_ge(z_done, it.b + 2)
                    nc.scalar.activation(az[:], z[:], ACT.Abs).then_inc(az_done, 1)
                    act.wait_ge(az_done, it.b + 2)
                    nc.scalar.activation(ez[:], az[:], ACT.Exp, scale=-1.0).then_inc(ez_done, 1)
                    act.wait_ge(ez_done, it.b + 2)
                    nc.scalar.activation(sp[:], ez[:], ACT.Ln, bias=1.0).then_inc(sp_done, 1)
                if it.cur:
                    take_rows(it, 0)
                if it.nxt:
                    bank = filled(act, it, "v")
                    nc.scalar.copy(v_sb[1 - it.par][:, :, 0:HD], bank[:, :].rearrange("p (h d) -> p h d", d=HD)).then_inc(v_done, 1)
                if it.cur:
                    take_turn(it, 2)
                    take_rows(it, 1)
                if it.nxt:
                    take_qk(it, 0)
                if it.cur:
                    take_turn(it, 3)
                if it.nxt:
                    take_qk(it, 1)
                if it.cur:
                    take_rows(it, 2)
                if it.nxt:
                    take_qk(it, 2)
                    take_decay(it, 0)
                    take_decay(it, 1)
                if it.cur:
                    take_rows(it, 3)

        @block.vector
        def _(dve):
            def rope(it, j, name):
                bank = filled(dve, it, name)
                if it.kind != "pro":
                    dve.wait_ge(qkT_done, 3 * it.b + (1 + j))
                q = bank[:, :].rearrange("p (h e i) -> p h e i", e=2, i=32)
                cosb = cos_sb[:, :].rearrange("p (o n) -> p o n", o=1).to_broadcast([P, 8, HD])
                nc.vector.tensor_tensor(t1[j][:].rearrange("p h e i -> p h (e i)"), q.rearrange("p h e i -> p h (e i)"), cosb, ALU.mult)
                for e in range(2):
                    sinb = sin_sb[:, 32 * e:32 * e + 32].rearrange("p (o n) -> p o n", o=1).to_broadcast([P, 8, 32])
                    last = nc.vector.tensor_tensor(t2[j][:, :, e, :], q[:, :, 1 - e, :], sinb, ALU.mult)
                last.then_inc(rope_done, 1)

            def weigh(it, g):
                b, half = it.b, g % 2
                dve.wait_ge(abs_done, 4 * b + (g + 1))
                if g == 0:
                    dve.wait_ge(decay_done, 2 * b + 2)
                if it.kind != "first":
                    dve.wait_ge(aT_done, 4 * b + (g - 3))
                nc.vector.scalar_tensor_tensor(
                    out=r_sb[g][:], in0=abs_s[g][:], scalar=1e-30, in1=decay[it.par][:, 4 * half:4 * half + 4, :],
                    op0=ALU.add, op1=ALU.mult).then_inc(r_done, 1)
                dve.wait_ge(r_done, 4 * b + (g + 1))
                nc.vector.tensor_reduce(rmax[:, 4 * g:4 * g + 4], r_sb[g][:], AX.X, ALU.max).then_inc(rmax_done, 1)
                dve.wait_ge(rmax_done, 4 * b + (g + 1))
                nc.vector.reciprocal(rinv[:, 4 * g:4 * g + 4], rmax[:, 4 * g:4 * g + 4]).then_inc(rinv_done, 1)

            def take_yT(it, j):
                bank = filled(dve, it, f"yT{j}")
                dve.wait_ge(yT_hi_done, 2 * it.b + (j - 1))
                cols = slice(4 * j, 4 * j + 4)
                nc.vector.tensor_tensor(yT_lo[:, cols, :].rearrange("p a b -> p (a b)"), bank[:, :],
                                        yT_hi[:, cols, :].bitcast(F32).rearrange("p a b -> p (a b)"), ALU.subtract).then_inc(yT_done, 1)

            def spreads(b, g):
                n, cols = 4 * b + (g + 1), slice(4 * g, 4 * g + 4)
                dve.wait_ge(sq_done, n)
                dve.wait_ge(y_done, n)
                nc.vector.tensor_scalar(den[:, cols].rearrange("p (h o) -> p h o", o=1), y_sb[:, cols, HD:HD + 1], 1e-6,
                                        (1e-9 * HD) ** 0.5, ALU.add, ALU.mult).then_inc(den_done, 1)
                dve.wait_ge(den_done, n)
                nc.vector.tensor_tensor(den2[:, cols], den[:, cols], den[:, cols], ALU.mult).then_inc(den2_done, 1)
                nc.vector.tensor_reduce(ms[:, cols], sq[:, cols, :], AX.X, ALU.add).then_inc(ms_done, 1)
                dve.wait_ge(den2_done, n)
                dve.wait_ge(ms_done, n)
                nc.vector.tensor_tensor(var_y[:, cols], den2[:, cols], ms[:, cols], ALU.add).then_inc(var_done, 1)

            def statistics(lo, hi, unroll, steps):
                with dve.Fori(lo // unroll, hi // unroll) as m:
                    for u in range(unroll):
                        last = nc.vector.bn_stats(bn6[:, m * unroll + u, :], x_sb[:, m * unroll + u, :])
                    last.then_inc(stats_done, 1)
                dve.wait_ge(stats_done, hi // unroll)
                sl = slice(lo, hi)
                col = lambda c: bn6[:, sl, c:c + 1].rearrange("p b o -> p (b o)")
                nc.vector.tensor_tensor(diff[:, sl], col(1), col(4), ALU.subtract).then_inc(stat_step, 1)
                nc.vector.tensor_tensor(mean[:, sl], col(1), col(4), ALU.add).then_inc(stat_step, 1)
                nc.vector.tensor_tensor(var[:, sl], col(2), col(5), ALU.add).then_inc(stat_step, 1)
                dve.wait_ge(stat_step, steps + 3)
                nc.vector.tensor_tensor(diff[:, sl], diff[:, sl], diff[:, sl], ALU.mult).then_inc(stat_step, 1)
                nc.vector.tensor_scalar(mean[:, sl], mean[:, sl], 0.5, None, ALU.mult).then_inc(stat_step, 1)
                nc.vector.tensor_scalar(var[:, sl], var[:, sl], 1.0 / D, 1e-5, ALU.mult, ALU.add).then_inc(stat_step, 1)
                dve.wait_ge(stat_step, steps + 6)
                nc.vector.scalar_tensor_tensor(out=var[:, sl], in0=diff[:, sl], scalar=0.25, in1=var[:, sl], op0=ALU.mult,
                                               op1=ALU.add).then_inc(x_var_done, 1)

            dve.wait_ge(x_in[0], 16)
            statistics(*x_parts[0], 2, 0)
            def split_low(n):
                dve.wait_ge(wa_hi_done, n + 1)
                cols = w_parts[n]
                nc.vector.tensor_tensor(wa_lo[:, :, cols], stage[:, :, cols], wa_hi[:, :, cols].bitcast(F32),
                                        ALU.subtract).then_inc(wa_done, 1)

            def split_weights():
                dve.wait_ge(wq_in, 16)
                split_low(0)
                dve.wait_ge(wkv_in, 16)
                vv = stage[:, :, QC + KC:G].rearrange("p k (h d) -> p k h d", d=HD)
                for k in range(KD):
                    last = nc.vector.tensor_reduce(vmean[:, k, :], vv[:, k, :, :], AX.X, ALU.add)
                last.then_inc(vmean_done, 1)
                dve.wait_ge(vmean_done, 1)
                nc.vector.tensor_scalar(vmean[:], vmean[:], 1.0 / HD, None, ALU.mult).then_inc(vmean_done, 1)
                dve.wait_ge(vmean_done, 2)
                for k in range(KD):
                    last = nc.vector.tensor_tensor(vv[:, k, :, :], vv[:, k, :, :],
                                                   vmean[:, k, :].rearrange("p (h o) -> p h o", o=1).to_broadcast([P, NKV, HD]),
                                                   ALU.subtract)
                last.then_inc(vcent_done, 1)
                split_low(1)
                split_low(2)

            dve.wait_ge(rstd_done, 1)
            for it in turns(dve, B, 2, 2):
                if it.kind == "mid" and it.m is None and it.b == 1:
                    dve.wait_ge(rstd_done, 2)
                if it.nxt:
                    col = bass.ds(it.b + 1, 1)
                    nc.vector.tensor_scalar(xn[:], x_sb[:, it.b + 1, :], mean[:, col], rstd[:, col], ALU.subtract,
                                            ALU.mult).then_inc(xn_done, 1)
                if it.prev:
                    spreads(it.b - 1, 2)
                if it.prev:
                    spreads(it.b - 1, 3)
                if it.nxt:
                    bank = filled(dve, it, "xT")
                    dve.wait_ge(xT_hi_done, it.b + 2)
                    nc.vector.tensor_tensor(xT_lo[:].rearrange("p a b -> p (a b)"), bank[:, 0:D],
                                            xT_hi[:].bitcast(F32).rearrange("p a b -> p (a b)"), ALU.subtract).then_inc(xT_done, 1)
                if it.kind == "pro":
                    split_weights()
                    dve.wait_ge(tab_in, 48)
                    dve.wait_ge(const_done, 1)
                if it.cur:
                    weigh(it, 0)
                    weigh(it, 1)
                if it.prev:
                    take_yT(it, 0)
                    take_yT(it, 1)
                if it.kind == "first":
                    dve.wait_ge(wp_scaled, 1)
                    dve.wait_ge(wp_hi_done, 1)
                    nc.vector.tensor_tensor(wp_lo[:], wp_stage, wp_hi[:].bitcast(F32), ALU.subtract).then_inc(wp_done, 1)
                if it.nxt:
                    rope(it, 0, "q0")
                if it.cur:
                    weigh(it, 2)
                if it.nxt:
                    rope(it, 1, "q1")
                if it.prev:
                    bank = filled(dve, it, "wproj")
                    xp = x_sb[:, it.b - 1, :]
                    nc.vector.tensor_tensor(xp, xp, bank[:, 0:D], ALU.add).then_inc(x_added, 1)
                if it.cur:
                    weigh(it, 3)
                if it.nxt:
                    bank = filled(dve, it, "g")
                    nc.vector.tensor_scalar(z[:], bank[:, 0:8], 6.906768, None, ALU.add).then_inc(z_done, 1)
                    rope(it, 2, "k")
                    dve.wait_ge(sp_done, it.b + 2)
                    nc.vector.scalar_tensor_tensor(out=lg[:], in0=z[:], scalar=0.0, in1=sp[:], op0=ALU.min,
                                                   op1=ALU.subtract).then_inc(lg_done, 1)
                    dve.wait_ge(lg_done, it.b + 2)
                    if it.kind != "pro":
                        dve.wait_ge(decay_done, 2 * it.b + 2)
                    nc.vector.tensor_copy(lg_hi[:], lg[:]).then_inc(lg_hi_done, 1)
                    dve.wait_ge(lg_hi_done, it.b + 2)
                    nc.vector.tensor_tensor(lg_lo[:], lg[:], lg_hi[:].bitcast(F32), ALU.subtract).then_inc(lg_lo_done, 1)
                    dve.wait_ge(lg_lo_done, it.b + 2)
                    spread_decay(nc.vector, d_lo, lg_lo).then_inc(d_lo_done, 1)
                if it.kind == "first":
                    dve.wait_ge(x_in[1], 16)
                    statistics(*x_parts[1], 2, 6)
                if it.kind == "mid" and it.m is None:
                    statistics(*(x_parts[it.b + 1]), 2, 6 + 6 * it.b)
                if it.cur:
                    spreads(it.b, 0)
                    spreads(it.b, 1)
                if it.kind == "pro":
                    dve.wait_ge(wp_in, 16)
                    nc.vector.tensor_scalar(wp_stage, wp_stage, lnw_sb[:, 0:1], float(HD) ** 0.5, ALU.mult, ALU.mult).then_inc(wp_scaled, 1)
                if it.kind == "mid" and it.m is None and it.b == 2:
                    dve.wait_ge(rstd_done, 4)

        @block.gpsimd
        def _(pool):
            def scale_rows(it, g):
                pool.wait_ge(rinv_done, 4 * it.b + (g + 1))
                r = r_sb[g][:]
                nc.gpsimd.tensor_tensor(r, r, rinv[:, 4 * g:4 * g + 4].rearrange("p (h o) -> p h o", o=1).to_broadcast([P, 4, P]),
                                        ALU.mult).then_inc(b_done, 1)

            def rope_add(it, j):
                pool.wait_ge(rope_done, 3 * it.b + (4 + j))
                nc.gpsimd.tensor_tensor(t1[j][:], t1[j][:], t2[j][:], ALU.add).then_inc(rope_added, 1)

            def normalise(b, g):
                cols = slice(4 * g, 4 * g + 4)
                pool.wait_ge(var_done, 4 * b + (g + 1))
                nc.gpsimd.tensor_tensor(f_sb[:, cols], var_y[:, cols], pow_half[:, 0:4], ALU.pow).then_inc(f_done, 1)
                pool.wait_ge(f_done, 4 * b + (g + 1))
                nc.gpsimd.tensor_tensor(yn[:, 2 * g:2 * g + 2, :].rearrange("p c (h d) -> p (c h) d", d=HD), y_sb[:, cols, 0:HD],
                                        f_sb[:, cols].rearrange("p (h o) -> p h o", o=1).to_broadcast([P, 4, HD]),
                                        ALU.mult).then_inc(yn_done, 1)

            nc.gpsimd.memset(ident[:], 0.0).then_inc(const_step, 1)
            nc.gpsimd.memset(zero_row[:], 0.0).then_inc(const_step, 1)
            nc.gpsimd.memset(until, 1.0).then_inc(const_step, 1)
            nc.gpsimd.memset(after[:], 1.0).then_inc(const_step, 1)
            nc.gpsimd.memset(hidden_b[:], 0.0).then_inc(const_step, 1)
            nc.gpsimd.memset(pow_half[:], -0.5).then_inc(const_step, 1)
            for v in v_sb:
                nc.gpsimd.memset(v[:], 1.0).then_inc(const_step, 1)
            pool.wait_ge(const_step, 8)
            nc.gpsimd.affine_select(out=ident[:], in_=ident[:], compare_op=ALU.not_equal, fill=1.0, base=0,
                                    pattern=[[-1, P]], channel_multiplier=1).then_inc(const_step, 1)
            nc.gpsimd.affine_select(out=until, in_=until, compare_op=ALU.is_ge, fill=0.0, base=0,
                                    pattern=[[1, P]], channel_multiplier=-1).then_inc(const_step, 1)
            nc.gpsimd.affine_select(out=after[:], in_=after[:], compare_op=ALU.is_ge, fill=0.0, base=-1,
                                    pattern=[[-1, P]], channel_multiplier=1).then_inc(const_step, 1)
            nc.gpsimd.affine_select(out=hidden_b[:], in_=hidden_b[:], compare_op=ALU.is_ge, fill=-30000.0, base=0,
                                    pattern=[[0, 4], [-1, P]], channel_multiplier=1).then_inc(const_step, 1)
            pool.wait_ge(const_step, 12)
            nc.gpsimd.tensor_copy(ident_b[:], ident[:]).then_inc(const_step, 1)
            nc.gpsimd.tensor_copy(until_r[:], until).then_inc(const_step, 1)
            pool.wait_ge(const_step, 14)
            pool.sem_inc(ident_done, 1)
            pool.sem_inc(const_done, 1)

            def x_rstd(n):
                cols = slice(*x_parts[n])
                pool.wait_ge(x_var_done, n + 1)
                nc.gpsimd.tensor_tensor(rstd[:, cols], var[:, cols], pow_half[:, cols], ALU.pow).then_inc(rstd_done, 1)

            x_rstd(0)
            for it in turns(pool, B, 2, 2):
                if it.prev:
                    normalise(it.b - 1, 2)
                    normalise(it.b - 1, 3)
                if it.cur:
                    scale_rows(it, 0)
                    scale_rows(it, 1)
                if it.nxt:
                    rope_add(it, 0)
                if it.cur:
                    scale_rows(it, 2)
                if it.nxt:
                    rope_add(it, 1)
                if it.cur:
                    scale_rows(it, 3)
                if it.nxt:
                    rope_add(it, 2)
                    pool.wait_ge(lg_hi_done, it.b + 2)
                    if it.kind != "pro":
                        pool.wait_ge(decay_done, 2 * it.b + 2)
                    spread_decay(nc.gpsimd, d_hi, lg_hi).then_inc(d_hi_done, 1)
                if it.kind == "first" or it.kind == "mid" and it.m is None:
                    x_rstd(it.b + 1)
                if it.cur:
                    if it.kind != "first":
                        pool.wait_ge(yT_hi_done, 2 * it.b)
                    normalise(it.b, 0)
                    normalise(it.b, 1)
    return jobs.end


def cross_attention(nc, sh, jobs_before, ctx_x, gate_w, raw_in, w1, w1_in, xs_dram, xs_cleared):
    B, x_sb, ident, pow_half, sem = sh.B, sh.x_sb, sh.ident, sh.pow_half, sh.sem
    ring, score_bank, ring_filled = sh.ring, sh.score_bank, sh.ring_filled
    rstd_all, shift_all, logits = sh.e_rstd, sh.e_shift, sh.logits
    PAIRS = B // 2
    LATE = 4
    SORT_AT = PAIRS - 1 - LATE
    SB = sh.seqs[0]
    assert SB <= 2 * (SORT_AT - 1)
    places = [(b, t) for b in range(SORT_AT + 2, PAIRS) for t in range(4)]
    SENT = {at: (n + 1) * SB // len(places) for n, at in enumerate(places)}
    KO = 8

    with ExitStack() as ctx:
        def sb(name, shape, dt=F32):
            return ctx.enter_context(nc.sbuf_tensor(name, shape, dt))

        w_raw = [sh.raw[:, 2048 * n:2048 * n + 2048] for n in range(4)]
        w_hi = [sb(f"cw_hi{n}", [P, 2048], F32R) for n in range(4)]
        w_lo = [sb(f"cw_lo{n}", [P, 2048], F32R) for n in range(4)]
        c_sb = sb("c_sb", [P, 2, D])
        bn6 = sb("c_bn6", [P, 2, 6])
        bn2 = sb("c_bn2", [P, 2, 2])
        vpe = sb("c_vpe", [P, 2])
        rstd = sb("c_rstd", [P, 2])
        xn = sb("c_xn", [P, 2, D])
        gate_sb = sb("gate_sb", [P, KD, E])
        sort = Sorting(nc, sh, ctx, 0)
        dispatch = Dispatch(nc, sh, ctx, "b", 2)
        r_bn6 = sb("r_bn6", [P, 2, 6])
        r_bn2 = sb("r_bn2", [P, 2, 2])
        r_vpe = sb("r_vpe", [P, 2])
        r_xn = sb("r_xn", [P, 2, D])
        r_xnT = sb("r_xnT", [P, 2, D])
        inT_hi = {n: sb(f"{n}T_hi2", [P, KD, 2, P], F32R) for n in "xc"}
        inT_lo = {n: sb(f"{n}T_lo2", [P, KD, 2, P], F32R) for n in "xc"}
        qT = sb("qT", [P, 8, 2 * P])
        kT = sb("kT", [P, 8, 2 * P])
        v_sb = [sb(f"c_v{u}", [P, 16 * HD]) for u in range(2)]
        p_sb = [sb(f"p_{i}", [P, 4, P]) for i in range(4)]
        smax = sb("smax", [P, 4, 4])
        den = sb("c_den", [P, 4, 4])
        rden = sb("rden", [P, 4, 4])
        pT = [sb(f"pT_{i}", [P, 4, P]) for i in range(2)]
        oT_hi = [sb(f"oT_hi{u}", [P, 8, P], F32R) for u in range(2)]
        oT_lo = [sb(f"oT_lo{u}", [P, 8, P], F32R) for u in range(2)]

        w_hi_done, w_done, c_in, gate_in = sem("cw_hi_done"), sem("cw_done"), sem("c_in"), sem("gate_in")
        r_bn6_done, r_bn6_seen, r_bn2_done, r_vpe_done, r_rstd_done, r_xn_done, r_xnT_done, r_shift_done, logits_done = (
            sem(f"r_{n}") for n in ("bn6_done", "bn6_seen", "bn2_done", "vpe_done", "rstd_done", "xn_done", "xnT_done",
                                    "shift_done", "logits_done"))
        bn6_done, bn6_seen, bn2_done, vpe_done, rstd_done, xn_done = (
            sem(f"c_{n}") for n in ("bn6_done", "bn6_seen", "bn2_done", "vpe_done", "rstd_done", "xn_done"))
        xT_hi_done, xT_done, cT_hi_done, cT_done = (sem(f"c_{n}") for n in ("xT_hi_done", "xT_done", "cT_hi_done", "cT_done"))
        q_done, k_done, v_done = (sem(f"c_{n}") for n in ("q_done", "k_done", "v_done"))
        scores_done, smax_done, sub_done, exp_done, den_done, rden_done, norm_done, pT_done = (
            sem(f"c_{n}") for n in ("scores_done", "smax_done", "sub_done", "exp_done", "den_done", "rden_done", "norm_done", "pT_done"))
        oT_hi_done, oT_done, x_added, x_seen = (sem(f"c_{n}") for n in ("oT_hi_done", "oT_done", "x_added", "x_seen"))

        mid = ["trA3", "trB3", "q2", "q3", "AV3", "wo0",
               "trA0", "trB0", "k2", "k3", "AV0", "wo1", "xT", "v01", "v11",
               "cT", "trA1", "trB1", "q0", "q1", "AV1",
               "rT", "trA2", "trB2", "k0", "rL", "k1", "AV2", "v00", "v10"]
        last_turn = ("trA3", "trB3", "AV3", "wo0", "wo1", "rT", "rL")
        next_turn = ("xT", "cT", "q0", "q1", "k0", "k1", "v00", "v10")
        jobs = Ring(ring, ring_filled, {
            "pro": list(next_turn),
            "first": [n for n in mid if n not in last_turn],
            "mid": mid,
            "last": [n for n in mid if n not in next_turn],
            "tail": list(last_turn),
        }, {
            "xT": (xT_done, 1, 2), "cT": (cT_done, 1, 2),
            "q0": (q_done, 4, 5), "q1": (q_done, 4, 6), "q2": (q_done, 4, 3), "q3": (q_done, 4, 4),
            "k0": (k_done, 4, 5), "k1": (k_done, 4, 6), "k2": (k_done, 4, 3), "k3": (k_done, 4, 4),
            "v00": (v_done, 4, 5), "v10": (v_done, 4, 6), "v01": (v_done, 4, 3), "v11": (v_done, 4, 4),
            **{f"tr{'AB'[h]}{t}": (pT_done, 8, 2 * t + h + 1) for t in range(3) for h in range(2)},
            "trA3": (pT_done, 8, -1), "trB3": (pT_done, 8, 0),
            **{f"AV{t}": (oT_done, 4, t + 1) for t in range(3)}, "AV3": (oT_done, 4, 0),
            "wo0": (x_added, 2, -1), "wo1": (x_added, 2, 0), "rT": (r_xnT_done, 1, 0), "rL": (logits_done, 1, 0),
        }, jobs_before, PAIRS - 2, 2)
        start, filled = jobs.start, jobs.filled

        def late(it, b):
            return it.m is None and it.b == b

        def to_send(it, quarter):
            if it.m is not None or (it.b, quarter) not in SENT:
                return range(0)
            done = [n for at, n in SENT.items() if at < (it.b, quarter)]
            return range(max(done, default=0), SENT[it.b, quarter])

        block = ctx.enter_context(nc.Block())

        @block.sync
        def _(sync):
            def load(it):
                src = ctx_x.rearrange("(n two) t d -> n t two d", two=2)[it.b + 1]
                sync.dma_start(c_sb[:], src).then_inc(c_in, 16)

            sync.dma_start(gate_sb[:], gate_w.rearrange("(k p) n -> p k n", p=P)).then_inc(gate_in, 16)
            for it in turns(sync, PAIRS, 2, 0, LATE):
                if it.nxt:
                    if it.kind != "pro":
                        if it.kind == "first":
                            jobs.wait_filled(sync, Turn("pro", -1), "cT")
                        else:
                            sync.wait_ge(cT_hi_done, it.b + 1)
                    load(it)
                if it.kind == "first":
                    sync.wait_ge(w_done, 4)
                    sync.dma_start(sh.raw[:, :].rearrange("p (e k n) -> p e k n", e=w1.shape[0], k=KD),
                                   w1.rearrange("e (k p) n -> p e k n", p=P)).then_inc(w1_in, 16)

        @block.tensor
        def _(pe):
            def three(out, pairs):
                for n, ((a_hi, a_lo), (b_hi, b_lo)) in enumerate(pairs):
                    nc.tensor.matmul(out, a_hi, b_lo, start=(n == 0), stop=False)
                    nc.tensor.matmul(out, a_lo, b_hi, start=False, stop=False)
                    last = nc.tensor.matmul(out, a_hi, b_hi, start=False, stop=(n == len(pairs) - 1))
                return last

            def weight(n, k, c0, c1):
                cols = 1024 if n < 3 else D
                return tuple(w[n][:, k * cols + c0:k * cols + c1] for w in (w_hi, w_lo))

            def turn_in(it, name, tile, ready):
                bank = start(pe, it, f"{name}T")
                pe.wait_ge(ready, (it.b + 2) * (1 if name == "x" else 16))
                for k in range(KD):
                    for u in range(2):
                        last = nc.tensor.transpose(bank[:, (2 * k + u) * P:(2 * k + u + 1) * P],
                                                   tile[:, u, k * P:(k + 1) * P], ident[:])
                last.then_inc(ring_filled, 1)

            def project_T(it, which, j):
                if it.kind == "pro":
                    pe.wait_ge(w_done, 1 if which == "q" else 2)
                bank = start(pe, it, f"{which}{j}")
                n, src = (0, "x") if which == "q" else (1, "c")
                for c in range(2):
                    last = three(bank[:, c * 2 * P:(c + 1) * 2 * P], [
                        (weight(n, k, (2 * j + c) * P, (2 * j + c + 1) * P),
                         tuple(t[src][:, k, :, :].rearrange("p u t -> p (u t)") for t in (inT_hi, inT_lo)))
                        for k in range(KD)])
                last.then_inc(ring_filled, 1)

            def project_v(it, u, o):
                if it.kind == "pro":
                    pe.wait_ge(w_done, 3)
                bank = start(pe, it, f"v{u}{o}")
                three(bank[:, :], [(tuple(t["c"][:, k, u, :] for t in (inT_hi, inT_lo)), weight(2, k, 512 * o, 512 * o + 512))
                                   for k in range(KD)]).then_inc(ring_filled, 1)

            def scores(it, t):
                u, o = t % 2, t // 2
                if t == 0:
                    pe.wait_ge(q_done, 4 * it.b + 2)
                    pe.wait_ge(k_done, 4 * it.b + 2)
                if t == 2:
                    pe.wait_ge(q_done, 4 * it.b + 4)
                    pe.wait_ge(k_done, 4 * it.b + 4)
                if it.kind != "first" or t >= 2:
                    pe.wait_ge(sub_done, 8 * it.b + (2 * t - 2))
                for k in range(4):
                    for half in range(2):
                        rows = slice(64 * half, 64 * half + 64)
                        cols = slice(u * P, (u + 1) * P)
                        last = nc.tensor.matmul(score_bank[2 * (t % 2) + half][:, k, :], qT[rows, 4 * o + k, cols],
                                                kT[rows, 4 * o + k, cols], start=True, stop=True)
                last.then_inc(scores_done, 1)

            def turn_rows(it, t):
                b = it.b - 1 if t == 3 else it.b
                for half in range(2):
                    bank = start(pe, it, f"tr{'AB'[half]}{t}")
                    pe.wait_ge(norm_done, 8 * b + (2 * t + half + 1))
                    for k in range(4):
                        last = nc.tensor.transpose(bank[:, k * P:(k + 1) * P], p_sb[2 * (t % 2) + half][:, k, :], ident[:])
                    last.then_inc(ring_filled, 1)

            def attend(it, t):
                b, u, o = it.b - 1 if t == 3 else it.b, t % 2, t // 2
                bank = start(pe, it, f"AV{t}")
                pe.wait_ge(v_done, 4 * b + (2 if o == 0 else 4))
                pe.wait_ge(pT_done, 8 * b + (2 * t + 2))
                for k in range(4):
                    for half in range(2):
                        h = 8 * o + 2 * k + half
                        last = nc.tensor.matmul(bank[64 * half:64 * half + 64, k * P:(k + 1) * P],
                                                v_sb[u][:, h * HD:(h + 1) * HD], pT[half][:, k, :], start=True, stop=True,
                                                skip_group_check=True)
                last.then_inc(ring_filled, 1)

            def project_out(it, u):
                bank = start(pe, it, f"wo{u}")
                pe.wait_ge(oT_done, 4 * it.b + (-1 if u == 0 else 0))
                three(bank[:, 0:D], [((oT_hi[u][:, k, :], oT_lo[u][:, k, :]), weight(3, k, 0, D))
                                     for k in range(KO)]).then_inc(ring_filled, 1)

            for it in turns(pe, PAIRS, 2, 0, LATE):
                if it.kind == "pro":
                    pe.wait_ge(gate_in, 16)
                if it.cur:
                    scores(it, 0)
                if it.prev:
                    turn_rows(it, 3)
                if it.kind == "first":
                    pe.wait_ge(w_done, 4)
                if it.cur:
                    project_T(it, "q", 2)
                    project_T(it, "q", 3)
                if it.prev:
                    attend(it, 3)
                    project_out(it, 0)
                if it.cur:
                    scores(it, 1)
                    turn_rows(it, 0)
                    project_T(it, "k", 2)
                    project_T(it, "k", 3)
                    attend(it, 0)
                if it.prev:
                    project_out(it, 1)
                if it.nxt:
                    turn_in(it, "x", xn, xn_done)
                if it.cur:
                    project_v(it, 0, 1)
                    project_v(it, 1, 1)
                if it.nxt:
                    turn_in(it, "c", c_sb, c_in)
                if it.cur:
                    scores(it, 2)
                    turn_rows(it, 1)
                if it.nxt:
                    pe.wait_ge(xT_done, it.b + 2)
                    project_T(it, "q", 0)
                    project_T(it, "q", 1)
                if it.cur:
                    attend(it, 1)
                    scores(it, 3)
                if it.prev:
                    bank = start(pe, it, "rT")
                    pe.wait_ge(r_xn_done, it.b)
                    for u in range(2):
                        for k in range(KD):
                            last = nc.tensor.transpose(bank[:, u * D + k * P:u * D + (k + 1) * P], r_xn[:, u, k * P:(k + 1) * P], ident[:])
                    last.then_inc(ring_filled, 1)
                if it.cur:
                    turn_rows(it, 2)
                if it.nxt:
                    pe.wait_ge(cT_done, it.b + 2)
                    project_T(it, "k", 0)
                if it.prev:
                    bank = start(pe, it, "rL")
                    pe.wait_ge(r_xnT_done, it.b)
                    for u in range(2):
                        for k in range(KD):
                            last = nc.tensor.matmul(bank[:, u * E:(u + 1) * E], r_xnT[:, u, k * P:(k + 1) * P], gate_sb[:, k, :],
                                                    start=(k == 0), stop=(k == KD - 1))
                    if late(it, SORT_AT):
                        last = sort.count(pe, bank)
                    last.then_inc(ring_filled, 1)
                if it.nxt:
                    project_T(it, "k", 1)
                if it.cur:
                    attend(it, 2)
                if it.nxt:
                    project_v(it, 0, 0)
                    project_v(it, 1, 0)

        @block.scalar
        def _(act):
            def expo(it, t):
                for half in range(2):
                    p = p_sb[2 * (t % 2) + half]
                    act.wait_ge(sub_done, 8 * it.b + (2 * t + half + 1))
                    nc.scalar.activation(p[:], p[:], ACT.Exp, scale=HD ** -0.5).then_inc(exp_done, 1)

            def take_turn(it, t):
                for half in range(2):
                    bank = filled(act, it, f"tr{'AB'[half]}{t}")
                    if t == 0 and it.kind != "first":
                        jobs.wait_filled(act, it, "AV3")
                    if t in (1, 2):
                        jobs.wait_filled(act, it, f"AV{t - 1}")
                    nc.scalar.copy(pT[half][:].rearrange("p a b -> p (a b)"), bank[:, :]).then_inc(pT_done, 1)

            def take_q(it, j):
                bank = filled(act, it, f"q{j}")
                nc.scalar.copy(qT[:, 2 * j:2 * j + 2, :].rearrange("p a b -> p (a b)"), bank[:, :]).then_inc(q_done, 1)

            def take_out(it, t):
                u, o = t % 2, t // 2
                bank = filled(act, it, f"AV{t}")
                if it.kind != "first" and t < 2:
                    jobs.wait_filled(act, it, f"wo{t}")
                nc.scalar.copy(oT_hi[u][:, 4 * o:4 * o + 4, :].rearrange("p a b -> p (a b)"), bank[:, :]).then_inc(oT_hi_done, 1)

            def take_in(it, n, done):
                bank = filled(act, it, f"{n}T")
                nc.scalar.copy(inT_hi[n][:].rearrange("p k u t -> p (k u t)"), bank[:, :]).then_inc(done, 1)

            def take_v(it, u, o):
                bank = filled(act, it, f"v{u}{o}")
                nc.scalar.copy(v_sb[u][:, 512 * o:512 * o + 512], bank[:, :]).then_inc(v_done, 1)

            act.wait_ge(raw_in, 64)
            def split_high(n):
                nc.scalar.copy(w_hi[n][:], w_raw[n]).then_inc(w_hi_done, 1)

            split_high(0)
            def send(it, quarter):
                for n in to_send(it, quarter):
                    if n == 0:
                        act.wait_ge(sort.slots_done, sort.done)
                    dispatch.lay_out(act, n, n % 2, 16 * (n // 2) if n >= 2 else None)

            for it in turns(act, PAIRS, 2, 0, LATE):
                if it.prev:
                    take_turn(it, 3)
                if it.cur:
                    expo(it, 0)
                    send(it, 0)
                    take_q(it, 2)
                    take_q(it, 3)
                if it.prev:
                    take_out(it, 3)
                if it.cur:
                    take_turn(it, 0)
                    expo(it, 1)
                    send(it, 1)
                    take_out(it, 0)
                if it.nxt:
                    take_in(it, "x", xT_hi_done)
                if it.cur:
                    take_v(it, 0, 1)
                    take_v(it, 1, 1)
                if it.nxt:
                    take_in(it, "c", cT_hi_done)
                if it.kind == "pro":
                    for n in range(1, 4):
                        split_high(n)
                if it.cur:
                    take_turn(it, 1)
                    expo(it, 2)
                    send(it, 2)
                if it.nxt:
                    take_q(it, 0)
                    take_q(it, 1)
                if it.cur:
                    take_out(it, 1)
                if it.prev:
                    bank = filled(act, it, "rT")
                    nc.scalar.copy(r_xnT[:].rearrange("p u d -> p (u d)"), bank[:, :]).then_inc(r_xnT_done, 1)
                if it.cur:
                    take_turn(it, 2)
                    expo(it, 3)
                    take_out(it, 2)
                if it.nxt:
                    take_v(it, 0, 0)
                    take_v(it, 1, 0)
                send(it, 3)

        @block.vector
        def _(dve):
            def softmax_in(it, t):
                for half in range(2):
                    i = 2 * (t % 2) + half
                    n = 8 * it.b + (2 * t + half + 1)
                    if half == 0:
                        dve.wait_ge(scores_done, 4 * it.b + (t + 1))
                    nc.vector.tensor_reduce(smax[:, i, :], score_bank[i][:], AX.X, ALU.max).then_inc(smax_done, 1)
                    if t >= 2 or it.kind != "first":
                        dve.wait_ge(pT_done, 8 * it.b + (2 * t + half - 3))
                    dve.wait_ge(smax_done, n)
                    nc.vector.tensor_tensor(p_sb[i][:], score_bank[i][:],
                                            smax[:, i, :].rearrange("p (h o) -> p h o", o=1).to_broadcast([P, 4, P]),
                                            ALU.subtract).then_inc(sub_done, 1)

            def sums(it, t):
                for half in range(2):
                    i = 2 * (t % 2) + half
                    n = 8 * it.b + (2 * t + half + 1)
                    dve.wait_ge(exp_done, n)
                    nc.vector.tensor_reduce(den[:, i, :], p_sb[i][:], AX.X, ALU.add).then_inc(den_done, 1)
                    dve.wait_ge(den_done, n)
                    nc.vector.reciprocal(rden[:, i, :], den[:, i, :]).then_inc(rden_done, 1)

            def take_low(it, name, hi, lo, hi_done, n, done):
                bank = filled(dve, it, name)
                dve.wait_ge(hi_done, n)
                nc.vector.tensor_tensor(lo, bank[:, :], hi.bitcast(F32), ALU.subtract).then_inc(done, 1)

            def take_out(it, t):
                u, o = t % 2, t // 2
                hi, lo = (x[u][:, 4 * o:4 * o + 4, :].rearrange("p a b -> p (a b)") for x in (oT_hi, oT_lo))
                take_low(it, f"AV{t}", hi, lo, oT_hi_done, 4 * it.b + (0 if t == 3 else t + 1), oT_done)

            def take_in(it, n, hi_done, done):
                hi, lo = (t[n][:].rearrange("p k u t -> p (k u t)") for t in (inT_hi, inT_lo))
                take_low(it, f"{n}T", hi, lo, hi_done, it.b + 2, done)

            def take_k(it, j):
                bank = filled(dve, it, f"k{j}")
                nc.vector.tensor_copy(kT[:, 2 * j:2 * j + 2, :].rearrange("p a b -> p (a b)"), bank[:, :]).then_inc(k_done, 1)

            def add_out(it, u):
                bank = filled(dve, it, f"wo{u}")
                xp = x_sb[:, 2 * it.b - 2 + u, :]
                nc.vector.tensor_tensor(xp, xp, bank[:, 0:D], ALU.add).then_inc(x_added, 1)

            def router_stats(it):
                dve.wait_ge(x_added, 2 * it.b)
                dve.sem_inc(x_seen, 1)
                for u in range(2):
                    last = nc.vector.bn_stats(r_bn6[:, u, :], x_sb[:, 2 * it.b - 2 + u, :])
                last.then_inc(r_bn6_done, 1)
                dve.wait_ge(r_bn6_done, it.b)
                dve.sem_inc(r_bn6_seen, 1)
                for u in range(2):
                    last = nc.vector.bn_aggr(r_bn2[:, u, :], r_bn6[:, u, :])
                last.then_inc(r_bn2_done, 1)
                dve.wait_ge(r_bn2_done, it.b)
                nc.vector.tensor_scalar(r_vpe[:].rearrange("p (u o) -> p u o", o=1), r_bn2[:, :, 1:2], 1e-5, None,
                                        ALU.add).then_inc(r_vpe_done, 1)

            def router_rows(it):
                dve.wait_ge(r_rstd_done, it.b)
                pair = bass.ds(2 * it.b - 2, 2)
                for u in range(2):
                    last = nc.vector.tensor_scalar(r_xn[:, u, :], x_sb[:, 2 * it.b - 2 + u, :], r_bn2[:, u, 0:1],
                                                   rstd_all[:, bass.ds(2 * it.b - 2 + u, 1)], ALU.subtract, ALU.mult)
                last.then_inc(r_xn_done, 1)
                one = lambda t: t.rearrange("p (u o) -> p u o", o=1)
                nc.vector.scalar_tensor_tensor(out=one(shift_all[:, pair]), in0=r_bn2[:, :, 0:1], scalar=-1.0,
                                               in1=one(rstd_all[:, pair]), op0=ALU.mult, op1=ALU.mult).then_inc(r_shift_done, 1)

            def split_low(n):
                dve.wait_ge(w_hi_done, n + 1)
                nc.vector.tensor_tensor(w_lo[n][:], w_raw[n], w_hi[n][:].bitcast(F32), ALU.subtract).then_inc(w_done, 1)

            for it in turns(dve, PAIRS, 2, 0, LATE):
                if it.nxt:
                    xb = [x_sb[:, 2 * it.b + 2 + u, :] for u in range(2)]
                    for u in range(2):
                        last = nc.vector.bn_stats(bn6[:, u, :], xb[u])
                    last.then_inc(bn6_done, 1)
                    dve.wait_ge(bn6_done, it.b + 2)
                    dve.sem_inc(bn6_seen, 1)
                    for u in range(2):
                        last = nc.vector.bn_aggr(bn2[:, u, :], bn6[:, u, :])
                    last.then_inc(bn2_done, 1)
                    dve.wait_ge(bn2_done, it.b + 2)
                    nc.vector.tensor_scalar(vpe[:].rearrange("p (u o) -> p u o", o=1), bn2[:, :, 1:2], 1e-5, None,
                                            ALU.add).then_inc(vpe_done, 1)
                if it.cur:
                    softmax_in(it, 0)
                if it.prev:
                    take_out(it, 3)
                if it.cur:
                    sums(it, 0)
                if it.prev:
                    add_out(it, 0)
                if it.nxt:
                    dve.wait_ge(rstd_done, it.b + 2)
                    if it.kind != "pro":
                        dve.wait_ge(xT_hi_done, it.b + 1)
                    for u in range(2):
                        last = nc.vector.tensor_scalar(xn[:, u, :], xb[u], bn2[:, u, 0:1], rstd[:, u:u + 1], ALU.subtract, ALU.mult)
                    last.then_inc(xn_done, 1)
                if late(it, SORT_AT):
                    dve.wait_ge(logits_done, SORT_AT - 1)
                    sort.choose(dve)
                if late(it, SORT_AT + 1):
                    sort.add_up(dve)
                if it.kind == "pro":
                    split_low(0)
                if it.cur:
                    softmax_in(it, 1)
                    take_k(it, 2)
                    take_k(it, 3)
                    sums(it, 1)
                    take_out(it, 0)
                if it.prev:
                    add_out(it, 1)
                    router_stats(it)
                if late(it, SORT_AT + 1):
                    sort.place(dve)
                if it.nxt:
                    take_in(it, "x", xT_hi_done, xT_done)
                    take_in(it, "c", cT_hi_done, cT_done)
                if it.cur:
                    softmax_in(it, 2)
                if it.kind == "pro":
                    for n in range(1, 4):
                        split_low(n)
                if it.cur:
                    sums(it, 2)
                if it.prev:
                    router_rows(it)
                if it.cur:
                    take_out(it, 1)
                    softmax_in(it, 3)
                if it.nxt:
                    take_k(it, 0)
                if it.prev:
                    bank = filled(dve, it, "rL")
                    if late(it, SORT_AT):
                        sort.take_counts(dve, bank)
                    nc.vector.tensor_copy(logits[:, bass.ds(2 * it.b - 2, 2), :],
                                          bank[:, 0:2 * E].rearrange("p (u e) -> p u e", e=E)).then_inc(logits_done, 1)
                if it.nxt:
                    take_k(it, 1)
                if it.cur:
                    sums(it, 3)
                    take_out(it, 2)

        @block.gpsimd
        def _(pool):
            def normalise(it, t):
                for half in range(2):
                    i = 2 * (t % 2) + half
                    pool.wait_ge(rden_done, 8 * it.b + (2 * t + half + 1))
                    nc.gpsimd.tensor_tensor(p_sb[i][:], p_sb[i][:],
                                            rden[:, i, :].rearrange("p (h o) -> p h o", o=1).to_broadcast([P, 4, P]),
                                            ALU.mult).then_inc(norm_done, 1)

            sort.constants(pool)
            pool.wait_ge(xs_cleared, 32)
            for it in turns(pool, PAIRS, 2, 0, LATE):
                if it.nxt:
                    pool.wait_ge(vpe_done, it.b + 2)
                    nc.gpsimd.tensor_tensor(rstd[:], vpe[:], pow_half[:, 0:2], ALU.pow).then_inc(rstd_done, 1)
                for t in range(4):
                    if it.cur:
                        normalise(it, t)
                    for n in to_send(it, t):
                        dispatch.scatter(pool, n + 1, n % 2, xs_dram[0])
                    if it.prev and t == 1:
                        pool.wait_ge(r_vpe_done, it.b)
                        nc.gpsimd.tensor_tensor(rstd_all[:, bass.ds(2 * it.b - 2, 2)], r_vpe[:], pow_half[:, 0:2],
                                                ALU.pow).then_inc(r_rstd_done, 1)
            dispatch.finish(pool, SB)
    return jobs.end


class Plan:

    def __init__(self, banks, filled_sem, before, lo, hi, order, read_by):
        self.banks, self.filled_sem, self.lo, self.hi, self.order, self.read_by = banks, filled_sem, lo, hi, order, read_by
        self.number, self.last = {}, {}
        jobs = []
        for b in range(lo, hi + 1):
            for name in order(b):
                self.number[b, name] = before + len(jobs)
                self.last[b, name] = jobs[-RING] if len(jobs) >= RING else None
                jobs.append((b, name))
        self.end = before + len(jobs)

    def turns(self, eng, *loops):
        b = self.lo
        for first, last, unroll in [*loops, (self.hi + 1, self.hi, 1)]:
            for b in range(b, first):
                yield PlanTurn(self, b)
            b = max(b, first)
            if last >= first:
                assert (last - first + 1) % unroll == 0
                for c in range(first, last + 1):
                    rep = first + (c - first) % unroll
                    for name in self.order(rep):
                        p, q = self.last[rep, name], self.last[c, name]
                        assert p and q and p[1] == q[1] and rep - p[0] == c - q[0]
                        assert (self.number[c, name] - self.number[rep, name]) % RING == 0
                with eng.Fori(0, (last - first + 1) // unroll) as m:
                    for u in range(unroll):
                        yield PlanTurn(self, first + u, m, unroll)
                b = last + 1


class PlanTurn:

    def __init__(self, plan, rep, m=None, unroll=1):
        self.plan, self.rep, self.m, self.unroll = plan, rep, m, unroll

    def at(self, a, c):
        return self.rep * a + c if self.m is None else self.m * (a * self.unroll) + (self.rep * a + c)

    def has(self, name):
        return (self.rep, name) in self.plan.number

    def wait_filled(self, eng, name):
        n = self.plan.number[self.rep, name] + 1
        if self.m is not None:
            n = self.m * (self.unroll * len(self.plan.order(self.rep))) + n
        eng.wait_ge(self.plan.filled_sem, n)

    def filled(self, eng, name):
        self.wait_filled(eng, name)
        return self.plan.banks[self.plan.number[self.rep, name] % RING]

    def start(self, pe, name):
        last = self.plan.last[self.rep, name]
        if last:
            read, a, c = self.plan.read_by[last[1]]
            pe.wait_ge(read, self.at(a, c + a * (last[0] - self.rep)))
        return self.plan.banks[self.plan.number[self.rep, name] % RING]


def experts(nc, sh, raw1, jobs_before, w2, raw1_in, xs_dram, out):
    B, x_sb, ident, sem = sh.B, sh.x_sb, sh.ident, sh.sem
    ring, ring_filled = sh.ring, sh.ring_filled
    top, slot, tile_w = sh.top, sh.slot, sh.tile_w
    KF = F // P
    S0, S1 = sh.seqs
    T0, T1 = sh.tiles
    NT = T0 + T1
    XG = 4
    assert EW == KF * D

    ys_dram = [nc.dram_tensor(f"ys_dram{s}", (n * P, D), F32).ap() for s, n in enumerate(sh.tiles)]

    with ExitStack() as ctx:
        def sb(name, shape, dt=F32):
            return ctx.enter_context(nc.sbuf_tensor(name, shape, dt))

        w1_lo = sb("w1_lo", [P, E * EW], F32R)
        with nc.sbuf_tensor("raw2", [P, E * EW], F32) as raw2:
            pass
        w2_lo = sb("w2_lo", [P, E * EW], F32R)
        w1_hi = sb("w1_hi", [P, E * EW], F32R)
        w2_hi = sb("w2_hi", [P, E * EW], F32R)
        sort = Sorting(nc, sh, ctx, 1)
        dispatch = Dispatch(nc, sh, ctx, "c", CS)
        share = sb("share", [P, 2, B])
        exp_d = sb("exp_d", [P, B])
        sum_of = sb("sum_of", [P, B])
        yg = [sb(f"yg{i}", [P, D]) for i in range(2 * CS)]
        xg = [sb(f"xg{i}", [P, D]) for i in range(XG)]
        gT_hi = [sb(f"gT_hi{i}", [P, KD, P], F32R) for i in range(2)]
        gT_lo = [sb(f"gT_lo{i}", [P, KD, P], F32R) for i in range(2)]
        h_sb = [sb(f"h{i}", [P, F]) for i in range(2)]
        hT_hi = [sb(f"hT_hi{i}", [P, KF, P], F32R) for i in range(2)]
        hT_lo = [sb(f"hT_lo{i}", [P, KF, P], F32R) for i in range(2)]
        y_sb = [sb(f"y_out{i}", [P, D]) for i in range(2)]
        take_at = [sb(f"take_at{i}", [P, 2, 1], mybir.dt.int32) for i in range(CS)]

        raw2_in = sem("raw2_in")
        w_hi_done, w1_done, w2_done = sem("ew_hi_done"), sem("w1_done"), sem("w2_done")
        exp_in, exp_done, share_step = sem("exp_in"), sem("exp_done"), sem("share_step")
        gather_ready = sem("gather_ready")
        seg_sent = sem("seg_sent")
        xg_in = [sem(f"xg_in{i}") for i in range(XG)]
        gT_hi_done, gT_done, silu_done, hT_hi_done, hT_done, y_done = (
            sem(n) for n in ("gT_hi_done", "gT_done", "silu_done", "hT_hi_done", "hT_done", "y_out_done"))
        y_stored = [sem(f"y_stored{i}") for i in range(2)]
        seg_stored = sem("seg_stored")
        take_at_done = sem("take_at_done")
        taken = [sem(f"taken{i}") for i in range(2 * CS)]
        comb_step, comb_done = sem("comb_step"), sem("comb_done")
        out_sent = [sem(f"out_sent{i}") for i in range(CS)]

        def tile_jobs(j):
            return (["h"] * (0 <= j < NT) + ["hT"] * (0 <= j - 1 < NT) + ["xT"] * (0 <= j + 2 < NT)
                    + ["y"] * (0 <= j - 2 < NT))

        tiles = Plan(ring, ring_filled, jobs_before + 1, -2, NT + 1, tile_jobs,
                     {"h": (silu_done, 1, 1), "y": (y_done, 1, -1), "hT": (hT_done, 1, 0), "xT": (gT_done, 1, 3)})
        tile_loop_end = 4 + (NT - 6) // 4 * 4 - 1
        send_to = 4 + S1 - CS - 1
        comb_from = T0 + 3
        assert comb_from % 2 == 0
        comb_to = comb_from + S0 - 1
        assert comb_to <= tile_loop_end

        def split_low(eng, ops, i, c, done):
            raw, hi, lo = ((raw1, w1_hi, w1_lo), (raw2, w2_hi, w2_lo))[i]
            cols = slice(c * 4 * EW, (c + 1) * 4 * EW)
            eng.wait_ge(w_hi_done, 2 * i + c + 1)
            ops.tensor_tensor(lo[:, cols], raw[:, cols], hi[:, cols].bitcast(F32), ALU.subtract).then_inc(done, 1)

        block = ctx.enter_context(nc.Block())

        @block.sync
        def _(sync):
            sync.dma_start(raw2[:, :].rearrange("p (e k n) -> p e k n", e=E, k=KF),
                           w2.rearrange("e (k p) n -> p e k n", p=P)).then_inc(raw2_in, 16)

            def rows(dram, it, by):
                s = int(it.rep + by >= T0)
                return dram[s][bass.ts(it.at(1, by - s * T0), P), :]

            def store_out(m, u):
                sync.wait_ge(comb_done, m * CS + (u + 1))
                sync.dma_start(out[m * CS + u], yg[2 * u][:]).then_inc(out_sent[u], 16)

            def store_all(tiles_so_far):
                for u in range(2):
                    sync.wait_ge(y_stored[u], 16 * ((tiles_so_far + 1 - u) // 2))
                sync.sem_inc(seg_stored, 1)

            for j in range(XG):
                sync.dma_start(xg[j][:], xs_dram[0][j * P:(j + 1) * P, :]).then_inc(xg_in[j], 16)
            for it in tiles.turns(sync, (4, 4 + (T0 - XG - 4) // 4 * 4 - 1, 4), (comb_from, comb_to, CS)):
                j = it.rep
                if j + XG == T0:
                    sync.wait_ge(seg_sent, 1)
                if 0 <= j and j + XG < NT:
                    sync.wait_ge(gT_hi_done, it.at(1, 1))
                    sync.dma_start(xg[j % XG][:], rows(xs_dram, it, XG)).then_inc(xg_in[j % XG], 16)
                if j >= 2:
                    sync.wait_ge(y_done, it.at(1, -1))
                    sync.dma_start(rows(ys_dram, it, -2), y_sb[j % 2][:]).then_inc(y_stored[j % 2], 16)
                if j == T0 + 2:
                    store_all(T0)
                if it.m is not None and j >= comb_from:
                    store_out(it.m, j - comb_from)
            store_all(NT)
            with sync.Fori(S0 // CS, B // CS) as m:
                for u in range(CS):
                    store_out(m, u)
            for u in range(CS):
                sync.wait_ge(out_sent[u], 16 * (B // CS))

        @block.tensor
        def _(pe):
            sort.count(pe, ring[jobs_before % RING]).then_inc(ring_filled, 1)
            pe.wait_ge(w1_done, 2)

            def expert_of(j):
                return pe.value_load(tile_w[0:1, bass.ds(j, 1)], min_val=0, max_val=(E - 1) * EW)

            for it in tiles.turns(pe, (4, tile_loop_end, 4)):
                j, u = it.rep, it.rep % 2
                if it.has("h"):
                    at_h = expert_of(it.at(1, 0))
                if it.has("y"):
                    at_y = expert_of(it.at(1, -2))
                if it.has("h"):
                    bank = it.start(pe, "h")
                    pe.wait_ge(gT_done, it.at(1, 1))
                    for k in range(KD):
                        hi, lo = (w[:, bass.ds(at_h + k * F, F)] for w in (w1_hi, w1_lo))
                        nc.tensor.matmul(bank[:, :], gT_hi[u][:, k, :], lo, start=(k == 0), stop=False)
                        nc.tensor.matmul(bank[:, :], gT_lo[u][:, k, :], hi, start=False, stop=False)
                        last = nc.tensor.matmul(bank[:, :], gT_hi[u][:, k, :], hi, start=False, stop=(k == KD - 1))
                    last.then_inc(ring_filled, 1)
                if it.has("hT"):
                    bank = it.start(pe, "hT")
                    pe.wait_ge(silu_done, it.at(1, 0))
                    for k in range(KF):
                        last = nc.tensor.transpose(bank[:, k * P:(k + 1) * P], h_sb[1 - u][:, k * P:(k + 1) * P], ident[:])
                    last.then_inc(ring_filled, 1)
                if it.has("xT"):
                    bank = it.start(pe, "xT")
                    v = 16 * ((j + 2) // XG + 1)
                    pe.wait_ge(xg_in[(j + 2) % XG], v if it.m is None else it.m * 16 + v)
                    for k in range(KD):
                        last = nc.tensor.transpose(bank[:, k * P:(k + 1) * P], xg[(j + 2) % XG][:, k * P:(k + 1) * P], ident[:])
                    last.then_inc(ring_filled, 1)
                if it.rep == 2:
                    pe.wait_ge(w2_done, 2)
                    pe.wait_ge(sort.tiles_done, sort.done)
                if it.has("y"):
                    bank = it.start(pe, "y")
                    pe.wait_ge(hT_done, it.at(1, -1))
                    for k in range(KF):
                        hi, lo = (w[:, bass.ds(at_y + k * D, D)] for w in (w2_hi, w2_lo))
                        nc.tensor.matmul(bank[:, 0:D], hT_hi[u][:, k, :], lo, start=(k == 0), stop=False)
                        nc.tensor.matmul(bank[:, 0:D], hT_lo[u][:, k, :], hi, start=False, stop=False)
                        last = nc.tensor.matmul(bank[:, 0:D], hT_hi[u][:, k, :], hi, start=False, stop=(k == KF - 1))
                    last.then_inc(ring_filled, 1)

        @block.scalar
        def _(act):
            def split_high(raw, hi):
                for c in range(2):
                    cols = slice(c * 4 * EW, (c + 1) * 4 * EW)
                    nc.scalar.copy(hi[:, cols], raw[:, cols]).then_inc(w_hi_done, 1)

            act.wait_ge(raw1_in, 16)
            split_high(raw1, w1_hi)
            act.wait_ge(raw2_in, 16)
            split_high(raw2, w2_hi)
            act.wait_ge(exp_in, 1)
            nc.scalar.activation(exp_d[:], exp_d[:], ACT.Exp).then_inc(exp_done, 1)
            act.wait_ge(sort.slots_done, sort.done)
            for u in range(CS):
                dispatch.lay_out(act, S0 + u, u, None)

            for it in tiles.turns(act, (4, send_to, CS), (send_to + 1, tile_loop_end, 2)):
                u = it.rep % 2
                if it.has("h"):
                    bank = it.filled(act, "h")
                    if it.rep >= 2:
                        PlanTurn(tiles, it.rep - 1, it.m, it.unroll).wait_filled(act, "hT")
                    nc.scalar.activation(h_sb[u][:], bank[:, :], ACT.Silu).then_inc(silu_done, 1)
                if it.has("hT"):
                    bank = it.filled(act, "hT")
                    if it.rep >= 3:
                        PlanTurn(tiles, it.rep - 1, it.m, it.unroll).wait_filled(act, "y")
                    nc.scalar.copy(hT_hi[1 - u][:].rearrange("p k t -> p (k t)"), bank[:, :]).then_inc(hT_hi_done, 1)
                if it.has("xT"):
                    bank = it.filled(act, "xT")
                    nc.scalar.copy(gT_hi[u][:].rearrange("p k t -> p (k t)"), bank[:, 0:D]).then_inc(gT_hi_done, 1)
                if it.has("y"):
                    bank = it.filled(act, "y")
                    if it.rep >= 4:
                        v = 16 * (it.rep // 2 - 1)
                        act.wait_ge(y_stored[u], v if it.m is None else it.m * (it.unroll * 8) + v)
                    nc.scalar.copy(y_sb[u][:], bank[:, 0:D]).then_inc(y_done, 1)
                if it.m is not None and it.rep <= send_to:
                    dispatch.lay_out(act, it.m * CS + (S0 + CS + it.rep % CS), it.rep % CS, it.m * 16 + 16)

        @block.vector
        def _(dve):
            sort.choose(dve)
            nc.vector.tensor_tensor(exp_d[:], top[:, 1, :], top[:, 0, :], ALU.subtract).then_inc(exp_in, 1)
            for c in range(2):
                split_low(dve, nc.vector, 0, c, w1_done)
            dve.wait_ge(ring_filled, jobs_before + 1)
            sort.take_counts(dve, ring[jobs_before % RING])
            sort.add_up(dve)
            nc.vector.memset(slot[:, :, B:B + CS], 0)
            sort.place(dve)
            split_low(dve, nc.vector, 1, 1, w2_done)
            dve.wait_ge(exp_done, 1)
            nc.vector.tensor_scalar(sum_of[:], exp_d[:], 1.0, None, ALU.add).then_inc(share_step, 1)
            dve.wait_ge(share_step, 1)
            nc.vector.reciprocal(share[:, 0, :], sum_of[:]).then_inc(share_step, 1)
            dve.wait_ge(share_step, 2)
            nc.vector.tensor_tensor(share[:, 1, :], exp_d[:], share[:, 0, :], ALU.mult).then_inc(share_step, 1)
            dve.wait_ge(share_step, 3)
            dve.wait_ge(sort.slots_done, sort.done)

            def combine(m, u):
                b = m * CS + u
                for k in range(2):
                    dve.wait_ge(taken[2 * u + k], m * 16 + 16)
                col = lambda k: share[:, k, bass.ds(b, 1)]
                nc.vector.scalar_tensor_tensor(out=yg[2 * u][:], in0=yg[2 * u][:], scalar=col(0), in1=x_sb[:, b, :], op0=ALU.mult,
                                               op1=ALU.add).then_inc(comb_step, 1)
                dve.wait_ge(comb_step, b + 1)
                nc.vector.scalar_tensor_tensor(out=yg[2 * u][:], in0=yg[2 * u + 1][:], scalar=col(1), in1=yg[2 * u][:],
                                               op0=ALU.mult, op1=ALU.add).then_inc(comb_done, 1)
                nc.vector.tensor_copy(take_at[u][:], slot[:, :, bass.ds(b + CS, 1)]).then_inc(take_at_done, 1)

            def low_halves(it):
                u = it.rep % 2
                if it.has("hT"):
                    bank = it.filled(dve, "hT")
                    dve.wait_ge(hT_hi_done, it.at(1, 0))
                    nc.vector.tensor_tensor(hT_lo[1 - u][:].rearrange("p k t -> p (k t)"), bank[:, :],
                                            hT_hi[1 - u][:].bitcast(F32).rearrange("p k t -> p (k t)"), ALU.subtract).then_inc(hT_done, 1)
                if it.has("xT"):
                    bank = it.filled(dve, "xT")
                    dve.wait_ge(gT_hi_done, it.at(1, 3))
                    nc.vector.tensor_tensor(gT_lo[u][:].rearrange("p k t -> p (k t)"), bank[:, 0:D],
                                            gT_hi[u][:].bitcast(F32).rearrange("p k t -> p (k t)"), ALU.subtract).then_inc(gT_done, 1)

            for u in range(CS):
                nc.vector.tensor_copy(take_at[u][:], slot[:, :, u:u + 1]).then_inc(take_at_done, 1)
            for it in tiles.turns(dve, (4, comb_from - 1, 2), (comb_from, comb_to, CS)):
                low_halves(it)
                if it.m is not None and it.rep >= comb_from:
                    combine(it.m, it.rep - comb_from)
            with dve.Fori(S0 // CS, B // CS) as m:
                for u in range(CS):
                    combine(m, u)

        @block.gpsimd
        def _(pool):
            sort.constants(pool)
            split_low(pool, nc.gpsimd, 1, 0, w2_done)
            with pool.Fori(0, S1 // CS) as m:
                for u in range(CS):
                    dispatch.scatter(pool, m * CS + (u + 1), u, xs_dram[1])
            dispatch.finish(pool, S1)
            pool.sem_inc(seg_sent, 1)

            def gather(m, waits, src):
                for u in range(CS):
                    if waits:
                        pool.wait_ge(out_sent[u], m * 16)
                    pool.wait_ge(take_at_done, m * CS + (u + 1))
                    pool.sem_inc(gather_ready, 1)
                    for k in range(2):
                        i = 2 * u + k
                        pool.indirect_dma_start(out=yg[i][:], out_offset=None, in_=src,
                                                in_offset=bass.IndirectOffsetOnAxis(ap=take_at[u][:, k, 0:1], axis=0)).then_inc(taken[i], 16)

            pool.wait_ge(seg_stored, 1)
            gather(0, False, ys_dram[0])
            with pool.Fori(1, S0 // CS) as m:
                gather(m, True, ys_dram[0])
            pool.wait_ge(seg_stored, 2)
            with pool.Fori(S0 // CS, B // CS) as m:
                gather(m, True, ys_dram[1])


def bass_decoder_layer(nc, x, ctx_x, w_attn, w_proj, ln_w2, rope_cos, rope_sin, w_q, w_k, w_v, w_o, gate_w, w1, w2, out):
    B = x.shape[0]
    with ExitStack() as ctx:
        sh = Shared(nc, ctx, B)
        cross_raw_in, w1_in, xs_cleared = (sh.sem(n) for n in ("cross_raw_in", "w1_in", "xs_cleared"))
        xs_dram = [nc.dram_tensor(f"xs_dram{s}", (n * P, D), F32).ap() for s, n in enumerate(sh.tiles)]
        with nc.sbuf_tensor("raw", [P, 8192], F32) as sh.raw:
            done = self_attention(nc, sh, x, w_attn, w_proj, ln_w2, rope_cos, rope_sin, (w_q, w_k, w_v, w_o), cross_raw_in,
                                  xs_dram, xs_cleared)
            done = cross_attention(nc, sh, done, ctx_x, gate_w, cross_raw_in, w1, w1_in, xs_dram, xs_cleared)
        experts(nc, sh, sh.raw, done, w2, w1_in, xs_dram, out)


def kernel(**inputs):
    import numpy as _np
    import concourse.bacc as _bacc
    from concourse import mybir as _mybir
    from concourse.bass_utils import run_bass_kernel_spmd as _run

    half_dims = _np.concatenate([_np.arange(0, HD, 2), _np.arange(1, HD, 2)])
    q_heads = [h + half for o in range(2) for k in range(4) for h in (2 * k + o,) for half in (0, 8)]
    k_heads = [k + half for k in range(4) for half in (0, 4)]
    cols = [h * HD + half_dims for h in q_heads] + [NQ * HD + h * HD + half_dims for h in k_heads]
    cols += [_np.arange((NQ + NKV) * HD, (NQ + 2 * NKV) * HD + 8)]
    cols = _np.concatenate(cols)
    slots = [8 * half + 2 * k + o for o in range(2) for half in range(2) for k in range(4)]
    rows = _np.concatenate([h * HD + _np.arange(HD) for h in slots])
    T = 128
    div = 2.0 * _np.pi / float(T) ** (_np.arange(0, HD, 2, dtype=_np.float32) / HD)
    ang = _np.arange(T, dtype=_np.float32)[:, None] * div.astype(_np.float32)[None, :]
    cos = _np.cos(ang.astype(_np.float64)).astype(_np.float32)
    sin = _np.sin(ang.astype(_np.float64)).astype(_np.float32)
    arrays = {
        "x": _np.ascontiguousarray(inputs["x"]),
        "ctx": _np.ascontiguousarray(inputs["ctx_1024"]),
        "w_attn": _np.ascontiguousarray(_np.asarray(inputs["L0_attn_w_attn"])[:, cols]),
        "w_proj": _np.ascontiguousarray(_np.asarray(inputs["L0_attn_w_proj"])[rows]),
        "ln_w2": _np.ascontiguousarray(_np.tile(_np.asarray(inputs["L0_attn_ln_w"]), 2).reshape(P, 1)),
        "rope_cos": _np.concatenate([cos, cos], axis=1),
        "rope_sin": _np.concatenate([-sin, sin], axis=1),
        **{n: _np.ascontiguousarray(inputs[f"L0_xattn_{n}"]) for n in ("w_q", "w_k", "w_v", "w_o")},
        **{n: _np.ascontiguousarray(inputs[f"L0_ffn_{n}"]) for n in ("gate_w", "w1", "w2")},
    }
    nc = _bacc.Bacc("TRN2", target_bir_lowering=False, num_devices=1)
    args = [nc.dram_tensor(f"in_{n}", a.shape, _mybir.dt.from_np(a.dtype), kind="ExternalInput").ap() for n, a in arrays.items()]
    out = nc.dram_tensor("out_0", (32, 128, 256), F32, kind="ExternalOutput").ap()
    bass_decoder_layer(nc, *args, out)
    r = _run(nc, [{f"in_{n}": a for n, a in arrays.items()}], core_ids=[0])
    return r.results[0]["out_0"]
```
